# Optimizing a Trainium2 kernel written in Bass

```python
import numpy as np
import jax
import jax.numpy as jnp

def _softmax(x, axis=-1):
    return jax.nn.softmax(x, axis=axis)

def _gelu(x):
    return jax.nn.gelu(x, approximate=True)

def _silu(x):
    return jax.nn.silu(x)

def _sigmoid(x):
    return jax.nn.sigmoid(x)

def _layernorm(x, axis=-1, eps=1e-05):
    m = jnp.mean(x, axis=axis, keepdims=True)
    v = jnp.var(x, axis=axis, keepdims=True)
    return (x - m) / jnp.sqrt(v + eps)

def _scatter_add(tgt, idx, src, axis=0):
    return tgt.at[idx].add(src)

def _segment_sum(src, seg, n):
    return jax.ops.segment_sum(src, seg, n)
kernel_name = 'mk_xattn_ffn_d4_seqx_r8_c94461'

def setup_inputs(seed: int=0):
    np.random.seed(seed)
    _w = jnp.asarray

    def _rec_inputs():
        import jax
        import jax.numpy as jnp
        _rk = jax.random.key(seed)
        x = 7.22e-05 + 1 * jax.random.normal(jax.random.fold_in(_rk, 1), (64, 64, 256), jnp.float32)
        _lenS = 64 - jax.random.randint(jax.random.fold_in(_rk, 7), (64,), 0, max(1, 64 // 4) + 1, jnp.int32)
        _lenS2 = 64 - jax.random.randint(jax.random.fold_in(_rk, 8), (64,), 0, max(1, 64 // 4) + 1, jnp.int32)
        _ctx_2048P = jax.random.normal(jax.random.fold_in(_rk, 11), (64, 16, 256), jnp.float32)
        _ctx_2048c = jax.random.dirichlet(jax.random.fold_in(_rk, 511), 0.3 * jnp.ones((16,), jnp.float32), (64, 64))
        _ctx_2048t = jnp.einsum('bsk,bkd->bsd', _ctx_2048c, _ctx_2048P)
        _ctx_2048t = _ctx_2048t * jax.lax.rsqrt(jnp.mean(jnp.square(_ctx_2048t)) + 1e-12) * 0.953939
        ctx_2048 = 4.13588e-05 + 0.999923 * (_ctx_2048t + 0.3 * jax.random.normal(jax.random.fold_in(_rk, 611), (64, 64, 256), jnp.float32))
        return (x, ctx_2048)
    x, ctx_2048 = _rec_inputs()

    def _L0_xattn_setup():
        import jax, jax.numpy as jnp
        import numpy as np
        N_HEAD = 8
        key = jax.random.key(seed)
        k1, k2, k3 = jax.random.split(key, 3)
        b, d, m = (4, 128, 256)
        c, n = (128, 256)
        q = jax.random.normal(k1, (b, d, m), dtype=jnp.float32)
        k = jax.random.normal(k2, (d // d * b, d, n), dtype=jnp.float32).reshape(b, d, n)
        v = jax.random.normal(k3, (b, c, n), dtype=jnp.float32)
        return {'q': q, 'k': k, 'v': v}
    _L0_xattn_all = _L0_xattn_setup()
    _L0_xattn_in = {k: v for k, v in _L0_xattn_all.items() if k in ()}
    del _L0_xattn_all

    def _L0_ffn_setup():
        import jax, jax.numpy as jnp
        import numpy as np
        B, L, D = (4, 512, 256)
        DF = 4 * D
        CAPACITY_RATIO = 0.5
        key = jax.random.key(seed)
        ks = jax.random.split(key, 4)
        s = 0.02
        return {'x': jax.random.normal(ks[0], (B, L, D), dtype=jnp.float32), 'w_r': jax.random.normal(ks[1], (D,), dtype=jnp.float32) * s, 'b_r': jnp.zeros((), dtype=jnp.float32), 'w1': jax.random.normal(ks[2], (D, DF), dtype=jnp.float32) * s, 'b1': jnp.zeros((DF,), dtype=jnp.float32), 'w2': jax.random.normal(ks[3], (DF, D), dtype=jnp.float32) * s, 'b2': jnp.zeros((D,), dtype=jnp.float32)}
    _L0_ffn_all = _L0_ffn_setup()
    _L0_ffn_in = {k: v for k, v in _L0_ffn_all.items() if k in ('w_r', 'b_r', 'w1', 'b1', 'w2', 'b2')}
    del _L0_ffn_all

    def _L1_xattn_setup():
        import jax, jax.numpy as jnp
        import numpy as np
        B, S, E, NH = (2, 128, 256, 16)
        DH = E // NH
        EPS = 1e-06

        def _mlstm_forward(q, k, v, Wi, bi, Wf, bf, ln_scale):
            b, s, e = q.shape
            nh = Wi.shape[1]
            dh = e // nh
            x = jnp.concatenate([q, k, v], axis=-1)
            ig = (x @ Wi + bi).transpose(0, 2, 1)[..., None]
            fg = (x @ Wf + bf).transpose(0, 2, 1)[..., None]
            split = lambda t: t.reshape(b, s, nh, dh).transpose(0, 2, 1, 3)
            qh, kh, vh = (split(q), split(k), split(v))
            log_f = jax.nn.log_sigmoid(fg)
            log_f_cum = jnp.concatenate([jnp.zeros((b, nh, 1, 1), q.dtype), jnp.cumsum(log_f, axis=2)], axis=2)
            fg_mat = log_f_cum - jnp.transpose(log_f_cum, (0, 1, 3, 2))
            ltr = jnp.tril(jnp.ones((s, s), dtype=bool))
            log_fg = jnp.where(ltr, fg_mat[:, :, 1:, 1:], -jnp.inf)
            log_D = log_fg + jnp.transpose(ig, (0, 1, 3, 2))
            max_log_D = jnp.max(log_D, axis=-1, keepdims=True)
            D = jnp.exp(log_D - max_log_D)
            qk = jnp.einsum('bhsd,bhtd->bhst', qh, kh) / jnp.sqrt(jnp.asarray(dh, q.dtype))
            C = qk * D
            normalizer = jnp.maximum(jnp.abs(C.sum(-1, keepdims=True)), jnp.exp(-max_log_D))
            Cn = C / (normalizer + EPS)
            h = jnp.einsum('bhst,bhtd->bhsd', Cn, vh)
            mu = h.mean(-1, keepdims=True)
            var = ((h - mu) ** 2).mean(-1, keepdims=True)
            hn = (h - mu) * jax.lax.rsqrt(var + EPS)
            hn = hn * ln_scale.reshape(1, nh, 1, dh)
            return hn.transpose(0, 2, 1, 3).reshape(b, s, e)
        key = jax.random.key(seed)
        ks = jax.random.split(key, 6)
        q = jax.random.normal(ks[0], (B, S, E), dtype=jnp.float32)
        k = jax.random.normal(ks[1], (B, S, E), dtype=jnp.float32)
        v = jax.random.normal(ks[2], (B, S, E), dtype=jnp.float32)
        Wi = jax.random.normal(ks[3], (3 * E, NH), dtype=jnp.float32) * 0.02
        bi = jax.random.normal(ks[4], (NH,), dtype=jnp.float32) * 0.1
        Wf = jax.random.normal(ks[5], (3 * E, NH), dtype=jnp.float32) * 0.02
        bf = jnp.linspace(3.0, 6.0, NH, dtype=jnp.float32)
        ln_scale = jnp.ones((E,), dtype=jnp.float32)
        return {'q': q, 'k': k, 'v': v, 'Wi': Wi, 'bi': bi, 'Wf': Wf, 'bf': bf, 'ln_scale': ln_scale}
    _L1_xattn_all = _L1_xattn_setup()
    _L1_xattn_in = {k: v for k, v in _L1_xattn_all.items() if k in ('Wi', 'bi', 'Wf', 'bf', 'ln_scale')}
    del _L1_xattn_all

    def _L1_ffn_setup():
        import jax, jax.numpy as jnp
        import numpy as np
        EPS = 1e-05

        def rms_norm(x):
            return x * jax.lax.rsqrt(jnp.mean(x * x, axis=-1, keepdims=True) + EPS)

        def act_quant(x):
            scale = 127.0 / jnp.clip(jnp.max(jnp.abs(x), axis=-1, keepdims=True), 1e-05)
            q = jnp.clip(jnp.round(x * scale), -128.0, 127.0) / scale
            return x + jax.lax.stop_gradient(q - x)

        def weight_quant(w):
            scale = 1.0 / jnp.clip(jnp.mean(jnp.abs(w)), 1e-05)
            q = jnp.clip(jnp.round(w * scale), -1.0, 1.0) / scale
            return w + jax.lax.stop_gradient(q - w)

        def bitlinear158(x, w, b):
            xq = act_quant(rms_norm(x))
            wq = weight_quant(w)
            return jnp.einsum('bsd,od->bso', xq, wq) + b

        def layer_norm(x, g, b):
            mu = jnp.mean(x, axis=-1, keepdims=True)
            var = jnp.mean((x - mu) ** 2, axis=-1, keepdims=True)
            return (x - mu) * jax.lax.rsqrt(var + EPS) * g + b
        key = jax.random.key(seed)
        ks = jax.random.split(key, 3)
        d, inner = (256, 1024)
        x = jax.random.normal(ks[0], (4, 256, d), dtype=jnp.float32)
        w1 = jax.random.normal(ks[1], (inner, d), dtype=jnp.float32) * 0.02
        b1 = jnp.zeros((inner,), jnp.float32)
        ln_g = jnp.ones((inner,), jnp.float32)
        ln_b = jnp.zeros((inner,), jnp.float32)
        w2 = jax.random.normal(ks[2], (d, inner), dtype=jnp.float32) * 0.02
        b2 = jnp.zeros((d,), jnp.float32)
        return {'x': x, 'w1': w1, 'b1': b1, 'ln_g': ln_g, 'ln_b': ln_b, 'w2': w2, 'b2': b2}
    _L1_ffn_all = _L1_ffn_setup()
    _L1_ffn_in = {k: v for k, v in _L1_ffn_all.items() if k in ('w1', 'b1', 'ln_g', 'ln_b', 'w2', 'b2')}
    del _L1_ffn_all

    def _L2_xattn_setup():
        import jax, jax.numpy as jnp
        import numpy as np
        D_MODEL = 256
        NUM_HEADS = 16
        HEAD_DIM = D_MODEL // NUM_HEADS
        key = jax.random.key(seed)
        ks = jax.random.split(key, 10)
        B, S, T = (4, 512, 128)
        s = 1.0 / np.sqrt(D_MODEL)
        inp = {'query': jax.random.normal(ks[0], (B, S, D_MODEL), jnp.float32), 'key_value': jax.random.normal(ks[1], (B, T, D_MODEL), jnp.float32), 'Wq': jax.random.normal(ks[2], (D_MODEL, D_MODEL), jnp.float32) * s, 'bq': jnp.zeros((D_MODEL,), jnp.float32), 'Wk': jax.random.normal(ks[3], (D_MODEL, D_MODEL), jnp.float32) * s, 'bk': jnp.zeros((D_MODEL,), jnp.float32), 'Wv': jax.random.normal(ks[4], (D_MODEL, D_MODEL), jnp.float32) * s, 'bv': jnp.zeros((D_MODEL,), jnp.float32), 'Wo': jax.random.normal(ks[5], (D_MODEL, D_MODEL), jnp.float32) * s, 'bo': jnp.zeros((D_MODEL,), jnp.float32)}
        return inp
    _L2_xattn_all = _L2_xattn_setup()
    _L2_xattn_in = {k: v for k, v in _L2_xattn_all.items() if k in ('Wq', 'bq', 'Wk', 'bk', 'Wv', 'bv', 'Wo', 'bo')}
    del _L2_xattn_all

    def _L2_ffn_setup():
        import jax, jax.numpy as jnp
        import numpy as np
        EPS = 1e-06

        def rmsnorm(x):
            return x * jax.lax.rsqrt(jnp.mean(x * x, axis=-1, keepdims=True) + EPS)

        def activation_quant(x):
            scale = 127.0 / jnp.clip(jnp.max(jnp.abs(x), axis=-1, keepdims=True), 1e-05, None)
            return jnp.clip(jnp.round(x * scale), -128, 127) / scale

        def weight_quant(w):
            scale = 1.0 / jnp.clip(jnp.mean(jnp.abs(w)), 1e-05, None)
            return jnp.clip(jnp.round(w * scale), -1, 1) / scale

        def ste(x, q):
            return x + jax.lax.stop_gradient(q - x)

        def bitlinear(x, w):
            xn = rmsnorm(x)
            xq = ste(xn, activation_quant(xn))
            wq = ste(w, weight_quant(w))
            return jnp.einsum('bsd,hd->bsh', xq, wq)
        key = jax.random.key(seed)
        k1, k2, k3, k4 = jax.random.split(key, 4)
        d_model, hidden = (256, 1024)
        x = jax.random.normal(k1, (4, 256, d_model), dtype=jnp.float32)
        w_gate = jax.random.normal(k2, (hidden, d_model), dtype=jnp.float32) * 0.02
        w_up = jax.random.normal(k3, (hidden, d_model), dtype=jnp.float32) * 0.02
        w_down = jax.random.normal(k4, (d_model, hidden), dtype=jnp.float32) * 0.02
        return {'x': x, 'w_gate': w_gate, 'w_up': w_up, 'w_down': w_down}
    _L2_ffn_all = _L2_ffn_setup()
    _L2_ffn_in = {k: v for k, v in _L2_ffn_all.items() if k in ('w_gate', 'w_up', 'w_down')}
    del _L2_ffn_all

    def _L3_xattn_setup():
        import jax, jax.numpy as jnp
        import numpy as np
        from jax import lax
        LN_EPS = 1e-05
        key = jax.random.key(seed)
        ks = jax.random.split(key, 8)
        B, S, T, D = (4, 128, 256, 256)
        scale = 0.02
        return {'Z': jax.random.normal(ks[0], (B, S, D), dtype=jnp.float32), 'kv': jax.random.normal(ks[1], (B, T, D), dtype=jnp.float32), 'decay': jnp.float32(0.9), 'W_in': jax.random.normal(ks[2], (D, D), dtype=jnp.float32) * scale, 'b_in': jnp.zeros((D,), dtype=jnp.float32), 'W_out': jax.random.normal(ks[3], (D, D), dtype=jnp.float32) * scale, 'b_out': jnp.zeros((D,), dtype=jnp.float32), 'gamma': jnp.ones((D,), dtype=jnp.float32), 'beta': jnp.zeros((D,), dtype=jnp.float32)}
    _L3_xattn_all = _L3_xattn_setup()
    _L3_xattn_in = {k: v for k, v in _L3_xattn_all.items() if k in ('decay', 'W_in', 'b_in', 'W_out', 'b_out', 'gamma', 'beta')}
    del _L3_xattn_all

    def _L3_ffn_setup():
        import jax, jax.numpy as jnp
        import numpy as np
        LHS_BITS = 8
        RHS_BITS = 8

        def fake_quant(x, bits, axes):
            qmax = 2.0 ** (bits - 1) - 1.0
            amax = jnp.max(jnp.abs(x), axis=axes, keepdims=True)
            scale = jnp.where(amax > 0, amax / qmax, jnp.ones_like(amax))
            q = jnp.clip(jnp.round(x / scale), -qmax, qmax) * scale
            return x + jax.lax.stop_gradient(q - x)
        key = jax.random.key(seed)
        k1, k2, k3 = jax.random.split(key, 3)
        B, S, D, F = (4, 256, 256, 256)
        x = jax.random.normal(k1, (B, S, D), dtype=jnp.float32)
        kernel = jax.random.normal(k2, (D, F), dtype=jnp.float32) * (1.0 / np.sqrt(D))
        bias = jax.random.normal(k3, (F,), dtype=jnp.float32) * 0.02
        return {'x': x, 'kernel': kernel, 'bias': bias}
    _L3_ffn_all = _L3_ffn_setup()
    _L3_ffn_in = {k: v for k, v in _L3_ffn_all.items() if k in ('kernel', 'bias')}
    del _L3_ffn_all
    return {'x': x, 'ctx_2048': ctx_2048, 'L0_ffn_w_r': _L0_ffn_in['w_r'], 'L0_ffn_b_r': _L0_ffn_in['b_r'], 'L0_ffn_w1': _L0_ffn_in['w1'], 'L0_ffn_b1': _L0_ffn_in['b1'], 'L0_ffn_w2': _L0_ffn_in['w2'], 'L0_ffn_b2': _L0_ffn_in['b2'], 'L1_xattn_Wi': _L1_xattn_in['Wi'], 'L1_xattn_bi': _L1_xattn_in['bi'], 'L1_xattn_Wf': _L1_xattn_in['Wf'], 'L1_xattn_bf': _L1_xattn_in['bf'], 'L1_xattn_ln_scale': _L1_xattn_in['ln_scale'], 'L1_ffn_w1': _L1_ffn_in['w1'], 'L1_ffn_b1': _L1_ffn_in['b1'], 'L1_ffn_ln_g': _L1_ffn_in['ln_g'], 'L1_ffn_ln_b': _L1_ffn_in['ln_b'], 'L1_ffn_w2': _L1_ffn_in['w2'], 'L1_ffn_b2': _L1_ffn_in['b2'], 'L2_xattn_Wq': _L2_xattn_in['Wq'], 'L2_xattn_bq': _L2_xattn_in['bq'], 'L2_xattn_Wk': _L2_xattn_in['Wk'], 'L2_xattn_bk': _L2_xattn_in['bk'], 'L2_xattn_Wv': _L2_xattn_in['Wv'], 'L2_xattn_bv': _L2_xattn_in['bv'], 'L2_xattn_Wo': _L2_xattn_in['Wo'], 'L2_xattn_bo': _L2_xattn_in['bo'], 'L2_ffn_w_gate': _L2_ffn_in['w_gate'], 'L2_ffn_w_up': _L2_ffn_in['w_up'], 'L2_ffn_w_down': _L2_ffn_in['w_down'], 'L3_xattn_decay': _L3_xattn_in['decay'], 'L3_xattn_W_in': _L3_xattn_in['W_in'], 'L3_xattn_b_in': _L3_xattn_in['b_in'], 'L3_xattn_W_out': _L3_xattn_in['W_out'], 'L3_xattn_b_out': _L3_xattn_in['b_out'], 'L3_xattn_gamma': _L3_xattn_in['gamma'], 'L3_xattn_beta': _L3_xattn_in['beta'], 'L3_ffn_kernel': _L3_ffn_in['kernel'], 'L3_ffn_bias': _L3_ffn_in['bias']}

def reference(x, ctx_2048, L0_ffn_w_r, L0_ffn_b_r, L0_ffn_w1, L0_ffn_b1, L0_ffn_w2, L0_ffn_b2, L1_xattn_Wi, L1_xattn_bi, L1_xattn_Wf, L1_xattn_bf, L1_xattn_ln_scale, L1_ffn_w1, L1_ffn_b1, L1_ffn_ln_g, L1_ffn_ln_b, L1_ffn_w2, L1_ffn_b2, L2_xattn_Wq, L2_xattn_bq, L2_xattn_Wk, L2_xattn_bk, L2_xattn_Wv, L2_xattn_bv, L2_xattn_Wo, L2_xattn_bo, L2_ffn_w_gate, L2_ffn_w_up, L2_ffn_w_down, L3_xattn_decay, L3_xattn_W_in, L3_xattn_b_in, L3_xattn_W_out, L3_xattn_b_out, L3_xattn_gamma, L3_xattn_beta, L3_ffn_kernel, L3_ffn_bias):
    import jax
    import jax.numpy as jnp

    def _L0_xattn_ref(q, k, v):
        import jax, jax.numpy as jnp
        import numpy as np
        N_HEAD = 8
        b, d, m = q.shape
        c = v.shape[1]
        h = N_HEAD
        qh = q.reshape(b * h, d // h, m)
        kh = k.reshape(b * h, d // h, -1)
        vh = v.reshape(b * h, c // h, -1)
        scale = 1.0 / jnp.sqrt(jnp.asarray(d // h, dtype=q.dtype))
        qk = jnp.einsum('bdm,bdn->bmn', qh, kh) * scale
        sm = jax.nn.softmax(qk, axis=-1)
        ret = jnp.einsum('bmn,bcn->bcm', sm, vh)
        return ret.reshape(b, c, m)

    def _L0_ffn_ref(x, w_r, b_r, w1, b1, w2, b2):
        import jax, jax.numpy as jnp
        import numpy as np
        B, L, D = (4, 512, 256)
        DF = 4 * D
        CAPACITY_RATIO = 0.5
        b, l, d = x.shape
        k = int(l * CAPACITY_RATIO)
        scores = jnp.einsum('bld,d->bl', x, w_r) + b_r
        _, idx = jax.lax.top_k(scores, k)
        x_sel = jnp.take_along_axis(x, idx[:, :, None], axis=1)
        h = jax.nn.gelu(jnp.einsum('bkd,df->bkf', x_sel, w1) + b1)
        out_sel = jnp.einsum('bkf,fd->bkd', h, w2) + b2
        batch_ix = jnp.arange(b)[:, None]
        out = jnp.zeros_like(x).at[batch_ix, idx].set(out_sel)
        return out

    def _L1_xattn_ref(q, k, v, Wi, bi, Wf, bf, ln_scale):
        import jax, jax.numpy as jnp
        import numpy as np
        B, S, E, NH = (2, 128, 256, 16)
        DH = E // NH
        EPS = 1e-06

        def _mlstm_forward(q, k, v, Wi, bi, Wf, bf, ln_scale):
            b, s, e = q.shape
            nh = Wi.shape[1]
            dh = e // nh
            x = jnp.concatenate([q, k, v], axis=-1)
            ig = (x @ Wi + bi).transpose(0, 2, 1)[..., None]
            fg = (x @ Wf + bf).transpose(0, 2, 1)[..., None]
            split = lambda t: t.reshape(b, s, nh, dh).transpose(0, 2, 1, 3)
            qh, kh, vh = (split(q), split(k), split(v))
            log_f = jax.nn.log_sigmoid(fg)
            log_f_cum = jnp.concatenate([jnp.zeros((b, nh, 1, 1), q.dtype), jnp.cumsum(log_f, axis=2)], axis=2)
            fg_mat = log_f_cum - jnp.transpose(log_f_cum, (0, 1, 3, 2))
            ltr = jnp.tril(jnp.ones((s, s), dtype=bool))
            log_fg = jnp.where(ltr, fg_mat[:, :, 1:, 1:], -jnp.inf)
            log_D = log_fg + jnp.transpose(ig, (0, 1, 3, 2))
            max_log_D = jnp.max(log_D, axis=-1, keepdims=True)
            D = jnp.exp(log_D - max_log_D)
            qk = jnp.einsum('bhsd,bhtd->bhst', qh, kh) / jnp.sqrt(jnp.asarray(dh, q.dtype))
            C = qk * D
            normalizer = jnp.maximum(jnp.abs(C.sum(-1, keepdims=True)), jnp.exp(-max_log_D))
            Cn = C / (normalizer + EPS)
            h = jnp.einsum('bhst,bhtd->bhsd', Cn, vh)
            mu = h.mean(-1, keepdims=True)
            var = ((h - mu) ** 2).mean(-1, keepdims=True)
            hn = (h - mu) * jax.lax.rsqrt(var + EPS)
            hn = hn * ln_scale.reshape(1, nh, 1, dh)
            return hn.transpose(0, 2, 1, 3).reshape(b, s, e)
        return _mlstm_forward(q, k, v, Wi, bi, Wf, bf, ln_scale)

    def _L1_ffn_ref(x, w1, b1, ln_g, ln_b, w2, b2):
        import jax, jax.numpy as jnp
        import numpy as np
        EPS = 1e-05

        def rms_norm(x):
            return x * jax.lax.rsqrt(jnp.mean(x * x, axis=-1, keepdims=True) + EPS)

        def act_quant(x):
            scale = 127.0 / jnp.clip(jnp.max(jnp.abs(x), axis=-1, keepdims=True), 1e-05)
            q = jnp.clip(jnp.round(x * scale), -128.0, 127.0) / scale
            return x + jax.lax.stop_gradient(q - x)

        def weight_quant(w):
            scale = 1.0 / jnp.clip(jnp.mean(jnp.abs(w)), 1e-05)
            q = jnp.clip(jnp.round(w * scale), -1.0, 1.0) / scale
            return w + jax.lax.stop_gradient(q - w)

        def bitlinear158(x, w, b):
            xq = act_quant(rms_norm(x))
            wq = weight_quant(w)
            return jnp.einsum('bsd,od->bso', xq, wq) + b

        def layer_norm(x, g, b):
            mu = jnp.mean(x, axis=-1, keepdims=True)
            var = jnp.mean((x - mu) ** 2, axis=-1, keepdims=True)
            return (x - mu) * jax.lax.rsqrt(var + EPS) * g + b
        h = jax.nn.silu(bitlinear158(x, w1, b1))
        h = jax.nn.gelu(h, approximate=False)
        h = layer_norm(h, ln_g, ln_b)
        return bitlinear158(h, w2, b2)

    def _L2_xattn_ref(query, key_value, Wq, bq, Wk, bk, Wv, bv, Wo, bo):
        import jax, jax.numpy as jnp
        import numpy as np
        D_MODEL = 256
        NUM_HEADS = 16
        HEAD_DIM = D_MODEL // NUM_HEADS
        B, S, _ = query.shape
        T = key_value.shape[1]
        Q = query @ Wq.T + bq
        K = key_value @ Wk.T + bk
        V = key_value @ Wv.T + bv
        Q = Q.reshape(B, S, NUM_HEADS, HEAD_DIM).transpose(0, 2, 1, 3)
        K = K.reshape(B, T, NUM_HEADS, HEAD_DIM).transpose(0, 2, 1, 3)
        V = V.reshape(B, T, NUM_HEADS, HEAD_DIM).transpose(0, 2, 1, 3)
        scale = 1.0 / np.sqrt(HEAD_DIM).astype(np.float32)
        scores = jnp.einsum('bhsd,bhtd->bhst', Q, K) * scale
        attn = jax.nn.softmax(scores, axis=-1)
        ctx = jnp.einsum('bhst,bhtd->bhsd', attn, V)
        ctx = ctx.transpose(0, 2, 1, 3).reshape(B, S, D_MODEL)
        return ctx @ Wo.T + bo

    def _L2_ffn_ref(x, w_gate, w_up, w_down):
        import jax, jax.numpy as jnp
        import numpy as np
        EPS = 1e-06

        def rmsnorm(x):
            return x * jax.lax.rsqrt(jnp.mean(x * x, axis=-1, keepdims=True) + EPS)

        def activation_quant(x):
            scale = 127.0 / jnp.clip(jnp.max(jnp.abs(x), axis=-1, keepdims=True), 1e-05, None)
            return jnp.clip(jnp.round(x * scale), -128, 127) / scale

        def weight_quant(w):
            scale = 1.0 / jnp.clip(jnp.mean(jnp.abs(w)), 1e-05, None)
            return jnp.clip(jnp.round(w * scale), -1, 1) / scale

        def ste(x, q):
            return x + jax.lax.stop_gradient(q - x)

        def bitlinear(x, w):
            xn = rmsnorm(x)
            xq = ste(xn, activation_quant(xn))
            wq = ste(w, weight_quant(w))
            return jnp.einsum('bsd,hd->bsh', xq, wq)
        gate = jax.nn.silu(bitlinear(x, w_gate))
        up = bitlinear(x, w_up)
        return bitlinear(gate * up, w_down)

    def _L3_xattn_ref(Z, kv, decay, W_in, b_in, W_out, b_out, gamma, beta):
        import jax, jax.numpy as jnp
        import numpy as np
        from jax import lax
        LN_EPS = 1e-05
        B, T, D = kv.shape
        K = jax.nn.sigmoid(decay)
        x = jnp.einsum('btd,ed->bte', kv, W_in) + b_in

        def scan_fn(s, xt):
            s = K * s + xt
            return (s, s)
        s0 = jnp.zeros((B, D), dtype=kv.dtype)
        _, states = lax.scan(scan_fn, s0, jnp.swapaxes(x, 0, 1))
        states = jnp.swapaxes(states, 0, 1)
        proj = jnp.einsum('btd,ed->bte', states, W_out) + b_out
        summary = jnp.mean(proj, axis=1, keepdims=True)
        y = Z + summary
        mu = jnp.mean(y, axis=-1, keepdims=True)
        var = jnp.mean((y - mu) ** 2, axis=-1, keepdims=True)
        return (y - mu) / jnp.sqrt(var + LN_EPS) * gamma + beta

    def _L3_ffn_ref(x, kernel, bias):
        import jax, jax.numpy as jnp
        import numpy as np
        LHS_BITS = 8
        RHS_BITS = 8

        def fake_quant(x, bits, axes):
            qmax = 2.0 ** (bits - 1) - 1.0
            amax = jnp.max(jnp.abs(x), axis=axes, keepdims=True)
            scale = jnp.where(amax > 0, amax / qmax, jnp.ones_like(amax))
            q = jnp.clip(jnp.round(x / scale), -qmax, qmax) * scale
            return x + jax.lax.stop_gradient(q - x)
        bq = fake_quant(bias, RHS_BITS, -1)
        xq = fake_quant(x, LHS_BITS, -1)
        kq = fake_quant(kernel, RHS_BITS, 0)
        y = jnp.einsum('bsd,df->bsf', xq, kq)
        y = y + bq[None, None, :]
        y = jax.nn.relu(y)
        return fake_quant(y, LHS_BITS, -1)
    x = x + _L0_xattn_ref(_layernorm(x, axis=-1), ctx_2048, ctx_2048)
    x = x + _L0_ffn_ref(_layernorm(x, axis=-1), L0_ffn_w_r, L0_ffn_b_r, L0_ffn_w1, L0_ffn_b1, L0_ffn_w2, L0_ffn_b2)
    x = x + _L1_xattn_ref(_layernorm(x, axis=-1), ctx_2048, ctx_2048, L1_xattn_Wi, L1_xattn_bi, L1_xattn_Wf, L1_xattn_bf, L1_xattn_ln_scale)
    x = x + _L1_ffn_ref(_layernorm(x, axis=-1), L1_ffn_w1, L1_ffn_b1, L1_ffn_ln_g, L1_ffn_ln_b, L1_ffn_w2, L1_ffn_b2)
    x = x + _L2_xattn_ref(_layernorm(x, axis=-1), ctx_2048, L2_xattn_Wq, L2_xattn_bq, L2_xattn_Wk, L2_xattn_bk, L2_xattn_Wv, L2_xattn_bv, L2_xattn_Wo, L2_xattn_bo)
    x = x + _L2_ffn_ref(_layernorm(x, axis=-1), L2_ffn_w_gate, L2_ffn_w_up, L2_ffn_w_down)
    x = x + _L3_xattn_ref(_layernorm(x, axis=-1), ctx_2048, L3_xattn_decay, L3_xattn_W_in, L3_xattn_b_in, L3_xattn_W_out, L3_xattn_b_out, L3_xattn_gamma, L3_xattn_beta)
    x = x + _L3_ffn_ref(_layernorm(x, axis=-1), L3_ffn_kernel, L3_ffn_bias)
    return x

_drawn_inputs = setup_inputs


def setup_inputs(seed=0):
    import zlib

    import numpy as np

    out = dict(_drawn_inputs(seed))
    spreads = {'L0_ffn_b1': (0.0, 0.374),
     'L0_ffn_b2': (0.0, 0.1),
     'L1_xattn_ln_scale': (1.0, 0.2),
     'L1_ffn_b1': (0.0, 0.1),
     'L1_ffn_ln_g': (1.0, 0.2),
     'L1_ffn_ln_b': (0.0, 0.373),
     'L1_ffn_b2': (0.0, 0.1),
     'L2_xattn_bq': (0.0, 0.638),
     'L2_xattn_bk': (0.0, 2.0),
     'L2_xattn_bv': (0.0, 0.1),
     'L2_xattn_bo': (0.0, 0.1),
     'L3_xattn_b_in': (0.0, 0.1),
     'L3_xattn_b_out': (0.0, 0.1),
     'L3_xattn_gamma': (1.0, 0.2),
     'L3_xattn_beta': (0.0, 0.281)}
    factors = {'L1_xattn_bi': 64.0, 'L1_xattn_Wf': 4.152, 'L3_ffn_bias': 8.0}
    for name, (base, spread) in spreads.items():
        noise = np.random.default_rng([zlib.crc32(name.encode()), seed]).standard_normal(out[name].shape)
        drawn = base * np.exp(spread * noise) if base else spread * noise
        out[name] = jnp.asarray(drawn.astype(out[name].dtype))
    for name, factor in factors.items():
        out[name] = (out[name] * factor).astype(out[name].dtype)
    return out
```

```python
from contextlib import ExitStack

import numpy as np

import concourse.bass as bass
from concourse import mybir

ALU = mybir.AluOpType
ACT = mybir.ActivationFunctionType
AX = mybir.AxisListType
F32 = mybir.dt.float32
BF16 = mybir.dt.bfloat16

P = 128
B, L, D = 64, 64, 256
N = B * L
T = N // P
G = 4
NG = T // G
KC = D // P
FF = 4 * D
NH0, DH0 = 8, 8
BH = B * NH0
NH, DH = 16, 16
KEEP = L // 2
LN_EPS = 1e-5
MAGIC = 12582912.0
BIG = 1.0e30

class Scope:

    def __init__(self, nc, ctx, name):
        self.nc, self.ctx, self.name, self.sems = nc, ctx, name, []
        ctx.callback(self.close)

    def sb(self, name, shape, dt=F32):
        return self.ctx.enter_context(self.nc.sbuf_tensor(f"{self.name}_{name}", shape, dt))

    def ps(self, name, shape, dt=F32):
        return self.ctx.enter_context(self.nc.psum_tensor(f"{self.name}_{name}", shape, dt))

    def sem(self, name):
        self.sems.append(self.nc.alloc_semaphore(name=f"{self.name}_{name}"))
        return self.sems[-1]

    def close(self):
        if self.sems:
            self.nc.clear_and_free_semaphores(self.sems)
            self.nc.all_engine_barrier()

class Steps:

    def __init__(self, engine, done, per, i=0):
        self.engine, self.done, self.per, self.i, self.n = engine, done, per, i, 0

    def __call__(self, instruction):
        self.n += 1
        instruction.then_inc(self.done, 1)
        self.engine.wait_ge(self.done, self.i * self.per + self.n)

    def end(self):
        assert self.n == self.per, (self.n, self.per)

def held(engine, value):
    return value if isinstance(value, int) else engine.snap(value)

def spread(ap, dim, n):
    return ap.unsqueeze(dim).to_broadcast(list(ap.shape[:dim]) + [n] + list(ap.shape[dim:]))

def prepare(nc, io, X, CT, ident, zq, ck):
    with ExitStack() as ctx:
        s = Scope(nc, ctx, "prep")
        C = s.sb("C", [P, 2, G, D])
        Z = s.sb("Z", [P, G, D])
        ZR = s.sb("ZR", [P, 2, G, D])
        CR = s.sb("CR", [P, 2, G, D])
        ZS = s.sb("ZS", [P, 3, G, D], BF16)
        CS = s.sb("CS", [P, 3, G, D], BF16)
        stats = s.sb("stats", [P, G, 6])
        mv = s.sb("mv", [P, G, 2])
        veps = s.sb("veps", [P, G])
        rstd = s.sb("rstd", [P, G])
        mhalf = s.sb("mhalf", [P, G])
        eps = s.sb("eps", [P, G])
        psC = s.ps("psC", [P, KC, G * P])
        ready = s.sem("ready")
        x_in, c_in = s.sem("x_in"), s.sem("c_in")
        stats_done, rstd_done, pool_step = s.sem("stats_done"), s.sem("rstd_done"), s.sem("pool_step")
        z_done = s.sem("z_done")
        z_part, z_rest, c_part, c_rest = s.sem("z_part"), s.sem("z_rest"), s.sem("c_part"), s.sem("c_rest")
        turned, ct_done = s.sem("turned"), s.sem("ct_done")
        z_out, c_out = s.sem("z_out"), s.sem("c_out")
        x_dram = io["x"].rearrange("(t u) l d -> t (u l) d", u=2)
        c_dram = io["ctx_2048"].rearrange("(t u) l d -> t (u l) d", u=2)
        zq_w = zq.rearrange("s r h t m -> s h r (t m)")
        ck_w = ck.rearrange("s r h t m -> s h r (t m)")

        with nc.Block() as block:

            @block.sync
            def _(sp):
                def load(t, w):
                    sp.dma_start(X[:, bass.ds(t, G), :],
                                 x_dram[bass.ds(t, G)].rearrange("t p d -> p t d")).then_inc(x_in, 16)
                    sp.dma_start(C[:, w], c_dram[bass.ds(t, G)].rearrange("t p d -> p t d")).then_inc(c_in, 16)

                load(0, 0)
                def turn(h, last):
                    for w in range(2):
                        g = h * 2 + w
                        to, ahead, loads, before = (held(sp, v) for v in (g * (G * D), g * G + G, g * 16 + 16, g * 16))
                        parts = [held(sp, g * 3 + part + 1) for part in range(3)]
                        sp.wait_ge(x_in, loads)
                        sp.wait_ge(c_in, loads)
                        sp.wait_ge(c_rest, before)
                        sp.wait_ge(turned, before)
                        if w == 0 or not last:
                            load(ahead, 1 - w)
                        for part in range(3):
                            sp.wait_ge(z_part, parts[part])
                            sp.dma_start(zq_w[part, :, :, bass.ds(to, G * D)],
                                         ZS[:, part].rearrange("p j m -> p (j m)")).then_inc(z_out, 16)
                        for part in range(3):
                            sp.wait_ge(c_part, parts[part])
                            sp.dma_start(ck_w[part, :, :, bass.ds(to, G * D)],
                                         CS[:, part].rearrange("p j m -> p (j m)")).then_inc(c_out, 16)

                with sp.Fori(0, NG // 2 - 1) as h:
                    turn(h, False)
                turn(NG // 2 - 1, True)
                sp.wait_ge(z_out, 16 * 3 * NG)
                sp.wait_ge(c_out, 16 * 3 * NG)

            @block.gpsimd
            def _(pool):
                nc.gpsimd.memset(mhalf[:], -0.5).then_inc(ready, 1)
                nc.gpsimd.memset(eps[:], LN_EPS).then_inc(ready, 1)
                nc.gpsimd.memset(ident[:], 0.0).then_inc(ready, 1)
                pool.wait_ge(ready, 3)
                nc.gpsimd.affine_select(out=ident[:], in_=ident[:], compare_op=ALU.not_equal, fill=1.0, base=0,
                                        pattern=[[-1, P]], channel_multiplier=1).then_inc(ready, 1)
                with pool.Fori(0, NG // 2) as h:
                    for w in range(2):
                        g = h * 2 + w
                        step = Steps(pool, pool_step, 1, g)
                        pool.wait_ge(stats_done, g * G + G)
                        step(nc.gpsimd.tensor_tensor(veps[:], mv[:, :, 1], eps[:], ALU.add))
                        nc.gpsimd.tensor_tensor(rstd[:], veps[:], mhalf[:], ALU.pow).then_inc(rstd_done, 1)
                        step.end()
                        pool.wait_ge(c_part, g * 3 + 1)
                        nc.gpsimd.tensor_tensor(CR[:, 0], C[:, w], CS[:, 0], ALU.subtract).then_inc(c_rest, 8)
                        pool.wait_ge(c_part, g * 3 + 2)
                        pool.wait_ge(c_rest, g * 16 + 8)
                        nc.gpsimd.tensor_tensor(CR[:, 1], CR[:, 0], CS[:, 1], ALU.subtract).then_inc(c_rest, 8)

            @block.tensor
            def _(pe):
                pe.wait_ge(ready, 4)
                with pe.Fori(0, NG // 2) as h:
                    for w in range(2):
                        g = h * 2 + w
                        pe.wait_ge(c_in, g * 16 + 16)
                        pe.wait_ge(ct_done, g * KC)
                        for k in range(KC):
                            for j in range(G):
                                mm = nc.tensor.transpose(psC[:, k, j * P:(j + 1) * P],
                                                         C[:, w, j, k * P:(k + 1) * P], ident[:])
                        mm.then_inc(turned, 16)

            @block.scalar
            def _(act):
                with act.Fori(0, NG // 2) as h:
                    for w in range(2):
                        g = h * 2 + w
                        act.wait_ge(c_in, g * 16 + 16)
                        act.wait_ge(c_out, g * (16 * 3))
                        nc.scalar.copy(CS[:, 0], C[:, w]).then_inc(c_part, 1)
                        act.wait_ge(z_done, g * G + G)
                        act.wait_ge(z_out, g * (16 * 3))
                        nc.scalar.copy(ZS[:, 0], Z[:]).then_inc(z_part, 1)
                        act.wait_ge(turned, g * 16 + 16)
                        for k in range(KC):
                            nc.scalar.copy(CT[:, k, bass.ds(g * (G * P), G * P)], psC[:, k, :]).then_inc(ct_done, 1)
                        act.wait_ge(c_rest, g * 16 + 8)
                        nc.scalar.copy(CS[:, 1], CR[:, 0]).then_inc(c_part, 1)
                        act.wait_ge(z_rest, g * 2 + 1)
                        nc.scalar.copy(ZS[:, 1], ZR[:, 0]).then_inc(z_part, 1)
                        act.wait_ge(c_rest, g * 16 + 16)
                        nc.scalar.copy(CS[:, 2], CR[:, 1]).then_inc(c_part, 1)
                        act.wait_ge(z_rest, g * 2 + 2)
                        nc.scalar.copy(ZS[:, 2], ZR[:, 1]).then_inc(z_part, 1)

            @block.vector
            def _(dve):
                with dve.Fori(0, NG // 2) as h:
                    for w in range(2):
                        g = h * 2 + w
                        dve.wait_ge(x_in, g * 16 + 16)
                        dve.wait_ge(rstd_done, g)
                        for j in range(G):
                            nc.vector.bn_stats(stats[:, j, :], X[:, g * G + j, :])
                        dve.drain()
                        for j in range(G):
                            nc.vector.bn_aggr(mv[:, j, :], stats[:, j, :]).then_inc(stats_done, 1)
                        dve.wait_ge(rstd_done, g + 1)
                        dve.wait_ge(stats_done, g * G + G)
                        for j in range(G):
                            nc.vector.tensor_scalar(Z[:, j, :], X[:, g * G + j, :], mv[:, j, 0:1], rstd[:, j:j + 1],
                                                    ALU.subtract, ALU.mult).then_inc(z_done, 1)
                        dve.wait_ge(z_part, g * 3 + 1)
                        dve.wait_ge(z_done, g * G + G)
                        nc.vector.tensor_tensor(ZR[:, 0], Z[:], ZS[:, 0], ALU.subtract).then_inc(z_rest, 1)
                        dve.wait_ge(z_part, g * 3 + 2)
                        dve.wait_ge(z_rest, g * 2 + 1)
                        nc.vector.tensor_tensor(ZR[:, 1], ZR[:, 0], ZS[:, 1], ALU.subtract).then_inc(z_rest, 1)

def row_attention(nc, io, X, CT, identb, zq, ck, o_num, o_den):
    R = 9 * DH0
    RM = R + 3
    H2 = 2 * NH0
    QUADS = H2 // 4
    PAIR = 16 * 12
    SCALE = float(DH0) ** -0.5
    with ExitStack() as ctx:
        s = Scope(nc, ctx, "ratt")
        Q9 = s.sb("Q9", [P, 2, H2, 2, D], BF16)
        K9 = s.sb("K9", [P, 2, H2, 2, D], BF16)
        E = s.sb("E", [P, 2, 4, KC, D])
        V9 = s.sb("V9", [P, 2, KC, NH0, 32])
        nmax = s.sb("nmax", [P, 2, 2, NH0])
        rest = s.sb("rest", [P, 2, 2, NH0])
        zero = s.sb("zero", [P, 2, NH0])
        parts = s.sb("parts", [P, 2, P], BF16)
        rows = s.sb("rows", [2 * 3 * NH0, 2, P], BF16)
        O = s.sb("O", [P, 2, QUADS, D])
        num = s.sb("num", [P, 2, D])
        den = s.sb("den", [P, 2, D])
        psS = s.ps("psS", [P, 2, 2, D])
        psT = s.ps("psT", [P, 2, 2, KC, D])
        psO = s.ps("psO", [P, 2, D])
        psM = s.ps("psM", [P, 2, 512], BF16)
        ready, ones_set = s.sem("ready"), s.sem("ones_set")
        pair_in = [s.sem(f"pair_in{b}") for b in range(2)]
        scores, maxed, pool_step, split, turned, row_out = (
            s.sem(x) for x in ("scores", "maxed", "pool_step", "split", "turned", "row_out"))
        row_in = [s.sem(f"row_in{b}") for b in range(2)]
        o_back = [s.sem(f"o_back{b}") for b in range(2)]
        shifted, exped, v_in, pv, o_out = (s.sem(x) for x in ("shifted", "exped", "v_in", "pv", "o_out"))
        to_dram, recip, scaled, added = (s.sem(x) for x in ("to_dram", "recip", "scaled", "added"))

        with nc.Block() as block:

            @block.gpsimd
            def _(pool):
                nc.gpsimd.memset(zero[:], 0.0).then_inc(ready, 1)
                nc.gpsimd.memset(parts[:], 0.0).then_inc(ready, 1)
                nc.gpsimd.memset(V9[:], 0.0).then_inc(ready, 1)
                pool.wait_ge(ready, 3)
                nc.gpsimd.memset(V9[:, :, :, :, DH0:DH0 + 1], 1.0).then_inc(ready, 1)
                pool.wait_ge(ready, 4)

                def take(t, b):
                    unit = t * 2 + b
                    if not isinstance(t, int) or t > 0:
                        pool.wait_ge(pv, t * QUADS + (2 * b - 2))
                    nc.gpsimd.tensor_copy(
                        V9[:, b, :, :, 0:DH0],
                        CT[:, :, bass.ds(t * P + b * L, L)].rearrange("p k (h r) -> p k h r", r=DH0),
                    ).then_inc(v_in, 1)

                def split_max(t, b):
                    unit = t * 2 + b
                    step = Steps(pool, pool_step, 4, unit)
                    pool.wait_ge(maxed, t * H2 + (b + 1) * NH0)
                    if not isinstance(t, int) or t > 0:
                        pool.wait_ge(turned, unit - 1)
                    p = parts[:, b].rearrange("p (c q) -> p c q", c=2)[:, :, 0:3 * NH0].rearrange(
                        "p c (s h) -> p c s h", s=3)
                    step(nc.gpsimd.tensor_tensor(p[:, :, 0], nmax[:, b], zero[:], ALU.add))
                    step(nc.gpsimd.tensor_tensor(rest[:, 0], nmax[:, b], p[:, :, 0], ALU.subtract))
                    step(nc.gpsimd.tensor_tensor(p[:, :, 1], rest[:, 0], zero[:], ALU.add))
                    step(nc.gpsimd.tensor_tensor(rest[:, 1], rest[:, 0], p[:, :, 1], ALU.subtract))
                    nc.gpsimd.tensor_tensor(p[:, :, 2], rest[:, 1], zero[:], ALU.add).then_inc(split, 1)
                    step.end()

                def scale(t, par):
                    pool.wait_ge(recip, t + 1)
                    nc.gpsimd.tensor_tensor(num[:, par], num[:, par], den[:, par], ALU.mult).then_inc(scaled, 1)

                def step(i, k, has_s=True, has_t=True):
                    t = i * 4 + k
                    for b in range(2):
                        if has_t:
                            take(t, b)
                        if has_s:
                            split_max(t + 1, b)
                    if has_t and (k > 0 or not isinstance(i, int) or i > 0):
                        scale(t - 1, (k + 1) % 2)

                split_max(0, 0)
                split_max(0, 1)
                step(0, 0)
                step(0, 1)
                step(0, 2)
                step(0, 3)
                with pool.Fori(1, T // 4 - 1) as i:
                    for k in range(4):
                        step(i, k)
                for k in range(4):
                    step(T // 4 - 1, k, has_s=k < 3)
                scale(T - 1, 1)

            @block.sync
            def _(sp):
                def load(t, pb):
                    for a in range(3):
                        sp.dma_start(Q9[24 * a:24 * a + 24, pb].rearrange("p h u m -> p h (u m)"),
                                     zq.rearrange("s r h t m -> (s r) h (t m)")[:, :, bass.ds(t * D, 2 * D)]
                                     ).then_inc(pair_in[pb], 16)
                    for a in range(3):
                        for c in range(3):
                            sp.dma_start(K9[24 * a + 8 * c:24 * a + 8 * c + 8, pb].rearrange("p h u m -> p h (u m)"),
                                         ck[a].rearrange("r h t m -> r h (t m)")[:, :, bass.ds(t * D, 2 * D)]
                                         ).then_inc(pair_in[pb], 16)

                def bring_row(t, pb, u, b):
                    sp.wait_ge(row_out, t * 2 + b + 1)
                    for c in range(2):
                        sp.dma_start(Q9[R:RM, pb, b * NH0:(b + 1) * NH0, u, c * P:(c + 1) * P],
                                     rows[c * 24:c * 24 + 24, b, :]).then_inc(row_in[b], 16)

                def out(t, par):
                    sp.wait_ge(o_out, t * QUADS + QUADS)
                    for g in range(4):
                        sp.dma_start(o_num.rearrange("t q g c m -> g c (t q) m")[g][:, bass.ds(t * QUADS, QUADS), :],
                                     O[32 * g:32 * g + DH0, par]).then_inc(to_dram, 16)
                        sp.dma_start(o_den.rearrange("t q g m -> g (t q) m")[g:g + 1][:, bass.ds(t * QUADS, QUADS), :],
                                     O[32 * g + DH0:32 * g + DH0 + 1, par]).then_inc(to_dram, 16)

                def back(t, par):
                    sp.wait_ge(to_dram, t * 128 + 128)
                    if not isinstance(t, int) or t > 1:
                        sp.wait_ge(added, t * 16 - 16)
                    sp.dma_start(num[:, par], o_num.rearrange("t q g c m -> (t q g c) m")[bass.ds(t * P, P)]
                                 ).then_inc(o_back[par], 16)
                    sp.dma_start(den[:, par],
                                 spread(o_den.rearrange("t q g m -> (t q g) m")[bass.ds(t * H2, H2)], 1, DH0)
                                 ).then_inc(o_back[par], 16)

                def step(i, k, has_s=True, has_t=True):
                    t = i * 4 + k
                    past = not isinstance(i, int) or i > 0
                    pb1, u1 = ((k + 1) // 2) % 2, (k + 1) % 2
                    if past or k > 0:
                        out(t - 1, (k + 1) % 2)
                    if has_s:
                        bring_row(t + 1, pb1, u1, 0)
                    if past or k > 0:
                        back(t - 1, (k + 1) % 2)
                    if k % 2 == 1 and has_s and not (isinstance(i, int) and i == T // 4 - 1):
                        sp.wait_ge(shifted, t * 8 + 8)
                        load(t + 3, (k // 2) % 2)
                    if has_s:
                        bring_row(t + 1, pb1, u1, 1)

                sp.wait_ge(ones_set, 1)
                load(0, 0)
                load(2, 1)
                bring_row(0, 0, 0, 0)
                bring_row(0, 0, 0, 1)
                for k in range(4):
                    step(0, k)
                with sp.Fori(1, T // 4 - 1) as i:
                    for k in range(4):
                        step(i, k)
                for k in range(4):
                    step(T // 4 - 1, k, has_s=k < 3)
                out(T - 1, 1)
                back(T - 1, 1)

            @block.tensor
            def _(pe):
                def score(t, pb, u, hh):
                    if not isinstance(t, int) or t > 0 or hh > 1:
                        pe.wait_ge(maxed, t * H2 + (hh - 1))
                    for c in range(2):
                        mm = nc.tensor.matmul(psS[:, hh % 2, c, :], Q9[0:R, pb, hh, u, c * P:(c + 1) * P],
                                              K9[0:R, pb, hh, u, :], start=True, stop=True)
                    mm.then_inc(scores, 1)

                def turn_max(t, b):
                    unit = t * 2 + b
                    pe.wait_ge(split, unit + 1)
                    pe.wait_ge(row_out, unit)
                    nc.tensor.transpose(psM[:, b, 0:P], parts[:, b, :], identb[:]).then_inc(turned, 1)

                def shift(t, pb, u, hh):
                    pair = t * 8 + hh // 2
                    if not isinstance(t, int) or t > 0 or hh > 2:
                        pe.wait_ge(exped, pair - 1)
                    for h in range(hh, hh + 2):
                        for c in range(KC):
                            mm = nc.tensor.matmul(psT[:, (hh // 2) % 2, h % 2, c, :],
                                                  K9[0:RM, pb, h, u, c * P:(c + 1) * P],
                                                  Q9[0:RM, pb, h, u, :], start=True, stop=True)
                    mm.then_inc(shifted, 1)

                def values(t, qd):
                    quad = t * QUADS + qd
                    pe.wait_ge(exped, t * 8 + 2 * qd + 2)
                    pe.wait_ge(v_in, t * 2 + qd // 2 + 1)
                    pe.wait_ge(o_out, quad)
                    for c in range(KC):
                        for g in range(4):
                            h = (qd * 4 + g) % NH0
                            mm = nc.tensor.matmul(psO[32 * g:32 * g + 32, qd % 2, :], V9[:, qd // 2, c, h, :],
                                                  E[:, qd % 2, g, c, :], start=(c == 0), stop=(c == KC - 1),
                                                  skip_group_check=True)
                    mm.then_inc(pv, 1)

                def step(i, k, has_s=True, has_t=True):
                    t = i * 4 + k
                    pb0, u0 = (k // 2) % 2, k % 2
                    pb1, u1 = ((k + 1) // 2) % 2, (k + 1) % 2
                    first_tile = isinstance(i, int) and i == 0 and k == 0
                    if has_s and k % 2 == 1:
                        pe.wait_ge(pair_in[pb1], (i + 1 + k // 2) * PAIR)
                    for b in range(2):
                        if has_t:
                            pe.wait_ge(row_in[b], t * 32 + 32)
                        for pr in range(4):
                            hh = b * NH0 + 2 * pr
                            if has_s:
                                score(t + 1, pb1, u1, hh)
                                score(t + 1, pb1, u1, hh + 1)
                            if pr == 2:
                                if b == 0:
                                    if not first_tile:
                                        turn_max(t, 1)
                                elif has_s:
                                    turn_max(t + 1, 0)
                            if has_t:
                                shift(t, pb0, u0, hh)
                                if pr % 2 == 1:
                                    qd = 2 * b + pr // 2
                                    if qd > 0:
                                        values(t, qd - 1)
                                    elif not first_tile:
                                        values(t - 1, QUADS - 1)

                pe.wait_ge(ready, 4)
                pe.wait_ge(pair_in[0], PAIR)
                for hh in range(H2):
                    score(0, 0, 0, hh)
                turn_max(0, 0)
                turn_max(0, 1)
                for k in range(4):
                    step(0, k)
                with pe.Fori(1, T // 4 - 1) as i:
                    for k in range(4):
                        step(i, k)
                for k in range(4):
                    step(T // 4 - 1, k, has_s=k < 3)
                values(T - 1, QUADS - 1)

            @block.scalar
            def _(act):
                def row(t, b):
                    unit = t * 2 + b
                    act.wait_ge(turned, unit + 1)
                    if not isinstance(t, int) or t > 0:
                        act.wait_ge(row_in[b], t * 32)
                    nc.scalar.copy(rows[:, b, :], psM[0:48, b, 0:P]).then_inc(row_out, 1)

                def exp(t, hh):
                    quad = t * QUADS + hh // 4
                    act.wait_ge(shifted, t * 8 + hh // 2 + 1)
                    if not isinstance(t, int) or t > 0 or hh > 7:
                        act.wait_ge(pv, quad - 1)
                    nc.scalar.activation(E[:, (hh // 4) % 2, hh % 4:hh % 4 + 2], psT[:, (hh // 2) % 2], ACT.Exp,
                                         scale=SCALE).then_inc(exped, 1)

                def leave(t, qd):
                    act.wait_ge(pv, t * QUADS + qd + 1)
                    if qd == 0 and (not isinstance(t, int) or t > 1):
                        act.wait_ge(to_dram, (t - 1) * 128)
                    par = leave.par
                    nc.scalar.copy(O[:, par, qd, :], psO[:, qd % 2, :]).then_inc(o_out, 1)

                def step(i, k, has_s=True, has_t=True):
                    t = i * 4 + k
                    first_tile = isinstance(i, int) and i == 0 and k == 0
                    for b in range(2):
                        for pr in range(4):
                            exp(t, b * NH0 + 2 * pr)
                            if pr == 2:
                                if b == 0:
                                    if not first_tile:
                                        row(t, 1)
                                elif has_s:
                                    row(t + 1, 0)
                            if pr % 2 == 1:
                                qd = 2 * b + pr // 2
                                if qd > 0:
                                    leave.par = k % 2
                                    leave(t, qd - 1)
                                elif not first_tile:
                                    leave.par = (k + 1) % 2
                                    leave(t - 1, QUADS - 1)

                row(0, 0)
                row(0, 1)
                for k in range(4):
                    step(0, k)
                with act.Fori(1, T // 4 - 1) as i:
                    for k in range(4):
                        step(i, k)
                for k in range(4):
                    step(T // 4 - 1, k, has_s=k < 3)
                leave.par = 1
                leave(T - 1, QUADS - 1)

            @block.vector
            def _(dve):
                def max_of(t, hh):
                    b = hh // NH0
                    if hh % NH0 == 0 and (not isinstance(t, int) or t > 0):
                        dve.wait_ge(split, t * 2 + b - 1)
                    dve.wait_ge(scores, t * H2 + hh + 1)
                    nc.vector.tensor_reduce(nmax[:, b, :, hh % NH0], psS[:, hh % 2], AX.X, ALU.max,
                                            negate=True).then_inc(maxed, 1)

                def invert(t, par, half):
                    dve.wait_ge(o_back[par], half * 32 + 32)
                    nc.vector.reciprocal(den[:, par], den[:, par]).then_inc(recip, 1)

                def add(t, par):
                    dve.wait_ge(scaled, t + 1)
                    nc.vector.tensor_tensor(X[:, t, :], X[:, t, :], num[:, par], ALU.add).then_inc(added, 16)

                def step(i, k, has_s=True, has_t=True):
                    t = i * 4 + k
                    past = not isinstance(i, int) or i > 0
                    if has_s:
                        for hh in range(H2):
                            max_of(t + 1, hh)
                            if hh == 7 and (past or k > 1):
                                add(t - 2, k % 2)
                    elif past:
                        add(t - 2, k % 2)
                    if past or k > 0:
                        invert(t - 1, (k + 1) % 2, i * 2 + (k - 1) // 2)

                nc.vector.memset(K9[64:96], 1.0).then_inc(ones_set, 1)
                for hh in range(H2):
                    max_of(0, hh)
                for k in range(4):
                    step(0, k)
                with dve.Fori(1, T // 4 - 1) as i:
                    for k in range(4):
                        step(i, k)
                for k in range(4):
                    step(T // 4 - 1, k, has_s=k < 3)
                add(T - 2, 0)
                invert(T - 1, 1, T // 2 - 1)
                add(T - 1, 1)

def pipeline(engine, front, back):
    front(0, 0)
    front(1, 1)
    back(0, 0)
    with engine.Fori(0, NG // 2 - 1) as h:
        front(h * 2 + 2, 0)
        back(h * 2 + 1, 1)
        front(h * 2 + 3, 1)
        back(h * 2 + 2, 0)
    back(NG - 1, 1)

def later(g, rounds):
    return not isinstance(g, int) or g >= rounds

class Norm:

    def __init__(self, nc, s, X, eps=LN_EPS):
        self.nc, self.X, self.eps_value = nc, X, eps
        self.stats = s.sb("stats", [P, G, 6])
        self.mv = s.sb("mv", [P, G, 2])
        self.veps = s.sb("veps", [P, G])
        self.rstd = s.sb("rstd", [P, G])
        self.mhalf = s.sb("mhalf", [P, G])
        self.eps = s.sb("eps", [P, G])
        self.set = s.sem("norm_set")
        self.stats_done, self.veps_done = s.sem("stats_done"), s.sem("veps_done")
        self.rstd_done, self.normed = s.sem("rstd_done"), s.sem("normed")

    def constants(self, pool):
        self.nc.gpsimd.memset(self.mhalf[:], -0.5).then_inc(self.set, 1)
        self.nc.gpsimd.memset(self.eps[:], self.eps_value).then_inc(self.set, 1)
        pool.wait_ge(self.set, 2)

    def on_pool(self, pool, g):
        pool.wait_ge(self.stats_done, g * G + G)
        self.nc.gpsimd.tensor_tensor(self.veps[:], self.mv[:, :, 1], self.eps[:], ALU.add).then_inc(self.veps_done, 1)
        pool.wait_ge(self.veps_done, g + 1)
        self.nc.gpsimd.tensor_tensor(self.rstd[:], self.veps[:], self.mhalf[:], ALU.pow).then_inc(self.rstd_done, 1)

    def on_vector(self, dve, g, Z):
        for j in range(G):
            self.nc.vector.bn_stats(self.stats[:, j, :], self.X[:, g * G + j, :])
        dve.drain()
        for j in range(G):
            self.nc.vector.bn_aggr(self.mv[:, j, :], self.stats[:, j, :]).then_inc(self.stats_done, 1)
        dve.wait_ge(self.rstd_done, g + 1)
        dve.wait_ge(self.stats_done, g * G + G)
        for j in range(G):
            self.nc.vector.tensor_scalar(Z[:, j, :], self.X[:, g * G + j, :], self.mv[:, j, 0:1],
                                         self.rstd[:, j:j + 1], ALU.subtract, ALU.mult).then_inc(self.normed, 1)

def selected_ffn(nc, io, X, ident):
    FC = FF // P
    SL = 2 * KEEP
    with ExitStack() as ctx:
        s = Scope(nc, ctx, "sffn")
        norm = Norm(nc, s, X)
        W1 = s.sb("W1", [P, KC, FF])
        W2 = s.sb("W2", [P, FC, D])
        b1 = s.sb("b1", [P, FC])
        b2 = s.sb("b2", [P, D])
        wr = s.sb("wr", [P, D])
        br = s.sb("br", [P, 1])
        Z = s.sb("Z", [P, 2, G, D])
        zw = s.sb("zw", [P, D])
        sc = s.sb("sc", [P, 2, G])
        same = s.sb("same", [P, P])
        own = s.sb("own", [P, L])
        before = s.sb("before", [P, L])
        slot = s.sb("slot", [P, SL])
        diag = s.sb("diag", [P, G, L])
        work = s.sb("work", [P, 3, G, L])
        mine = s.sb("mine", [P, G])
        rank = s.sb("rank", [P, G])
        pick = s.sb("pick", [P, 2, G, SL])
        XS = s.sb("XS", [P, KC, G * SL])
        PT = s.sb("PT", [P, G, P])
        H = s.sb("H", [P, FC, G * SL])
        OS = s.sb("OS", [P, 2, D])
        psR = s.ps("psR", [P, G, L + L])
        psG = s.ps("psG", [P, KC, G * SL])
        psP = s.ps("psP", [P, 4, P])
        psH = s.ps("psH", [P, 2, 2, G * SL])
        psO = s.ps("psO", [P, 2, D])
        psX = s.ps("psX", [P, G, D])
        w_in, ready = s.sem("w_in"), s.sem("ready")
        steps, diag_done, rows_done, pick_done = (s.sem(x) for x in ("steps", "diag_done", "rows_done", "pick_done"))
        gathered, turned, xs_done, pt_done = (s.sem(x) for x in ("gathered", "turned", "xs_done", "pt_done"))
        hidden, gelued, put, os_done, scattered, x_done = (
            s.sem(x) for x in ("hidden", "gelued", "put", "os_done", "scattered", "x_done"))
        PER = 12

        with nc.Block() as block:

            @block.sync
            def _(sp):
                sp.dma_start(W1[:], io["L0_ffn_w1"].rearrange("(k p) f -> p k f", p=P)).then_inc(w_in, 16)
                sp.dma_start(W2[:], io["L0_ffn_w2"].rearrange("(k p) d -> p k d", p=P)).then_inc(w_in, 16)
                with nc.allow_non_contiguous_dma(reason="one column of biases for each chunk"):
                    sp.dma_start(b1[:], io["L0_ffn_b1"].rearrange("(k p) -> p k", p=P)).then_inc(w_in, 16)
                sp.dma_start(b2[:], spread(io["L0_ffn_b2"], 0, P)).then_inc(w_in, 16)
                sp.dma_start(wr[:], spread(io["L0_ffn_w_r"], 0, P)).then_inc(w_in, 16)
                sp.dma_start(br[:], spread(io["L0_ffn_b_r"], 0, P)).then_inc(w_in, 16)
                sp.wait_ge(w_in, 96)

            @block.gpsimd
            def _(pool):
                step = Steps(pool, ready, 14)
                select = lambda out, op, fill, base, cm, pattern: step(nc.gpsimd.affine_select(
                    out=out, in_=out, compare_op=op, fill=fill, base=base, pattern=pattern, channel_multiplier=cm))
                step(nc.gpsimd.memset(same[:], 1.0))
                select(same[0:L, :], ALU.is_ge, 0.0, L - 1, 0, [[-1, P]])
                select(same[L:P, :], ALU.is_ge, 0.0, -L, 0, [[1, P]])
                step(nc.gpsimd.memset(own[:], 0.0))
                select(own[0:L, :], ALU.not_equal, 1.0, 0, 1, [[-1, L]])
                select(own[L:P, :], ALU.not_equal, 1.0, 0, 1, [[-1, L]])
                step(nc.gpsimd.memset(before[:], 1.0))
                select(before[0:L, :], ALU.is_gt, 0.0, 0, 1, [[-1, L]])
                select(before[L:P, :], ALU.is_gt, 0.0, 0, 1, [[-1, L]])
                step(nc.gpsimd.iota(slot[:], pattern=[[0, 2], [1, KEEP]], base=0, channel_multiplier=0,
                                    allow_small_or_imprecise_dtypes=True))
                step(nc.gpsimd.memset(slot[0:L, KEEP:], -1.0))
                step(nc.gpsimd.memset(slot[L:P, 0:KEEP], -1.0))
                step(nc.gpsimd.memset(PT[0:L, :, :], 0.0))
                step(nc.gpsimd.memset(PT[L:P, :, :], 0.0))
                step.end()
                norm.constants(pool)
                pipeline(pool, lambda g, w: norm.on_pool(pool, g), lambda g, w: None)

            @block.vector
            def _(dve):
                def front(g, w):
                    if later(g, 2):
                        dve.wait_ge(gathered, g - 1)
                        dve.wait_ge(turned, g - 1)
                    norm.on_vector(dve, g, Z[:, w])
                    step = Steps(dve, steps, PER, g)
                    dve.wait_ge(norm.normed, g * G + G)
                    dve.wait_ge(w_in, 96)
                    dve.wait_ge(ready, 14)
                    for j in range(G):
                        step(nc.vector.tensor_tensor_reduce(zw[:], Z[:, w, j, :], wr[:], 1.0, 0.0, ALU.mult, ALU.add,
                                                            sc[:, 0, j:j + 1]))
                    step(nc.vector.tensor_scalar(sc[:, 1], sc[:, 0], br[:, 0:1], None, ALU.add))
                    nc.vector.tensor_tensor(diag[:], spread(own[:], 1, G), spread(sc[:, 1], 2, L),
                                            ALU.mult).then_inc(diag_done, 1)
                    dve.wait_ge(rows_done, g + 1)
                    R = psR[:, :, 0:L]
                    step(nc.vector.tensor_tensor(work[:, 0], R, spread(own[:], 1, G), ALU.mult))
                    step(nc.vector.tensor_reduce(mine[:], work[:, 0], AX.X, ALU.add))
                    step(nc.vector.tensor_tensor(work[:, 1], R, spread(mine[:], 2, L), ALU.is_equal))
                    step(nc.vector.tensor_tensor(work[:, 2], work[:, 1], spread(before[:], 1, G), ALU.mult))
                    step(nc.vector.tensor_tensor(work[:, 0], R, spread(mine[:], 2, L), ALU.is_gt))
                    step(nc.vector.tensor_tensor(work[:, 1], work[:, 0], work[:, 2], ALU.add))
                    step(nc.vector.tensor_reduce(rank[:], work[:, 1], AX.X, ALU.add))
                    nc.vector.tensor_tensor(pick[:, w], spread(slot[:], 1, G), spread(rank[:], 2, SL),
                                            ALU.is_equal).then_inc(pick_done, 1)
                    step.end()

                def back(g, w):
                    dve.wait_ge(put, g + 1)
                    dve.wait_ge(w_in, 96)
                    dve.wait_ge(scattered, g)
                    nc.vector.tensor_tensor(OS[:], psO[:], spread(b2[:], 1, 2), ALU.add).then_inc(os_done, 1)
                    dve.wait_ge(scattered, g + 1)
                    nc.vector.tensor_tensor(X[:, bass.ds(g * G, G), :], X[:, bass.ds(g * G, G), :], psX[:],
                                            ALU.add).then_inc(x_done, 1)

                pipeline(dve, front, back)

            @block.tensor
            def _(pe):
                def front(g, w):
                    pe.wait_ge(diag_done, g + 1)
                    pe.wait_ge(pick_done, g)
                    nc.tensor.matmul(psR[:, :, 0:L], same[:], diag[:], start=True, stop=True).then_inc(rows_done, 1)

                def back(g, w):
                    pe.wait_ge(pick_done, g + 1)
                    pe.wait_ge(xs_done, g)
                    for k in range(KC):
                        for j in range(G):
                            mm = nc.tensor.matmul(psG[:, k, j * SL:(j + 1) * SL], Z[:, w, j, k * P:(k + 1) * P],
                                                  pick[:, w, j, :], start=True, stop=True)
                    mm.then_inc(gathered, 1)
                    pe.wait_ge(pt_done, g * 2)
                    for jj in range(2):
                        mm = nc.tensor.transpose(psP[:, jj, :], pick[:, w, 2 * jj:2 * jj + 2, :].rearrange(
                            "p j s -> p (j s)"), ident[:])
                    mm.then_inc(turned, 1)
                    pe.wait_ge(xs_done, g + 1)
                    pe.wait_ge(w_in, 96)
                    for f in range(FC // 2):
                        if later(g, 1) or f > 1:
                            pe.wait_ge(gelued, g * FC + 2 * f - 2)
                        for ff in range(2):
                            c = 2 * f + ff
                            for k in range(KC):
                                mm = nc.tensor.matmul(psH[:, f % 2, ff, :], W1[:, k, c * P:(c + 1) * P], XS[:, k, :],
                                                      start=(k == 0), stop=(k == KC - 1))
                        mm.then_inc(hidden, 1)
                    pe.wait_ge(gelued, g * FC + FC)
                    pe.wait_ge(os_done, g)
                    for b in range(2):
                        for c in range(FC):
                            mm = nc.tensor.matmul(psO[:, b, :], H[:, c, b * P:(b + 1) * P], W2[:, c, :],
                                                  start=(c == 0), stop=(c == FC - 1))
                    mm.then_inc(put, 1)
                    pe.wait_ge(os_done, g + 1)
                    pe.wait_ge(pt_done, g * 2 + 2)
                    pe.wait_ge(x_done, g)
                    for j in range(G):
                        mm = nc.tensor.matmul(psX[:, j, :], PT[:, j, :], OS[:, j // 2, :], start=True, stop=True)
                    mm.then_inc(scattered, 1)

                pe.wait_ge(ready, 14)
                pipeline(pe, front, back)

            @block.scalar
            def _(act):
                def back(g, w):
                    act.wait_ge(gathered, g + 1)
                    nc.scalar.copy(XS[:], psG[:]).then_inc(xs_done, 1)
                    act.wait_ge(turned, g + 1)
                    act.wait_ge(scattered, g)
                    nc.scalar.copy(PT[0:SL, 0:G:2, :], psP[0:SL, 0:2, :]).then_inc(pt_done, 1)
                    nc.scalar.copy(PT[SL:P, 1:G:2, :], psP[SL:P, 0:2, :]).then_inc(pt_done, 1)
                    for c in range(FC):
                        act.wait_ge(hidden, g * (FC // 2) + c // 2 + 1)
                        if c == 0:
                            act.wait_ge(put, g)
                        nc.scalar.activation(H[:, c, :], psH[:, (c // 2) % 2, c % 2, :], ACT.Gelu_apprx_tanh,
                                             bias=b1[:, c:c + 1]).then_inc(gelued, 1)

                act.wait_ge(w_in, 96)
                act.wait_ge(ready, 14)
                pipeline(act, lambda g, w: None, back)

HC = NH // KC
NP = NH // 2
VW = DH + 1
BG = 2 * G
HG = G * P // 2

def turn_weights(nc, name, ident, matrices):
    with ExitStack() as ctx:
        s = Scope(nc, ctx, name)
        M = len(matrices)
        W = s.sb("W", [P, M, KC, D])
        psT = s.ps("psT", [P, M, KC, D])
        w_in, turned, taken = (s.sem(x) for x in ("w_in", "turned", "taken"))
        with nc.Block() as block:

            @block.sync
            def _(sp):
                for m, (dram, WT) in enumerate(matrices):
                    sp.dma_start(W[:, m], dram.rearrange("(k p) d -> p k d", p=P)).then_inc(w_in, 16)
                sp.wait_ge(w_in, 16 * M)

            @block.tensor
            def _(pe):
                pe.wait_ge(w_in, 16 * M)
                for m in range(M):
                    for k in range(KC):
                        for c in range(KC):
                            mm = nc.tensor.transpose(psT[:, m, k, c * P:(c + 1) * P], W[:, m, c, k * P:(k + 1) * P],
                                                     ident[:])
                    mm.then_inc(turned, 1)

            @block.scalar
            def _(act):
                for m, (dram, WT) in enumerate(matrices):
                    act.wait_ge(turned, m + 1)
                    nc.scalar.copy(WT[:], psT[:, m]).then_inc(taken, 1)

class Heads:

    def __init__(self, nc, s, ident):
        self.nc, self.ident = nc, ident
        self.KX = s.sb("KX", [P, 2, KC, HC, HG])
        self.VB = s.sb("VB", [P, 2, BG, NP, 2, VW])
        self.QT = s.sb("QT", [P, 2, KC, G * P])
        self.PB = s.sb("PB", [P, 2, NH, L])
        self.PT = s.sb("PT", [P, 2, NP, P])
        self.psS = s.ps("psS", [P, KC, HC * L])
        self.psP = s.ps("psP", [P, 2, NP // 2, P])
        self.psO = s.ps("psO", [P, 512])
        self.set = s.sem("h_set")
        self.kx_in = [s.sem(f"kx_in{w}") for w in range(2)]
        self.scored, self.s_taken, self.weighted, self.turned, self.pt_done, self.valued, self.o_taken = (
            s.sem(x) for x in ("scored", "s_taken", "weighted", "p_turned", "pt_done", "valued", "o_taken"))

    def constants(self, pool):
        gp = self.nc.gpsimd
        gp.memset(self.KX[:], 0.0).then_inc(self.set, 1)
        gp.memset(self.VB[:], 0.0).then_inc(self.set, 1)
        pool.wait_ge(self.set, 2)
        gp.memset(self.VB[0:L, :, :, :, 0, DH:], 1.0).then_inc(self.set, 1)
        gp.memset(self.VB[L:P, :, :, :, 1, DH:], 1.0).then_inc(self.set, 1)
        pool.wait_ge(self.set, 4)

    def expand(self, sp, g, keys, free):
        for half in range(2):
            if free[half] is not None:
                sp.wait_ge(self.scored, free[half])
            for c in range(KC):
                for h in range(HC):
                    rows = slice(h * DH, (h + 1) * DH)
                    sp.dma_start(self.KX[rows, half, c, h, :], keys(rows, c, half)).then_inc(self.kx_in[half], 16)

    def free_after(self, sp, g):
        return [held(sp, g * G - 2) if later(g, 1) else None, held(sp, g * G)]

    def scores(self, pe, g, w, j):
        pe.wait_ge(self.s_taken, g * G + j)
        if j % 2 == 0:
            pe.wait_ge(self.kx_in[j // 2], g * 256 + 256)
        for c in range(KC):
            for b in range(2):
                at, key = (2 * j + b) * L, (2 * (j % 2) + b) * L
                mm = self.nc.tensor.matmul(self.psS[b * L:(b + 1) * L, c, :], self.QT[:, w, c, at:at + L],
                                           self.KX[:, j // 2, c, :, key:key + L], start=True, stop=True,
                                           skip_group_check=True)
        mm.then_inc(self.scored, 1)

    def turn(self, pe, g, j):
        t = g * G + j
        pe.wait_ge(self.weighted, t + 1)
        pe.wait_ge(self.pt_done, t * 2)
        for i in range(NP):
            mm = self.nc.tensor.transpose(self.psP[:, i // (NP // 2), i % (NP // 2), :],
                                          self.PB[:, j % 2, 2 * i:2 * i + 2, :].rearrange("p h t -> p (h t)"),
                                          self.ident[:])
            if i % (NP // 2) == NP // 2 - 1:
                mm.then_inc(self.turned, 1)

    def copy_turned(self, act, g, j):
        t = g * G + j
        for half in range(2):
            act.wait_ge(self.turned, 2 * t + half + 1)
            if later(g, 1) or j > 1:
                act.wait_ge(self.valued, t - 1)
            self.nc.scalar.copy(self.PT[:, j % 2, half * (NP // 2):(half + 1) * (NP // 2), :],
                                self.psP[:, half]).then_inc(self.pt_done, 1)

    def values(self, pe, g, w, j):
        t = g * G + j
        pe.wait_ge(self.pt_done, 2 * t + 2)
        pe.wait_ge(self.o_taken, t)
        for i in range(NP):
            for b in range(2):
                mm = self.nc.tensor.matmul(self.psO[b * L:(b + 1) * L, i * 2 * VW:(i + 1) * 2 * VW],
                                           self.PT[:, j % 2, i, b * L:(b + 1) * L],
                                           self.VB[:, w, 2 * j + b, i].rearrange("p h d -> p (h d)"), start=True,
                                           stop=True, skip_group_check=True)
        mm.then_inc(self.valued, 1)

    def out(self):
        return self.psO[:, 0:NH * VW].rearrange("p (h d) -> p h d", d=VW)

def pipeline3(engine, front_a, front_b, back, tail):
    def front(g, w, tail_too=True):
        front_a(g, w)
        if tail_too:
            tail(g - 2, w)
        front_b(g, w)

    front(0, 0, False)
    front(1, 1, False)
    back(0, 0)
    with engine.Fori(0, NG // 2 - 1) as h:
        front(h * 2 + 2, 0)
        back(h * 2 + 1, 1)
        front(h * 2 + 3, 1)
        back(h * 2 + 2, 0)
    tail(NG - 2, 0)
    back(NG - 1, 1)
    tail(NG - 1, 1)

def gated_attention(nc, io, X, CT, ident, identb):
    NG2 = 2 * NH
    with ExitStack() as ctx:
        s = Scope(nc, ctx, "gatt")
        norm = Norm(nc, s, X)
        heads = Heads(nc, s, ident)
        heads.s_taken = heads.weighted
        WZ, WK_, WV_, WC = (s.sb(x, [P, KC, NG2]) for x in ("WZ", "WK", "WV", "WC"))
        gbias = s.sb("gbias", [P, NG2])
        lscale = s.sb("lscale", [P, D])
        same, tri = s.sb("same", [P, P]), s.sb("tri", [P, P])
        own = s.sb("own", [P, L])
        mask = s.sb("mask", [P, HC, L], BF16)
        one = s.sb("one", [P, 1])
        mhalf64 = s.sb("mhalf64", [P, G * NH])
        Z = s.sb("Z", [P, G, D])
        CG = s.sb("CG", [P, KC, G * P])
        V2 = s.sb("V2", [P, BG, D])
        gates = s.sb("gates", [P, G, NG2])
        fw = s.sb("fw", [P, 5, G, NH])
        cum = s.sb("cum", [P, 2, G, NH])
        a = s.sb("a", [P, 2, G, NH])
        DA = s.sb("DA", [P, 2, NH, L])
        DB = s.sb("DB", [P, 2, NH, L])
        mx = s.sb("mx", [P, 2, G, NH])
        OG = s.sb("OG", [P, 2, G, NH, VW])
        cen = s.sb("cen", [P, G, NH, DH])
        sq = s.sb("sq", [P, G, NH, DH])
        tw = s.sb("tw", [P, 13, G, NH])
        psA = s.ps("psA", [P, 2, HC * L])
        psG = s.ps("psG", [P, 512])
        (w_in, ready, wc_steps, cg_in, v_in, used, g_used, taken, v_copied, f_steps, f_exp, f_ln, da_done,
         a_spread, maxed, a_taken, d_done, t_steps, e_done, sq_done, r_done, scaled, x_done) = (
             s.sem(x) for x in (
                 "w_in", "ready", "wc_steps", "cg_in", "v_in", "used", "g_used", "taken", "v_copied", "f_steps",
                 "f_exp", "f_ln", "da_done", "a_spread", "maxed", "a_taken", "d_done", "t_steps", "e_done",
                 "sq_done", "r_done", "scaled", "x_done"))
        READY = 16
        FPER, TPER = 6, 15

        with nc.Block() as block:

            @block.sync
            def _(sp):
                with nc.allow_non_contiguous_dma(reason="16 gates for each feature"):
                    for part, W in enumerate((WZ, WK_, WV_)):
                        for n, name in enumerate(("Wi", "Wf")):
                            sp.dma_start(W[:, :, n * NH:(n + 1) * NH],
                                         io["L1_xattn_" + name][part * D:(part + 1) * D, :].rearrange(
                                             "(k p) h -> p k h", p=P)).then_inc(w_in, 16)
                sp.dma_start(gbias[:, 0:NH], spread(io["L1_xattn_bi"], 0, P)).then_inc(w_in, 16)
                sp.dma_start(gbias[:, NH:NG2], spread(io["L1_xattn_bf"], 0, P)).then_inc(w_in, 16)
                sp.dma_start(lscale[:], spread(io["L1_xattn_ln_scale"], 0, P)).then_inc(w_in, 16)
                sp.wait_ge(w_in, 144)
                sp.wait_ge(heads.set, 4)
                c_dram = io["ctx_2048"].rearrange("b t d -> t b d")

                def front(g, w):
                    at, b0, vc = (held(sp, v) for v in (g * (G * P), g * BG, g * 2))
                    free = heads.free_after(sp, g)
                    sp.wait_ge(v_copied, vc)
                    for hp in range(2):
                        sp.dma_start(V2[hp * L:(hp + 1) * L], c_dram[:, bass.ds(b0, BG), :]).then_inc(v_in, 16)
                    sp.wait_ge(g_used, vc)
                    sp.dma_start(CG[:], CT[:, :, bass.ds(at, G * P)]).then_inc(cg_in, 16)
                    starts = [at, held(sp, at + HG)]
                    heads.expand(sp, g, lambda rows, c, half: CT[rows, c, bass.ds(starts[half], HG)], free)

                pipeline3(sp, front, lambda g, w: None, lambda g, w: None, lambda g, w: None)

            @block.gpsimd
            def _(pool):
                gp = nc.gpsimd
                heads.constants(pool)
                norm.constants(pool)
                step = Steps(pool, ready, READY)
                select = lambda out, op, fill, base, cm, pattern: step(gp.affine_select(
                    out=out, in_=out, compare_op=op, fill=fill, base=base, pattern=pattern, channel_multiplier=cm))
                step(gp.memset(same[:], 1.0))
                select(same[0:L, :], ALU.is_ge, 0.0, L - 1, 0, [[-1, P]])
                select(same[L:P, :], ALU.is_ge, 0.0, -L, 0, [[1, P]])
                step(gp.memset(tri[:], 1.0))
                select(tri[0:L, :], ALU.is_ge, 0.0, L - 1, 0, [[-1, P]])
                select(tri[0:L, :], ALU.is_ge, 0.0, 0, -1, [[1, P]])
                select(tri[L:P, :], ALU.is_ge, 0.0, -L, -1, [[1, P]])
                step(gp.memset(own[:], 0.0))
                select(own[0:L, :], ALU.not_equal, 1.0, 0, 1, [[-1, L]])
                select(own[L:P, :], ALU.not_equal, 1.0, 0, 1, [[-1, L]])
                step(gp.memset(mask[:], 0.0))
                select(mask[0:L], ALU.is_ge, -BIG, 0, 1, [[0, HC], [-1, L]])
                select(mask[L:P], ALU.is_ge, -BIG, 0, 1, [[0, HC], [-1, L]])
                step(gp.memset(one[:], 1.0))
                step(gp.memset(mhalf64[:], -0.5))
                step(gp.memset(OG[:], 0.0))
                step.end()
                pool.wait_ge(w_in, 144)

                def back(g, w):
                    for i in range(G):
                        t = g * G + i
                        pool.wait_ge(f_steps, g * FPER + FPER)
                        if later(g, 1) or i > 1:
                            pool.wait_ge(a_spread, t - 1)
                        gp.tensor_tensor(DA[:, i % 2], spread(own[:], 1, NH), spread(a[:, w, i], 2, L),
                                         ALU.mult).then_inc(da_done, 1)

                def tail(g, w):
                    pool.wait_ge(t_steps, g * TPER + 13)
                    gp.tensor_tensor(tw[:, 9].rearrange("p j h -> p (j h)"), tw[:, 8].rearrange("p j h -> p (j h)"),
                                     mhalf64[:], ALU.pow).then_inc(r_done, 1)
                    pool.wait_ge(t_steps, g * TPER + 15)
                    flat = cen[:].rearrange("p j h d -> p j (h d)")
                    gp.tensor_tensor(flat, flat, spread(lscale[:], 1, G), ALU.mult).then_inc(scaled, 1)
                    pool.wait_ge(scaled, g + 1)
                    xs = X[:, bass.ds(g * G, G), :]
                    gp.tensor_tensor(xs, xs, flat, ALU.add).then_inc(x_done, 1)

                pipeline3(pool, lambda g, w: norm.on_pool(pool, g), lambda g, w: None, back, tail)

            @block.vector
            def _(dve):
                v = nc.vector
                dve.wait_ge(w_in, 144)
                v.tensor_tensor(WC[:], WK_[:], WV_[:], ALU.add).then_inc(wc_steps, 1)
                dve.wait_ge(heads.set, 4)
                dve.wait_ge(ready, READY)

                def front_a(g, w):
                    dve.wait_ge(used, g * 2)
                    norm.on_vector(dve, g, Z)

                def front_b(g, w):
                    step = Steps(dve, f_steps, FPER, g)
                    dve.wait_ge(g_used, g * 2 + 1)
                    step(v.tensor_tensor(gates[:], psG[:, 0:G * NG2].rearrange("p (j n) -> p j n", n=NG2),
                                         spread(gbias[:], 1, G), ALU.add))
                    f = gates[:, :, NH:NG2]
                    step(v.scalar_tensor_tensor(fw[:, 0], f, -1.0, f, ALU.mult, ALU.min))
                    step(v.tensor_scalar(fw[:, 3], f, 0.0, None, ALU.min))
                    dve.wait_ge(f_ln, g + 1)
                    step(v.tensor_tensor(fw[:, 4], fw[:, 3], fw[:, 2], ALU.subtract))
                    dve.wait_ge(g_used, g * 2 + 2)
                    step(v.tensor_copy(cum[:, w].rearrange("p j h -> p (j h)"), psG[:, 0:G * NH]))
                    step(v.tensor_tensor(a[:, w], gates[:, :, 0:NH], cum[:, w], ALU.subtract))
                    step.end()

                def back(g, w):
                    for i in range(G + 1):
                        if i < G:
                            t = g * G + i
                            A = psA[:].rearrange("p c (h t) -> p (c h) t", t=L)
                            dve.wait_ge(a_spread, t + 1)
                            v.tensor_reduce(mx[:, w, i], A, AX.X, ALU.max).then_inc(maxed, 1)
                            dve.wait_ge(maxed, t + 1)
                            v.tensor_tensor(DB[:, i % 2], A, spread(mx[:, w, i], 2, L), ALU.subtract).then_inc(
                                a_taken, 1)
                        if i >= 1:
                            t = g * G + i - 1
                            p = (i - 1) % 2
                            dve.wait_ge(heads.scored, t + 1)
                            dve.wait_ge(d_done, t + 1)
                            if later(g, 1) or i > 2:
                                dve.wait_ge(heads.turned, 2 * t - 2)
                            v.scalar_tensor_tensor(heads.PB[:, p],
                                                   heads.psS[:].rearrange("p c (h t) -> p (c h) t", t=L),
                                                   float(DH) ** -0.5, DB[:, p], ALU.mult, ALU.mult).then_inc(
                                                       heads.weighted, 1)

                def tail(g, w):
                    step = Steps(dve, t_steps, TPER, g)
                    O = OG[:, w, :, :, 0:DH]
                    dve.wait_ge(heads.o_taken, g * G + G)
                    step(v.tensor_tensor(tw[:, 0], mx[:, w], cum[:, w], ALU.add))
                    step(v.tensor_reduce(tw[:, 1], O, AX.X, ALU.add))
                    step(v.tensor_scalar(tw[:, 2], tw[:, 1], 1.0 / DH, None, ALU.mult))
                    dve.wait_ge(x_done, g)
                    step(v.tensor_tensor(cen[:], O, spread(tw[:, 2], 3, DH), ALU.subtract))
                    dve.wait_ge(e_done, g + 1)
                    S = OG[:, w, :, :, DH]
                    step(v.scalar_tensor_tensor(tw[:, 4], S, -1.0, S, ALU.mult, ALU.max))
                    step(v.tensor_tensor(tw[:, 5], tw[:, 4], tw[:, 3], ALU.max))
                    step(v.tensor_scalar(tw[:, 6], tw[:, 5], 1e-6, None, ALU.add))
                    step(v.reciprocal(tw[:, 7], tw[:, 6]))
                    step(v.tensor_tensor(tw[:, 10], tw[:, 7], tw[:, 7], ALU.mult))
                    dve.wait_ge(sq_done, g + 1)
                    step(v.tensor_reduce(tw[:, 11], sq[:], AX.X, ALU.add))
                    step(v.tensor_tensor(tw[:, 12], tw[:, 10], tw[:, 11], ALU.mult))
                    step(v.tensor_scalar(tw[:, 1], tw[:, 12], 1.0 / DH, None, ALU.mult))
                    step(v.tensor_scalar(tw[:, 8], tw[:, 1], 1e-6, None, ALU.add))
                    dve.wait_ge(r_done, g + 1)
                    step(v.tensor_tensor(tw[:, 10], tw[:, 9], tw[:, 7], ALU.mult))
                    step(v.tensor_tensor(cen[:], cen[:], spread(tw[:, 10], 3, DH), ALU.mult))
                    step.end()

                pipeline3(dve, front_a, front_b, back, tail)

            @block.tensor
            def _(pe):
                pe.wait_ge(heads.set, 4)
                pe.wait_ge(ready, READY)
                pe.wait_ge(w_in, 144)
                pe.wait_ge(wc_steps, 1)

                def front_a(g, w):
                    pe.wait_ge(norm.normed, g * G + G)
                    pe.wait_ge(f_steps, g * FPER)
                    for k in range(KC):
                        pe.wait_ge(taken, g * 2 + k)
                        for j in range(G):
                            mm = nc.tensor.transpose(psG[:, j * P:(j + 1) * P], Z[:, j, k * P:(k + 1) * P], ident[:])
                        mm.then_inc(used, 1)

                def front_b(g, w):
                    pe.wait_ge(taken, g * 2 + 2)
                    pe.wait_ge(cg_in, g * 16 + 16)
                    for j in range(G):
                        tile = slice(j * P, (j + 1) * P)
                        for n, (src, W) in enumerate([(heads.QT[:, w, k, tile], WZ[:, k, :]) for k in range(KC)]
                                                     + [(CG[:, k, tile], WC[:, k, :]) for k in range(KC)]):
                            mm = nc.tensor.matmul(psG[:, j * NG2:(j + 1) * NG2], src, W, start=(n == 0),
                                                  stop=(n == 2 * KC - 1))
                    mm.then_inc(g_used, 1)
                    pe.wait_ge(f_steps, g * FPER + 4)
                    nc.tensor.matmul(psG[:, 0:G * NH], tri[:], fw[:, 4].rearrange("p j h -> p (j h)"), start=True,
                                     stop=True).then_inc(g_used, 1)

                def back(g, w):
                    for i in range(G + 2):
                        if i < G:
                            t = g * G + i
                            pe.wait_ge(da_done, t + 1)
                            pe.wait_ge(a_taken, t)
                            for half in range(2):
                                nc.tensor.matmul(psA[:, half, :], same[:],
                                                 DA[:, i % 2, half * HC:(half + 1) * HC, :].rearrange(
                                                     "p h t -> p (h t)"), start=True, stop=False)
                                mm = nc.tensor.matmul(psA[:, half, :], identb[:],
                                                      mask[:].rearrange("p h t -> p (h t)"), start=False, stop=True)
                            mm.then_inc(a_spread, 1)
                        if 1 <= i <= G:
                            heads.scores(pe, g, w, i - 1)
                        if i >= 2:
                            if i == 2:
                                pe.wait_ge(v_copied, g * 2 + 2)
                            heads.turn(pe, g, i - 2)
                            heads.values(pe, g, w, i - 2)

                pipeline3(pe, front_a, front_b, back, lambda g, w: None)

            @block.scalar
            def _(act):
                sc = nc.scalar
                act.wait_ge(ready, READY)
                act.wait_ge(heads.set, 4)

                def front_a(g, w):
                    if later(g, 2):
                        act.wait_ge(heads.scored, g * G - G)
                    for k in range(KC):
                        act.wait_ge(used, g * 2 + k + 1)
                        sc.copy(heads.QT[:, w, k, :], psG[:]).then_inc(taken, 1)
                    act.wait_ge(v_in, g * 32 + 32)
                    if later(g, 2):
                        act.wait_ge(heads.valued, g * G - G)
                    for hp in range(2):
                        rows = slice(hp * L, (hp + 1) * L)
                        sc.copy(heads.VB[rows, w, :, :, hp, 0:DH],
                                V2[rows].rearrange("p b (i h d) -> p b i h d", h=2, d=DH)[:, :, :, hp, :]).then_inc(
                                    v_copied, 1)

                def front_b(g, w):
                    act.wait_ge(f_steps, g * FPER + 2)
                    sc.activation(fw[:, 1], fw[:, 0], ACT.Exp).then_inc(f_exp, 1)
                    act.wait_ge(f_exp, g + 1)
                    sc.activation(fw[:, 2], fw[:, 1], ACT.Ln, bias=one[:, 0:1]).then_inc(f_ln, 1)

                def back(g, w):
                    for i in range(G + 2):
                        if i < G:
                            act.wait_ge(a_taken, g * G + i + 1)
                            sc.activation(DB[:, i % 2], DB[:, i % 2], ACT.Exp).then_inc(d_done, 1)
                        if i >= 2:
                            heads.copy_turned(act, g, i - 2)
                            act.wait_ge(heads.valued, g * G + i - 1)
                            sc.copy(OG[:, w, i - 2], heads.out()).then_inc(heads.o_taken, 1)

                def tail(g, w):
                    act.wait_ge(t_steps, g * TPER + 1)
                    sc.activation(tw[:, 3], tw[:, 0], ACT.Exp, scale=-1.0).then_inc(e_done, 1)
                    act.wait_ge(t_steps, g * TPER + 4)
                    sc.activation(sq[:], cen[:], ACT.Square).then_inc(sq_done, 1)

                pipeline3(act, front_a, front_b, back, tail)

def ternary(nc, name, identb, matrices):
    NB = 8
    with ExitStack() as ctx:
        s = Scope(nc, ctx, name)
        M = len(matrices)
        W = s.sb("W", [P, M, FF * D // P])
        R = s.sb("R", [P, M, FF * D // P], BF16)
        ones = s.sb("ones", [P, P])
        rowsum = s.sb("rowsum", [P, M])
        inv = s.sb("inv", [P, M])
        psum = s.ps("psum", [P, M])
        psT = s.ps("psT", [P, 2, NB, P], BF16)
        w_in, set_, steps, summed, totalled, ternary_done, turned, taken = (
            s.sem(x) for x in ("w_in", "set", "steps", "summed", "totalled", "ternary", "turned", "taken"))
        with nc.Block() as block:

            @block.sync
            def _(sp):
                for m, (dram, WT, scale) in enumerate(matrices):
                    I = dram.shape[1]
                    sp.dma_start(W[:, m].rearrange("p (c i) -> p c i", i=I),
                                 dram.rearrange("(c p) i -> p c i", p=P)).then_inc(w_in, 16)
                    sp.wait_ge(w_in, 16 * m + 16)

            @block.gpsimd
            def _(pool):
                nc.gpsimd.memset(ones[:], 1.0).then_inc(set_, 1)

            @block.vector
            def _(dve):
                step = Steps(dve, steps, 4 * M)
                for m, (dram, WT, scale) in enumerate(matrices):
                    dve.wait_ge(w_in, 16 * m + 16)
                    nc.vector.tensor_reduce(rowsum[:, m:m + 1], W[:, m], AX.X, ALU.add,
                                            apply_absolute_value=True).then_inc(summed, 1)
                for m, (dram, WT, scale) in enumerate(matrices):
                    dve.wait_ge(totalled, m + 1)
                    if m == 0:
                        dve.wait_ge(totalled, M)
                    step(nc.vector.tensor_scalar(scale[:, 0:1], psum[:, m:m + 1], 1.0 / (FF * D), 1e-5, ALU.mult,
                                                 ALU.max))
                    step(nc.vector.reciprocal(inv[:, m:m + 1], scale[:, 0:1]))
                    step(nc.vector.tensor_scalar(W[:, m], W[:, m], inv[:, m:m + 1], MAGIC, ALU.mult, ALU.add))
                    step(nc.vector.tensor_scalar(W[:, m], W[:, m], MAGIC, 1.0, ALU.subtract, ALU.min))
                    nc.vector.tensor_scalar(R[:, m], W[:, m], -1.0, None, ALU.max).then_inc(ternary_done, 1)
                step.end()

            @block.tensor
            def _(pe):
                pe.wait_ge(set_, 1)
                for m in range(M):
                    pe.wait_ge(summed, m + 1)
                    nc.tensor.matmul(psum[:, m:m + 1], ones[:], rowsum[:, m:m + 1], start=True,
                                     stop=True).then_inc(totalled, 1)
                for m, (dram, WT, scale) in enumerate(matrices):
                    O, I = dram.shape
                    pe.wait_ge(ternary_done, m + 1)
                    blocks = [(k, c) for k in range(I // P) for c in range(O // P)]
                    for half in range(2):
                        if m > 0:
                            pe.wait_ge(taken, 2 * m - 1 + half)
                        for n, (k, c) in enumerate(blocks[half * NB:half * NB + NB]):
                            mm = nc.tensor.transpose(psT[:, half, n, :], R[:, m, c * I + k * P:c * I + (k + 1) * P],
                                                     identb[:])
                        mm.then_inc(turned, 1)

            @block.scalar
            def _(act):
                for m, (dram, WT, scale) in enumerate(matrices):
                    flat = WT[:].rearrange("p k o -> p (k o)")
                    for half in range(2):
                        act.wait_ge(turned, 2 * m + half + 1)
                        nc.scalar.copy(flat[:, half * NB * P:(half + 1) * NB * P],
                                       psT[:, half].rearrange("p n q -> p (n q)")).then_inc(taken, 1)

class Rounded:

    def __init__(self, nc, s, X, ident, rms_eps, floor):
        self.nc, self.ident, self.rms_eps, self.floor = nc, ident, rms_eps, floor
        self.norm = Norm(nc, s, X)
        self.Z = s.sb("Z", [P, G, D])
        self.ZM = s.sb("ZM", [P, G, D])
        self.QT = s.sb("QT", [P, 2, KC, G * P], BF16)
        self.amax = s.sb("amax", [P, G])
        self.am = s.sb("am", [P, G])
        self.unit = s.sb("unit", [P, 2, G])
        self.inv = s.sb("inv", [P, G])
        self.qs = s.sb("qs", [P, G])
        self.u = s.sb("u", [P, 3, G])
        self.r = s.sb("r", [P, G])
        self.rms_e = s.sb("rms_e", [P, G])
        self.neg = s.sb("neg", [P, 1])
        self.psT = s.ps("psT", [P, KC, G * P])
        self.steps, self.rounded, self.turned, self.qt_done = (
            s.sem(x) for x in ("q_steps", "rounded", "q_turned", "qt_done"))
        self.set, self.rms_steps, self.r_done = s.sem("q_set"), s.sem("rms_steps"), s.sem("r_done")
        self.PER = 5 if rms_eps else 3

    def constants(self, pool):
        self.nc.gpsimd.memset(self.neg[:], -MAGIC).then_inc(self.set, 1)
        self.nc.gpsimd.memset(self.rms_e[:], self.rms_eps or 0.0).then_inc(self.set, 1)
        pool.wait_ge(self.set, 2)
        self.norm.constants(pool)

    def on_pool(self, pool, g):
        self.norm.on_pool(pool, g)
        if self.rms_eps:
            gp, n = self.nc.gpsimd, self.norm
            step = Steps(pool, self.rms_steps, 3, g)
            pool.wait_ge(n.rstd_done, g + 1)
            step(gp.tensor_tensor(self.u[:, 0], n.mv[:, :, 1], n.rstd[:], ALU.mult))
            step(gp.tensor_tensor(self.u[:, 1], self.u[:, 0], n.rstd[:], ALU.mult))
            step(gp.tensor_tensor(self.u[:, 2], self.u[:, 1], self.rms_e[:], ALU.add))
            gp.tensor_tensor(self.r[:], self.u[:, 2], n.mhalf[:], ALU.pow).then_inc(self.r_done, 1)
            step.end()

    def on_vector(self, dve, g, w):
        v, Z = self.nc.vector, self.Z
        self.norm.on_vector(dve, g, Z)
        step = Steps(dve, self.steps, self.PER, g)
        dve.wait_ge(self.norm.normed, g * G + G)
        step(v.tensor_reduce(self.amax[:], Z[:], AX.X, ALU.max, apply_absolute_value=True))
        am, qs = self.amax, self.inv
        if self.rms_eps:
            dve.wait_ge(self.r_done, g + 1)
            step(v.tensor_tensor(self.am[:], self.amax[:], self.r[:], ALU.mult))
            am, qs = self.am, self.qs
        step(v.tensor_scalar(self.unit[:, w], am[:], self.floor, 1.0 / 127.0, ALU.max, ALU.mult))
        step(v.reciprocal(self.inv[:], self.unit[:, w]))
        if self.rms_eps:
            step(v.tensor_tensor(self.qs[:], self.inv[:], self.r[:], ALU.mult))
        step.end()
        dve.wait_ge(self.turned, g * KC)
        for j in range(G):
            v.tensor_scalar(self.ZM[:, j, :], Z[:, j, :], qs[:, j:j + 1], MAGIC, ALU.mult,
                            ALU.add).then_inc(self.rounded, 1)

    def on_tensor(self, pe, g):
        pe.wait_ge(self.rounded, g * G + G)
        pe.wait_ge(self.qt_done, g * KC)
        for k in range(KC):
            for j in range(G):
                mm = self.nc.tensor.transpose(self.psT[:, k, j * P:(j + 1) * P], self.ZM[:, j, k * P:(k + 1) * P],
                                              self.ident[:])
            mm.then_inc(self.turned, 1)

    def on_scalar(self, act, g, w):
        for k in range(KC):
            act.wait_ge(self.turned, g * KC + k + 1)
            self.nc.scalar.activation(self.QT[:, w, k, :], self.psT[:, k, :], ACT.Identity,
                                      bias=self.neg[:, 0:1]).then_inc(self.qt_done, 1)

class Down:

    def __init__(self, nc, s, X, identb, W2, w2_unit, eps, bias):
        self.nc, self.X, self.identb, self.W2, self.w2_unit, self.eps, self.bias = (
            nc, X, identb, W2, w2_unit, eps, bias)
        self.square = s.sb("square", [P, 2, FF], BF16)
        self.ms = s.sb("ms", [P, G])
        self.me = s.sb("me", [P, G])
        self.r = s.sb("d_r", [P, G])
        self.mhalf = s.sb("d_mhalf", [P, G])
        self.amax = s.sb("d_amax", [P, G])
        self.am = s.sb("d_am", [P, G])
        self.unit = s.sb("d_unit", [P, G])
        self.inv = s.sb("d_inv", [P, G])
        self.qs = s.sb("d_qs", [P, G])
        self.uw = s.sb("d_uw", [P, G])
        self.magic = s.sb("magic", [P, 1])
        self.HM = s.sb("HM", [P, 2, FF])
        self.HB = s.sb("HB", [P, 2, FF], BF16)
        self.HT = s.sb("HT", [P, 2, FF // P, P], BF16)
        self.psV = s.ps("psV", [P, FF // P, P], BF16)
        self.psO = s.ps("psO", [P, D])
        self.set = s.sem("d_set")
        (self.squared, self.steps, self.r_done, self.scaled, self.hm_done, self.hb_done, self.turned, self.ht_done,
         self.out, self.x_done, self.tmp_done) = (s.sem(x) for x in (
             "squared", "d_steps", "d_r_done", "d_scaled", "hm_done", "hb_done", "d_turned", "ht_done", "out",
             "x_done", "tmp_done"))

    def constants(self, pool):
        self.nc.gpsimd.memset(self.magic[:], MAGIC).then_inc(self.set, 1)
        self.nc.gpsimd.memset(self.mhalf[:], -0.5).then_inc(self.set, 1)
        pool.wait_ge(self.set, 2)

    def on_pool(self, pool, g):
        pool.wait_ge(self.steps, g * 7 + 2)
        self.nc.gpsimd.tensor_tensor(self.r[:], self.me[:], self.mhalf[:], ALU.pow).then_inc(self.r_done, 1)

    def scalar_square(self, act, g, j, Hj):
        if j == 0:
            act.wait_ge(self.steps, g * 7)
        if later(g, 1) or j > 1:
            act.wait_ge(self.squared, g * G + j - 1)
        self.nc.scalar.activation(self.square[:, j % 2], Hj, ACT.Square, accum_out=self.ms[:, j:j + 1]).then_inc(
            self.squared, 1)

    def on_vector(self, dve, g, H):
        v = self.nc.vector
        step = Steps(dve, self.steps, 7, g)
        step(v.tensor_reduce(self.amax[:], H, AX.X, ALU.max, apply_absolute_value=True))
        dve.wait_ge(self.squared, g * G + G)
        step(v.tensor_scalar(self.me[:], self.ms[:], 1.0 / FF, self.eps, ALU.mult, ALU.add))
        dve.wait_ge(self.r_done, g + 1)
        step(v.tensor_tensor(self.am[:], self.amax[:], self.r[:], ALU.mult))
        step(v.tensor_scalar(self.unit[:], self.am[:], 1e-5, 1.0 / 127.0, ALU.max, ALU.mult))
        step(v.reciprocal(self.inv[:], self.unit[:]))
        dve.wait_ge(self.hm_done, g * G)
        step(v.tensor_tensor(self.qs[:], self.inv[:], self.r[:], ALU.mult))
        step(v.tensor_scalar(self.uw[:], self.unit[:], self.w2_unit[:, 0:1], None, ALU.mult))
        step.end()
        for j in range(G + 1):
            if j < G:
                dve.wait_ge(self.hm_done, g * G + j + 1)
                if later(g, 1) or j > 1:
                    dve.wait_ge(self.turned, g * G + j - 1)
                v.tensor_scalar(self.HB[:, j % 2], self.HM[:, j % 2], MAGIC, None, ALU.subtract).then_inc(
                    self.hb_done, 1)
            if j > 0:
                t = g * G + j - 1
                x = self.X[:, t, :]
                dve.wait_ge(self.out, t + 1)
                v.scalar_tensor_tensor(x, self.psO[:], self.uw[:, j - 1:j], x, ALU.mult, ALU.add).then_inc(
                    self.x_done, 1)
        if self.bias is not None:
            dve.wait_ge(self.x_done, g * G + G)
            xs = self.X[:, bass.ds(g * G, G), :]
            v.tensor_tensor(xs, xs, spread(self.bias[:], 1, G), ALU.add).then_inc(self.tmp_done, 1)

    def round_on_scalar(self, act, g, H):
        act.wait_ge(self.steps, g * 7 + 7)
        for j in range(G + 1):
            if j < G:
                if later(g, 1) or j > 1:
                    act.wait_ge(self.hb_done, g * G + j - 1)
                self.nc.scalar.activation(self.HM[:, j % 2], H[:, j], ACT.Identity, bias=self.magic[:, 0:1],
                                          scale=self.qs[:, j:j + 1]).then_inc(self.hm_done, 1)
            if j > 0:
                t = g * G + j - 1
                act.wait_ge(self.turned, t + 1)
                if later(g, 1) or j > 2:
                    act.wait_ge(self.out, t - 1)
                self.nc.scalar.copy(self.HT[:, (j - 1) % 2], self.psV[:]).then_inc(self.ht_done, 1)

    def on_tensor(self, pe, g):
        for j in range(G):
            t = g * G + j
            pe.wait_ge(self.hb_done, t + 1)
            pe.wait_ge(self.ht_done, t)
            for c in range(FF // P):
                mm = self.nc.tensor.transpose(self.psV[:, c, :], self.HB[:, j % 2, c * P:(c + 1) * P], self.identb[:])
            mm.then_inc(self.turned, 1)
            pe.wait_ge(self.ht_done, t + 1)
            pe.wait_ge(self.x_done, t)
            for c in range(FF // P):
                mm = self.nc.tensor.matmul(self.psO[:], self.HT[:, j % 2, c, :], self.W2[:, c, :], start=(c == 0),
                                           stop=(c == FF // P - 1))
            mm.then_inc(self.out, 1)

HALF = FF // 2

def normed_ffn(nc, io, X, ident, identb):
    with ExitStack() as ctx:
        s = Scope(nc, ctx, "nffn")
        W1 = s.sb("W1", [P, KC, FF], BF16)
        W2 = s.sb("W2", [P, FF // P, D], BF16)
        u1, u2 = s.sb("u1", [P, 1]), s.sb("u2", [P, 1])
        ternary(nc, "nffn_weights", identb, [(io["L1_ffn_w1"], W1, u1), (io["L1_ffn_w2"], W2, u2)])
        b1, gam, bet, b2 = s.sb("b1", [P, FF]), s.sb("gam", [P, FF]), s.sb("bet", [P, FF]), s.sb("b2", [P, D])
        H = s.sb("H", [P, 2, G, FF])
        q = Rounded(nc, s, X, ident, 1e-5, 1e-5)
        down = Down(nc, s, X, identb, W2, u2, 1e-5, b2)
        uw = s.sb("uw", [P, G])
        stats = s.sb("stats2", [P, G, 2, 6])
        mv = s.sb("mv2", [P, G, 2])
        rstd = s.sb("rstd2", [P, G])
        veps = s.sb("veps2", [P, G])
        psH = s.ps("psH", [P, 2, HALF])
        (b_in, uw_done, up, affined, silued, gelued, agg, veps_done, rstd_done, normed, gained, shifted) = (
            s.sem(x) for x in ("b_in", "uw_done", "up", "affined", "silued", "gelued", "agg2", "veps2_done",
                               "rstd2_done", "normed2", "gained", "shifted"))

        with nc.Block() as block:

            @block.sync
            def _(sp):
                for tile, name in ((b1, "b1"), (gam, "ln_g"), (bet, "ln_b"), (b2, "b2")):
                    sp.dma_start(tile[:], spread(io["L1_ffn_" + name], 0, P)).then_inc(b_in, 16)
                sp.wait_ge(b_in, 64)

            @block.gpsimd
            def _(pool):
                q.constants(pool)
                down.constants(pool)
                pool.wait_ge(b_in, 64)

                def back(g, w):
                    pool.wait_ge(agg, g * G + G)
                    nc.gpsimd.tensor_tensor(veps[:], mv[:, :, 1], q.norm.eps[:], ALU.add).then_inc(veps_done, 1)
                    pool.wait_ge(veps_done, g + 1)
                    nc.gpsimd.tensor_tensor(rstd[:], veps[:], q.norm.mhalf[:], ALU.pow).then_inc(rstd_done, 1)
                    for j in range(G):
                        pool.wait_ge(normed, g * G + j + 1)
                        nc.gpsimd.tensor_tensor(H[:, w, j], H[:, w, j], gam[:], ALU.mult).then_inc(gained, 1)
                        pool.wait_ge(gained, g * G + j + 1)
                        nc.gpsimd.tensor_tensor(H[:, w, j], H[:, w, j], bet[:], ALU.add).then_inc(shifted, 1)
                    down.on_pool(pool, g)

                pipeline(pool, lambda g, w: q.on_pool(pool, g), back)

            @block.vector
            def _(dve):
                dve.wait_ge(b_in, 64)

                def front(g, w):
                    q.on_vector(dve, g, w)
                    nc.vector.tensor_scalar(uw[:], q.unit[:, w], u1[:, 0:1], None, ALU.mult).then_inc(uw_done, 1)
                    dve.wait_ge(uw_done, g + 1)
                    for j in range(G):
                        for h in range(2):
                            half = slice(h * HALF, (h + 1) * HALF)
                            dve.wait_ge(up, (g * G + j) * 2 + h + 1)
                            nc.vector.scalar_tensor_tensor(H[:, w, j, half], psH[:, h, :], uw[:, j:j + 1], b1[:, half],
                                                           ALU.mult, ALU.add).then_inc(affined, 1)

                def back(g, w):
                    dve.wait_ge(gelued, g + 1)
                    for j in range(G):
                        for h in range(2):
                            nc.vector.bn_stats(stats[:, j, h, :], H[:, w, j, h * HALF:(h + 1) * HALF])
                    dve.drain()
                    for j in range(G):
                        nc.vector.bn_aggr(mv[:, j, :], stats[:, j].rearrange("p h s -> p (h s)")).then_inc(agg, 1)
                    dve.wait_ge(rstd_done, g + 1)
                    dve.wait_ge(agg, g * G + G)
                    for j in range(G):
                        nc.vector.tensor_scalar(H[:, w, j], H[:, w, j], mv[:, j, 0:1], rstd[:, j:j + 1],
                                                ALU.subtract, ALU.mult).then_inc(normed, 1)
                    dve.wait_ge(shifted, g * G + G)
                    down.on_vector(dve, g, H[:, w])

                pipeline(dve, front, back)

            @block.tensor
            def _(pe):
                def front(g, w):
                    q.on_tensor(pe, g)
                    pe.wait_ge(q.qt_done, g * KC + KC)
                    for j in range(G):
                        for h in range(2):
                            if later(g, 1) or j > 0:
                                pe.wait_ge(affined, (g * G + j) * 2 + h - 1)
                            for k in range(KC):
                                mm = nc.tensor.matmul(psH[:, h, :], q.QT[:, w, k, j * P:(j + 1) * P],
                                                      W1[:, k, h * HALF:(h + 1) * HALF], start=(k == 0),
                                                      stop=(k == KC - 1))
                            mm.then_inc(up, 1)

                pipeline(pe, front, lambda g, w: down.on_tensor(pe, g))

            @block.scalar
            def _(act):
                def front(g, w):
                    q.on_scalar(act, g, w)
                    for j in range(G):
                        act.wait_ge(affined, (g * G + j) * 2 + 2)
                        nc.scalar.activation(H[:, w, j], H[:, w, j], ACT.Silu).then_inc(silued, 1)
                    act.wait_ge(silued, g * G + G)
                    nc.scalar.activation(H[:, w], H[:, w], ACT.Gelu).then_inc(gelued, 1)

                def back(g, w):
                    for j in range(G):
                        act.wait_ge(shifted, g * G + j + 1)
                        down.scalar_square(act, g, j, H[:, w, j])
                    down.round_on_scalar(act, g, H[:, w])

                pipeline(act, front, back)

def softmax_attention(nc, io, X, CT, ident):
    USES = 2 * KC + 2 + BG
    with ExitStack() as ctx:
        s = Scope(nc, ctx, "satt")
        WQ, WK, WV, WO = (s.sb(x, [P, KC, D]) for x in ("WQ", "WK", "WV", "WO"))
        turn_weights(nc, "satt_wqk", ident, [(io["L2_xattn_Wq"], WQ), (io["L2_xattn_Wk"], WK)])
        turn_weights(nc, "satt_wvo", ident, [(io["L2_xattn_Wv"], WV), (io["L2_xattn_Wo"], WO)])
        norm = Norm(nc, s, X)
        heads = Heads(nc, s, ident)
        bq, bk = s.sb("bq", [P, KC]), s.sb("bk", [P, KC])
        bv, bo = s.sb("bv", [P, D]), s.sb("bo", [P, D])
        Z = s.sb("Z", [P, G, D])
        ZT = s.sb("ZT", [P, KC, G * P])
        KT = s.sb("KT", [P, KC, G * P])
        CG = s.sb("CG", [P, KC, G * P])
        mx = s.sb("mx", [P, 2, NH])
        rs = s.sb("rs", [P, 2, NH])
        AO = s.sb("AO", [P, 2, NH, DH])
        AT = s.sb("AT", [P, 2, KC, P])
        psG = s.ps("psG", [P, 2, 512])
        psF = s.ps("psF", [P, 512])
        (b_in, c_in, used, taken, v_used, v_taken, maxed, subbed, inverted, ao_done, ao_turned, at_done, projected,
         x_done, bo_added) = (s.sem(x) for x in (
             "b_in", "c_in", "used", "taken", "v_used", "v_taken", "maxed", "subbed", "inverted", "ao_done",
             "ao_turned", "at_done", "projected", "x_done", "bo_added"))

        with nc.Block() as block:

            @block.sync
            def _(sp):
                with nc.allow_non_contiguous_dma(reason="one column of biases for each chunk"):
                    sp.dma_start(bq[:], io["L2_xattn_bq"].rearrange("(k p) -> p k", p=P)).then_inc(b_in, 16)
                    sp.dma_start(bk[:], io["L2_xattn_bk"].rearrange("(k p) -> p k", p=P)).then_inc(b_in, 16)
                sp.dma_start(bv[:], spread(io["L2_xattn_bv"], 0, P)).then_inc(b_in, 16)
                sp.dma_start(bo[:], spread(io["L2_xattn_bo"], 0, P)).then_inc(b_in, 16)
                sp.wait_ge(b_in, 64)
                sp.wait_ge(heads.set, 4)

                def front(g, w):
                    at, vs, ks = (held(sp, v) for v in (g * (G * P), g * BG, g * 6 + 6))
                    free = heads.free_after(sp, g)
                    sp.wait_ge(v_used, vs)
                    sp.dma_start(CG[:], CT[:, :, bass.ds(at, G * P)]).then_inc(c_in, 16)
                    sp.wait_ge(taken, ks)
                    heads.expand(sp, g, lambda rows, c, half: KT[rows, c, half * HG:(half + 1) * HG], free)

                pipeline(sp, front, lambda g, w: None)

            @block.gpsimd
            def _(pool):
                heads.constants(pool)
                norm.constants(pool)
                pool.wait_ge(b_in, 64)

                def back(g, w):
                    pool.wait_ge(x_done, g * G + G)
                    xs = X[:, bass.ds(g * G, G), :]
                    nc.gpsimd.tensor_tensor(xs, xs, spread(bo[:], 1, G), ALU.add).then_inc(bo_added, 1)

                pipeline(pool, lambda g, w: norm.on_pool(pool, g), back)

            @block.vector
            def _(dve):
                v = nc.vector
                dve.wait_ge(heads.set, 4)
                dve.wait_ge(b_in, 64)

                def front(g, w):
                    dve.wait_ge(used, g * 6)
                    norm.on_vector(dve, g, Z)
                    for b in range(BG):
                        dve.wait_ge(v_used, g * BG + b + 1)
                        if b == 0 and later(g, 2):
                            dve.wait_ge(heads.valued, g * G - G)
                        for hp in range(2):
                            rows = slice(hp * L, (hp + 1) * L)
                            take = lambda x: x.rearrange("p (i h d) -> p i h d", h=2, d=DH)[:, :, hp, :]
                            v.tensor_tensor(heads.VB[rows, w, b, :, hp, 0:DH], take(psG[rows, b % 2, 0:D]),
                                            take(bv[rows, :]), ALU.add).then_inc(v_taken, 1)

                def back(g, w):
                    for i in range(G + 2):
                        if i < G:
                            t = g * G + i
                            p = i % 2
                            S = heads.psS[:].rearrange("p c (h t) -> p (c h) t", t=L)
                            dve.wait_ge(heads.scored, t + 1)
                            v.tensor_reduce(mx[:, p], S, AX.X, ALU.max).then_inc(maxed, 1)
                            if later(g, 1) or i > 1:
                                dve.wait_ge(heads.turned, 2 * t - 2)
                            dve.wait_ge(maxed, t + 1)
                            v.tensor_tensor(heads.PB[:, p], S, spread(mx[:, p], 2, L), ALU.subtract).then_inc(
                                heads.s_taken, 1)
                        if 1 <= i <= G:
                            t = g * G + i - 1
                            p = (i - 1) % 2
                            dve.wait_ge(heads.valued, t + 1)
                            v.reciprocal(rs[:, p], heads.out()[:, :, DH]).then_inc(inverted, 1)
                            dve.wait_ge(inverted, t + 1)
                            if later(g, 1) or i > 2:
                                dve.wait_ge(ao_turned, t - 1)
                            v.tensor_tensor(AO[:, p], heads.out()[:, :, 0:DH], spread(rs[:, p], 2, DH),
                                            ALU.mult).then_inc(heads.o_taken, 1)
                        if i >= 2:
                            t = g * G + i - 2
                            dve.wait_ge(projected, t + 1)
                            v.tensor_tensor(X[:, t, :], psF[:, 0:D], X[:, t, :], ALU.add).then_inc(x_done, 1)

                pipeline(dve, front, back)

            @block.tensor
            def _(pe):
                pe.wait_ge(heads.set, 4)

                def front(g, w):
                    pe.wait_ge(norm.normed, g * G + G)
                    for k in range(KC):
                        pe.wait_ge(v_taken, g * 2 * BG)
                        for j in range(G):
                            mm = nc.tensor.transpose(psG[:, k, j * P:(j + 1) * P], Z[:, j, k * P:(k + 1) * P], ident[:])
                        mm.then_inc(used, 1)
                    pe.wait_ge(c_in, g * 16 + 16)
                    for m, (W, src) in enumerate(((WQ, ZT), (WK, CG))):
                        for e in range(KC):
                            pe.wait_ge(taken, g * 6 + 2 * m + (2 if m == 0 else e + 1))
                            for k in range(KC):
                                mm = nc.tensor.matmul(psG[:, e, :], W[:, k, e * P:(e + 1) * P], src[:, k, :],
                                                      start=(k == 0), stop=(k == KC - 1))
                            mm.then_inc(used, 1)
                    for b in range(BG):
                        if b < 2:
                            pe.wait_ge(taken, g * 6 + 5 + b)
                        else:
                            pe.wait_ge(v_taken, g * 2 * BG + 2 * (b - 1))
                        for k in range(KC):
                            for hp in range(2):
                                mm = nc.tensor.matmul(psG[hp * L:(hp + 1) * L, b % 2, 0:D],
                                                      CG[:, k, b * L:(b + 1) * L], WV[:, k, :], start=(k == 0),
                                                      stop=(k == KC - 1), skip_group_check=True)
                        mm.then_inc(v_used, 1)

                def back(g, w):
                    for i in range(G + 2):
                        if i == 0:
                            pe.wait_ge(taken, g * 6 + 4)
                            pe.wait_ge(v_taken, (g + 1) * 2 * BG)
                        if i < G:
                            heads.scores(pe, g, w, i)
                        if 1 <= i <= G:
                            heads.turn(pe, g, i - 1)
                            heads.values(pe, g, w, i - 1)
                        if i >= 2:
                            j = i - 2
                            t = g * G + j
                            pe.wait_ge(heads.o_taken, t + 1)
                            pe.wait_ge(x_done, t)
                            for c in range(KC):
                                mm = nc.tensor.transpose(psF[:, c * P:(c + 1) * P],
                                                         AO[:, j % 2, c * HC:(c + 1) * HC, :].rearrange(
                                                             "p h d -> p (h d)"), ident[:])
                            mm.then_inc(ao_turned, 1)
                            pe.wait_ge(at_done, t + 1)
                            for c in range(KC):
                                mm = nc.tensor.matmul(psF[:, 0:D], AT[:, j % 2, c, :], WO[:, c, :], start=(c == 0),
                                                      stop=(c == KC - 1))
                            mm.then_inc(projected, 1)

                pipeline(pe, front, back)

            @block.scalar
            def _(act):
                act.wait_ge(b_in, 64)
                SCALE = float(DH) ** -0.5

                def front(g, w):
                    for k in range(KC):
                        act.wait_ge(used, g * 6 + k + 1)
                        nc.scalar.copy(ZT[:, k, :], psG[:, k, :]).then_inc(taken, 1)
                    if later(g, 2):
                        act.wait_ge(heads.scored, g * G - G)
                    for e in range(KC):
                        act.wait_ge(used, g * 6 + 3 + e)
                        nc.scalar.activation(heads.QT[:, w, e, :], psG[:, e, :], ACT.Identity,
                                             bias=bq[:, e:e + 1]).then_inc(taken, 1)
                    for e in range(KC):
                        act.wait_ge(used, g * 6 + 5 + e)
                        if e == 0:
                            for half in range(2):
                                act.wait_ge(heads.kx_in[half], g * 256)
                        nc.scalar.activation(KT[:, e, :], psG[:, e, :], ACT.Identity,
                                             bias=bk[:, e:e + 1]).then_inc(taken, 1)

                def back(g, w):
                    for i in range(G + 2):
                        if i < G:
                            t = g * G + i
                            act.wait_ge(heads.s_taken, t + 1)
                            nc.scalar.activation(heads.PB[:, i % 2], heads.PB[:, i % 2], ACT.Exp,
                                                 scale=SCALE).then_inc(heads.weighted, 1)
                        if 1 <= i <= G:
                            heads.copy_turned(act, g, i - 1)
                        if i >= 2:
                            j = i - 2
                            t = g * G + j
                            act.wait_ge(ao_turned, t + 1)
                            if later(g, 1) or j > 1:
                                act.wait_ge(projected, t - 1)
                            nc.scalar.copy(AT[:, j % 2].rearrange("p c t -> p (c t)"), psF[:, 0:D]).then_inc(
                                at_done, 1)

                pipeline(act, front, back)

def gated_ffn(nc, io, X, ident, identb):
    with ExitStack() as ctx:
        s = Scope(nc, ctx, "gffn")
        WG = s.sb("WG", [P, KC, FF], BF16)
        WU = s.sb("WU", [P, KC, FF], BF16)
        W2 = s.sb("W2", [P, FF // P, D], BF16)
        ug, uu, u2 = s.sb("ug", [P, 1]), s.sb("uu", [P, 1]), s.sb("u2", [P, 1])
        ternary(nc, "gffn_weights", identb, [(io["L2_ffn_w_gate"], WG, ug), (io["L2_ffn_w_up"], WU, uu),
                                       (io["L2_ffn_w_down"], W2, u2)])
        H = s.sb("H", [P, 2, G, FF])
        S = s.sb("S", [P, 2, HALF])
        q = Rounded(nc, s, X, ident, 1e-6, 1e-5)
        down = Down(nc, s, X, identb, W2, u2, 1e-6, None)
        uwg, uwu = s.sb("uwg", [P, 2, G]), s.sb("uwu", [P, 2, G])
        psG = s.ps("psG", [P, 2, HALF])
        psU = s.ps("psU", [P, 2, HALF])
        uw_done, up, gated, taken = (s.sem(x) for x in ("uw_done", "up", "gated", "taken"))

        with nc.Block() as block:

            @block.gpsimd
            def _(pool):
                q.constants(pool)
                down.constants(pool)
                pipeline(pool, lambda g, w: q.on_pool(pool, g), lambda g, w: down.on_pool(pool, g))

            @block.vector
            def _(dve):
                def front(g, w):
                    q.on_vector(dve, g, w)
                    nc.vector.tensor_scalar(uwg[:, w], q.unit[:, w], ug[:, 0:1], None, ALU.mult).then_inc(uw_done, 1)
                    nc.vector.tensor_scalar(uwu[:, w], q.unit[:, w], uu[:, 0:1], None, ALU.mult).then_inc(uw_done, 1)
                    dve.wait_ge(uw_done, g * 2 + 2)
                    for j in range(G):
                        for h in range(2):
                            dve.wait_ge(gated, (g * G + j) * 2 + h + 1)
                            nc.vector.scalar_tensor_tensor(H[:, w, j, h * HALF:(h + 1) * HALF], psU[:, h, :],
                                                           uwu[:, w, j:j + 1], S[:, h, :], ALU.mult,
                                                           ALU.mult).then_inc(taken, 1)

                def back(g, w):
                    dve.wait_ge(taken, g * (2 * G) + 2 * G)
                    down.on_vector(dve, g, H[:, w])

                pipeline(dve, front, back)

            @block.tensor
            def _(pe):
                def front(g, w):
                    q.on_tensor(pe, g)
                    pe.wait_ge(q.qt_done, g * KC + KC)
                    for j in range(G):
                        for h in range(2):
                            if later(g, 1) or j > 0:
                                pe.wait_ge(taken, (g * G + j) * 2 + h - 1)
                            for bank, W in ((psG, WG), (psU, WU)):
                                for k in range(KC):
                                    mm = nc.tensor.matmul(bank[:, h, :], q.QT[:, w, k, j * P:(j + 1) * P],
                                                          W[:, k, h * HALF:(h + 1) * HALF], start=(k == 0),
                                                          stop=(k == KC - 1))
                            mm.then_inc(up, 1)

                pipeline(pe, front, lambda g, w: down.on_tensor(pe, g))

            @block.scalar
            def _(act):
                def front(g, w):
                    q.on_scalar(act, g, w)
                    act.wait_ge(uw_done, g * 2 + 2)
                    for j in range(G):
                        for h in range(2):
                            act.wait_ge(up, (g * G + j) * 2 + h + 1)
                            if later(g, 1) or j > 0:
                                act.wait_ge(taken, (g * G + j) * 2 + h - 1)
                            nc.scalar.activation(S[:, h, :], psG[:, h, :], ACT.Silu,
                                                 scale=uwg[:, w, j:j + 1]).then_inc(gated, 1)

                def back(g, w):
                    for j in range(G):
                        act.wait_ge(taken, (g * G + j) * 2 + 2)
                        down.scalar_square(act, g, j, H[:, w, j])
                    down.round_on_scalar(act, g, H[:, w])

                pipeline(act, front, back)

def quantized_ffn(nc, io, X, ident, out):
    with ExitStack() as ctx:
        s = Scope(nc, ctx, "qffn")
        K = s.sb("K", [P, KC, D])
        KT = s.sb("KT", [P, KC, D])
        W = s.sb("W", [P, KC, D], BF16)
        cols = s.sb("cols", [P, KC, 4])
        unit_w = s.sb("unit_w", [P, D])
        bias = s.sb("bias", [P, D])
        bq = s.sb("bq", [P, D])
        bs = s.sb("bs", [P, 4])
        diag = s.sb("diag", [P, KC, P])
        ones = s.sb("ones", [P, P])
        Y = s.sb("Y", [P, 2, G, D])
        YR = s.sb("YR", [P, G, D])
        q = Rounded(nc, s, X, ident, None, 1e-35)
        ymax, yunit, yinv = s.sb("ymax", [P, G]), s.sb("yunit", [P, G]), s.sb("yinv", [P, G])
        psK = s.ps("psK", [P, KC, D])
        psW = s.ps("psW", [P, D])
        psU = s.ps("psU", [P, D])
        psY = s.ps("psY", [P, 2, 512])
        (w_in, set_, k_steps, turned, back_turned, spread_out, up, scaled, y_steps,
         x_done, stored) = (s.sem(x) for x in ("w_in", "set", "k_steps", "turned", "back_turned", "spread_out",
                                               "up", "scaled", "y_steps", "x_done",
                                               "stored"))
        SETUP = 20

        with nc.Block() as block:

            @block.sync
            def _(sp):
                sp.dma_start(K[:], io["L3_ffn_kernel"].rearrange("(k p) f -> p k f", p=P)).then_inc(w_in, 16)
                sp.dma_start(bias[:], spread(io["L3_ffn_bias"], 0, P)).then_inc(w_in, 16)
                sp.wait_ge(w_in, 32)
                o = out.rearrange("(t u) l d -> (u l) t d", u=2)
                with sp.Fori(0, NG) as g:
                    sp.wait_ge(x_done, g + 1)
                    sp.dma_start(o[:, bass.ds(g * G, G), :], X[:, bass.ds(g * G, G), :]).then_inc(stored, 16)
                sp.wait_ge(stored, 16 * NG)

            @block.gpsimd
            def _(pool):
                nc.gpsimd.memset(ones[:], 1.0).then_inc(set_, 1)
                q.constants(pool)
                pipeline(pool, lambda g, w: q.on_pool(pool, g), lambda g, w: None)

            @block.vector
            def _(dve):
                v = nc.vector
                step = Steps(dve, k_steps, SETUP)
                dve.wait_ge(w_in, 32)
                dve.wait_ge(turned, 2)
                for k in range(KC):
                    step(v.tensor_reduce(cols[:, k, 0:1], psK[:, k, :], AX.X, ALU.max, apply_absolute_value=True))
                    step(v.tensor_scalar(cols[:, k, 1:2], cols[:, k, 0:1], 1e-35, 1.0 / 127.0, ALU.max, ALU.mult))
                    step(v.reciprocal(cols[:, k, 2:3], cols[:, k, 1:2]))
                    step(v.tensor_scalar(KT[:, k, :], psK[:, k, :], cols[:, k, 2:3], MAGIC, ALU.mult, ALU.add))
                    step(v.tensor_scalar(KT[:, k, :], KT[:, k, :], MAGIC, None, ALU.subtract))
                    step(v.tensor_scalar(diag[:, k, :], ident[:], cols[:, k, 1:2], None, ALU.mult))
                step(v.tensor_reduce(bs[:, 0:1], bias[:], AX.X, ALU.max, apply_absolute_value=True))
                step(v.tensor_scalar(bs[:, 1:2], bs[:, 0:1], 1e-35, 1.0 / 127.0, ALU.max, ALU.mult))
                step(v.reciprocal(bs[:, 2:3], bs[:, 1:2]))
                step(v.tensor_scalar(bq[:], bias[:], bs[:, 2:3], MAGIC, ALU.mult, ALU.add))
                step(v.tensor_scalar(bq[:], bq[:], MAGIC, bs[:, 1:2], ALU.subtract, ALU.mult))
                dve.wait_ge(spread_out, 1)
                step(v.tensor_copy(unit_w[:], psU[:]))
                dve.wait_ge(back_turned, 1)
                step(v.tensor_copy(W[:, 0, :], psW[:]))
                dve.wait_ge(back_turned, 2)
                step(v.tensor_copy(W[:, 1, :], psW[:]))
                step.end()

                def back(g, w):
                    for j in range(G):
                        t = g * G + j
                        dve.wait_ge(up, t + 1)
                        v.scalar_tensor_tensor(Y[:, w, j], psY[:, j % 2, 0:D], q.unit[:, w, j:j + 1], unit_w[:],
                                               ALU.mult, ALU.mult).then_inc(scaled, 1)
                    dve.wait_ge(scaled, g * G + G)
                    step = Steps(dve, y_steps, 7, g)
                    y = Y[:, w]
                    step(v.tensor_tensor(y, y, spread(bq[:], 1, G), ALU.add))
                    step(v.tensor_scalar(y, y, 0.0, None, ALU.max))
                    step(v.tensor_reduce(ymax[:], y, AX.X, ALU.max))
                    step(v.tensor_scalar(yunit[:], ymax[:], 1e-35, 1.0 / 127.0, ALU.max, ALU.mult))
                    step(v.reciprocal(yinv[:], yunit[:]))
                    step(v.tensor_tensor(YR[:], y, spread(yinv[:], 2, D), ALU.mult))
                    step(v.tensor_scalar(YR[:], YR[:], MAGIC, MAGIC, ALU.add, ALU.subtract))
                    step.end()
                    for j in range(G):
                        x = X[:, g * G + j, :]
                        m = v.scalar_tensor_tensor(x, YR[:, j], yunit[:, j:j + 1], x, ALU.mult, ALU.add)
                    m.then_inc(x_done, 1)

                pipeline(dve, lambda g, w: q.on_vector(dve, g, w), back)

            @block.tensor
            def _(pe):
                pe.wait_ge(w_in, 32)
                for f in range(KC):
                    for k in range(KC):
                        mm = nc.tensor.transpose(psK[:, f, k * P:(k + 1) * P], K[:, k, f * P:(f + 1) * P], ident[:])
                    mm.then_inc(turned, 1)
                pe.wait_ge(k_steps, 12)
                pe.wait_ge(set_, 1)
                for f in range(KC):
                    mm = nc.tensor.matmul(psU[:, f * P:(f + 1) * P], ones[:], diag[:, f, :], start=True, stop=True)
                mm.then_inc(spread_out, 1)
                for k in range(KC):
                    if k == 1:
                        pe.wait_ge(k_steps, SETUP - 1)
                    for f in range(KC):
                        mm = nc.tensor.transpose(psW[:, f * P:(f + 1) * P], KT[:, f, k * P:(k + 1) * P], ident[:])
                    mm.then_inc(back_turned, 1)
                pe.wait_ge(k_steps, SETUP)

                def back(g, w):
                    pe.wait_ge(q.qt_done, g * KC + KC)
                    for j in range(G):
                        t = g * G + j
                        if later(g, 1) or j > 1:
                            pe.wait_ge(scaled, t - 1)
                        for k in range(KC):
                            mm = nc.tensor.matmul(psY[:, j % 2, 0:D], q.QT[:, w, k, j * P:(j + 1) * P], W[:, k, :],
                                                  start=(k == 0), stop=(k == KC - 1))
                        mm.then_inc(up, 1)

                pipeline(pe, lambda g, w: q.on_tensor(pe, g), back)

            @block.scalar
            def _(act):
                def front(g, w):
                    if later(g, 2):
                        act.wait_ge(up, g * G - G)
                    q.on_scalar(act, g, w)

                pipeline(act, front, lambda g, w: None)

def summary_mix(nc, io, X, CT, ident, sums):
    with ExitStack() as ctx:
        s = Scope(nc, ctx, "mix")
        norm = Norm(nc, s, X)
        WI, WO = s.sb("WI", [P, KC, D]), s.sb("WO", [P, KC, D])
        WIT, WOT = s.sb("WIT", [P, KC, D]), s.sb("WOT", [P, KC, D])
        bi = s.sb("bi", [P, KC])
        bo = s.sb("bo", [L, D])
        gam, bet = s.sb("gam", [P, D]), s.sb("bet", [P, D])
        decay, k = s.sb("decay", [P, 1]), s.sb("k", [P, 3])
        ones = s.sb("ones", [P, L])
        powers, weights, wsum = s.sb("powers", [P, L]), s.sb("weights", [P, L]), s.sb("wsum", [P, 1])
        flip, flipped = s.sb("flip", [L, L]), s.sb("flipped", [L, L])
        col, diag, all1 = s.sb("col", [L, 1]), s.sb("diag", [L, L]), s.sb("all1", [L, P])
        weighted = s.sb("weighted", [P, 2, B // 2, L])
        ST = s.sb("ST", [P, KC, B])
        bw = s.sb("bw", [P, KC])
        HT = s.sb("HT", [P, KC, B])
        SUM = s.sb("SUM", [B, D])
        SM = s.sb("SM", [P, T, D])
        Y = s.sb("Y", [P, 2, G, D])
        stats, mv = s.sb("stats2", [P, G, 6]), s.sb("mv2", [P, G, 2])
        veps, rstd = s.sb("veps2", [P, G]), s.sb("rstd2", [P, G])
        psW = s.ps("psW", [P, 2, KC, D])
        psB = s.ps("psB", [P, 512])
        psH = s.ps("psH", [P, KC, 512])
        psS = s.ps("psS", [B, 512])
        (w_in, ready, steps, expd, w_turned, w_copied, wide, hid, summed, sum_out, sum_in, added, stats_done,
         veps_done, rstd_done, normed, gained, y_steps) = (s.sem(x) for x in (
             "w_in", "ready", "steps", "expd", "w_turned", "w_copied", "wide", "hid", "summed", "sum_out", "sum_in",
             "added", "stats2_done", "veps2_done", "rstd2_done", "normed2", "gained", "y_steps"))
        SETUP = 21

        with nc.Block() as block:

            @block.sync
            def _(sp):
                sp.dma_start(decay[:], spread(io["L3_xattn_decay"], 0, P)).then_inc(w_in, 16)
                sp.dma_start(WI[:], io["L3_xattn_W_in"].rearrange("(k p) d -> p k d", p=P)).then_inc(w_in, 16)
                sp.dma_start(WO[:], io["L3_xattn_W_out"].rearrange("(k p) d -> p k d", p=P)).then_inc(w_in, 16)
                with nc.allow_non_contiguous_dma(reason="one column of biases for each chunk"):
                    sp.dma_start(bi[:], io["L3_xattn_b_in"].rearrange("(k p) -> p k", p=P)).then_inc(w_in, 16)
                sp.dma_start(bo[:], spread(io["L3_xattn_b_out"], 0, L)).then_inc(w_in, 16)
                sp.dma_start(gam[:], spread(io["L3_xattn_gamma"], 0, P)).then_inc(w_in, 16)
                sp.dma_start(bet[:], spread(io["L3_xattn_beta"], 0, P)).then_inc(w_in, 16)
                sp.wait_ge(w_in, 112)
                sp.wait_ge(steps, SETUP)
                sp.dma_start(sums, SUM[:]).then_inc(sum_out, 16)
                sp.wait_ge(sum_out, 16)
                for u in range(2):
                    sp.dma_start(SM[u * L:(u + 1) * L],
                                 spread(sums.rearrange("(t u) d -> u t d", u=2)[u], 0, L)).then_inc(sum_in, 16)

            @block.gpsimd
            def _(pool):
                nc.gpsimd.memset(ones[:], 1.0).then_inc(ready, 1)
                nc.gpsimd.memset(all1[:], 1.0).then_inc(ready, 1)
                nc.gpsimd.memset(flip[:], 0.0).then_inc(ready, 1)
                pool.wait_ge(ready, 3)
                nc.gpsimd.affine_select(out=flip[:], in_=flip[:], compare_op=ALU.not_equal, fill=1.0, base=1 - L,
                                        pattern=[[1, L]], channel_multiplier=1).then_inc(ready, 1)
                norm.constants(pool)
                pool.wait_ge(w_in, 112)

                def front(g, w):
                    norm.on_pool(pool, g)
                    pool.wait_ge(norm.normed, g * G + G)
                    if not later(g, 1):
                        pool.wait_ge(sum_in, 32)
                    nc.gpsimd.tensor_tensor(Y[:, w], Y[:, w], SM[:, bass.ds(g * G, G), :], ALU.add).then_inc(added, 1)

                def back(g, w):
                    pool.wait_ge(stats_done, g * G + G)
                    nc.gpsimd.tensor_tensor(veps[:], mv[:, :, 1], norm.eps[:], ALU.add).then_inc(veps_done, 1)
                    pool.wait_ge(veps_done, g + 1)
                    nc.gpsimd.tensor_tensor(rstd[:], veps[:], norm.mhalf[:], ALU.pow).then_inc(rstd_done, 1)
                    pool.wait_ge(normed, g * G + G)
                    nc.gpsimd.tensor_tensor(Y[:, w], Y[:, w], spread(gam[:], 1, G), ALU.mult).then_inc(gained, 1)

                pipeline(pool, front, back)

            @block.vector
            def _(dve):
                v = nc.vector
                step = Steps(dve, steps, SETUP)
                dve.wait_ge(ready, 4)
                dve.wait_ge(expd, 1)
                step(v.tensor_scalar(k[:, 1:2], k[:, 0:1], 1.0, None, ALU.add))
                step(v.reciprocal(k[:, 2:3], k[:, 1:2]))
                step(v.tensor_scalar(weights[:], ones[:], k[:, 2:3], None, ALU.mult))
                step(v.tensor_tensor_scan(powers[:], weights[:], ones[:], 0.0, ALU.mult, ALU.add))
                step(v.tensor_tensor(flipped[:], powers[0:L, :], flip[:], ALU.mult))
                step(v.tensor_reduce(col[:], flipped[:], AX.X, ALU.add))
                step(v.tensor_scalar(diag[:], ident[0:L, 0:L], col[:, 0:1], None, ALU.mult))
                dve.wait_ge(wide, 1)
                step(v.tensor_copy(weights[:], psB[:, 0:L]))
                step(v.tensor_reduce(wsum[:], weights[:], AX.X, ALU.add))
                dve.wait_ge(w_in, 112)
                step(v.tensor_scalar(bw[:], bi[:], wsum[:, 0:1], None, ALU.mult))
                for c in range(KC):
                    for half in range(2):
                        seg = CT[:, c, half * (N // 2):(half + 1) * (N // 2)].rearrange("p (b l) -> p b l", l=L)
                        step(v.tensor_tensor(weighted[:, half], seg, spread(weights[:], 1, B // 2), ALU.mult))
                        step(v.tensor_reduce(ST[:, c, half * (B // 2):(half + 1) * (B // 2)], weighted[:, half], AX.X,
                                             ALU.add))
                for c in range(KC):
                    dve.wait_ge(hid, c + 1)
                    step(v.tensor_scalar(HT[:, c, :], psH[:, c, 0:B], bw[:, c:c + 1], None, ALU.add))
                dve.wait_ge(summed, 1)
                step(v.scalar_tensor_tensor(SUM[:], psS[:, 0:D], 1.0 / L, bo[:], ALU.mult, ALU.add))
                step.end()

                def back(g, w):
                    dve.wait_ge(added, g + 1)
                    for j in range(G):
                        v.bn_stats(stats[:, j, :], Y[:, w, j, :])
                    dve.drain()
                    for j in range(G):
                        v.bn_aggr(mv[:, j, :], stats[:, j, :]).then_inc(stats_done, 1)
                    dve.wait_ge(rstd_done, g + 1)
                    dve.wait_ge(stats_done, g * G + G)
                    for j in range(G):
                        v.tensor_scalar(Y[:, w, j], Y[:, w, j], mv[:, j, 0:1], rstd[:, j:j + 1], ALU.subtract,
                                        ALU.mult).then_inc(normed, 1)
                    dve.wait_ge(gained, g + 1)
                    step = Steps(dve, y_steps, 2, g)
                    step(v.tensor_tensor(Y[:, w], Y[:, w], spread(bet[:], 1, G), ALU.add))
                    xs = X[:, bass.ds(g * G, G), :]
                    step(v.tensor_tensor(xs, xs, Y[:, w], ALU.add))
                    step.end()

                pipeline(dve, lambda g, w: norm.on_vector(dve, g, Y[:, w]), back)

            @block.tensor
            def _(pe):
                pe.wait_ge(w_in, 112)
                for m, W in enumerate((WI, WO)):
                    for k_ in range(KC):
                        for c in range(KC):
                            mm = nc.tensor.transpose(psW[:, m, k_, c * P:(c + 1) * P], W[:, c, k_ * P:(k_ + 1) * P],
                                                     ident[:])
                    mm.then_inc(w_turned, 1)
                pe.wait_ge(steps, 7)
                nc.tensor.matmul(psB[:, 0:L], all1[:], diag[:], start=True, stop=True).then_inc(wide, 1)
                pe.wait_ge(steps, 18)
                pe.wait_ge(w_copied, 1)
                for e in range(KC):
                    for c in range(KC):
                        mm = nc.tensor.matmul(psH[:, e, 0:B], WIT[:, c, e * P:(e + 1) * P], ST[:, c, :],
                                              start=(c == 0), stop=(c == KC - 1))
                    mm.then_inc(hid, 1)
                pe.wait_ge(steps, 20)
                pe.wait_ge(w_copied, 2)
                for e in range(KC):
                    mm = nc.tensor.matmul(psS[:, 0:D], HT[:, e, :], WOT[:, e, :], start=(e == 0), stop=(e == KC - 1))
                mm.then_inc(summed, 1)

            @block.scalar
            def _(act):
                act.wait_ge(w_in, 112)
                nc.scalar.activation(k[:, 0:1], decay[:], ACT.Exp, scale=-1.0).then_inc(expd, 1)
                for m, WT in enumerate((WIT, WOT)):
                    act.wait_ge(w_turned, m + 1)
                    nc.scalar.copy(WT[:], psW[:, m]).then_inc(w_copied, 1)

def mk_xattn_ffn_d4(nc, io, out):
    zq = nc.dram_tensor("z_parts", (3, DH0, 2 * NH0, T, D), BF16, kind="Internal").ap()
    ck = nc.dram_tensor("context_parts", (3, DH0, 2 * NH0, T, D), BF16, kind="Internal").ap()
    o_num = nc.dram_tensor("o_num", (T, 4, 4, DH0, D), F32, kind="Internal").ap()
    o_den = nc.dram_tensor("o_den", (T, 4, 4, D), F32, kind="Internal").ap()
    sums = nc.dram_tensor("summaries", (B, D), F32, kind="Internal").ap()
    with ExitStack() as ctx:
        s = Scope(nc, ctx, "all")
        X = s.sb("X", [P, T, D])
        CT = s.sb("CT", [P, KC, N])
        ident = s.sb("ident", [P, P])
        identb = s.sb("identb", [P, P], BF16)
        prepare(nc, io, X, CT, ident, zq, ck)
        with nc.Block() as block:

            @block.vector
            def _(dve):
                nc.vector.tensor_copy(identb[:], ident[:])

        row_attention(nc, io, X, CT, identb, zq, ck, o_num, o_den)
        selected_ffn(nc, io, X, ident)
        gated_attention(nc, io, X, CT, ident, identb)
        normed_ffn(nc, io, X, ident, identb)
        softmax_attention(nc, io, X, CT, ident)
        gated_ffn(nc, io, X, ident, identb)
        summary_mix(nc, io, X, CT, ident, sums)
        quantized_ffn(nc, io, X, ident, out)

_INS = ["x", "ctx_2048", "L0_ffn_w_r", "L0_ffn_b_r", "L0_ffn_w1", "L0_ffn_b1", "L0_ffn_w2", "L0_ffn_b2",
        "L1_xattn_Wi", "L1_xattn_bi", "L1_xattn_Wf", "L1_xattn_bf", "L1_xattn_ln_scale", "L1_ffn_w1", "L1_ffn_b1",
        "L1_ffn_ln_g", "L1_ffn_ln_b", "L1_ffn_w2", "L1_ffn_b2", "L2_xattn_Wq", "L2_xattn_bq", "L2_xattn_Wk",
        "L2_xattn_bk", "L2_xattn_Wv", "L2_xattn_bv", "L2_xattn_Wo", "L2_xattn_bo", "L2_ffn_w_gate", "L2_ffn_w_up",
        "L2_ffn_w_down", "L3_xattn_decay", "L3_xattn_W_in", "L3_xattn_b_in", "L3_xattn_W_out", "L3_xattn_b_out",
        "L3_xattn_gamma", "L3_xattn_beta", "L3_ffn_kernel", "L3_ffn_bias"]

def kernel(**inputs):
    import numpy as _np
    import concourse.bacc as _bacc
    from concourse import mybir as _mybir
    from concourse.bass_utils import run_bass_kernel_spmd as _run

    nc = _bacc.Bacc("TRN2", target_bir_lowering=False, num_devices=1)
    arrays, io = {}, {}
    for name in _INS:
        a = _np.ascontiguousarray(inputs[name])
        if a.ndim == 0:
            a = a.reshape(1)
        arrays[f"in_{name}_dram"] = a
        io[name] = nc.dram_tensor(f"in_{name}_dram", a.shape, _mybir.dt.from_np(a.dtype), kind="ExternalInput").ap()
    out = nc.dram_tensor("out_0_dram", (B, L, D), F32, kind="ExternalOutput").ap()
    mk_xattn_ffn_d4(nc, io, out)
    r = _run(nc, [arrays], core_ids=[0])
    return r.results[0]["out_0_dram"]
```

```python
from contextlib import ExitStack

import numpy as np

import concourse.bass as bass
from concourse import mybir

ALU = mybir.AluOpType
ACT = mybir.ActivationFunctionType
AX = mybir.AxisListType
F32 = mybir.dt.float32
BF16 = mybir.dt.bfloat16

P = 128
B, L, D = 64, 64, 256
N = B * L
T = N // P
G = 4
NG = T // G
KC = D // P
FF = 4 * D
NH0, DH0 = 8, 8
BH = B * NH0
NH, DH = 16, 16
KEEP = L // 2
LN_EPS = 1e-5
MAGIC = 12582912.0
BIG = 1.0e30

class Scope:

    def __init__(self, nc, ctx, name):
        self.nc, self.ctx, self.name, self.sems = nc, ctx, name, []
        ctx.callback(self.close)

    def sb(self, name, shape, dt=F32):
        return self.ctx.enter_context(self.nc.sbuf_tensor(f"{self.name}_{name}", shape, dt))

    def ps(self, name, shape, dt=F32):
        return self.ctx.enter_context(self.nc.psum_tensor(f"{self.name}_{name}", shape, dt))

    def sem(self, name):
        self.sems.append(self.nc.alloc_semaphore(name=f"{self.name}_{name}"))
        return self.sems[-1]

    def close(self):
        if self.sems:
            self.nc.clear_and_free_semaphores(self.sems)
            self.nc.all_engine_barrier()

class Steps:

    def __init__(self, engine, done, per, i=0):
        self.engine, self.done, self.per, self.i, self.n = engine, done, per, i, 0

    def __call__(self, instruction):
        self.n += 1
        instruction.then_inc(self.done, 1)
        self.engine.wait_ge(self.done, self.i * self.per + self.n)

    def end(self):
        assert self.n == self.per, (self.n, self.per)

def held(engine, value):
    return value if isinstance(value, int) else engine.snap(value)

def spread(ap, dim, n):
    return ap.unsqueeze(dim).to_broadcast(list(ap.shape[:dim]) + [n] + list(ap.shape[dim:]))

def prepare(nc, io, X, CT, ident, zq, ck):
    with ExitStack() as ctx:
        s = Scope(nc, ctx, "prep")
        C = s.sb("C", [P, 2, G, D])
        Z = s.sb("Z", [P, G, D])
        ZR = s.sb("ZR", [P, 2, G, D])
        CR = s.sb("CR", [P, 2, G, D])
        ZS = s.sb("ZS", [P, 3, G, D], BF16)
        CS = s.sb("CS", [P, 3, G, D], BF16)
        stats = s.sb("stats", [P, G, 6])
        mv = s.sb("mv", [P, G, 2])
        veps = s.sb("veps", [P, G])
        rstd = s.sb("rstd", [P, G])
        mhalf = s.sb("mhalf", [P, G])
        eps = s.sb("eps", [P, G])
        psC = s.ps("psC", [P, KC, G * P])
        ready = s.sem("ready")
        x_in, c_in = s.sem("x_in"), s.sem("c_in")
        stats_done, rstd_done, pool_step = s.sem("stats_done"), s.sem("rstd_done"), s.sem("pool_step")
        z_done = s.sem("z_done")
        z_part, z_rest, c_part, c_rest = s.sem("z_part"), s.sem("z_rest"), s.sem("c_part"), s.sem("c_rest")
        turned, ct_done = s.sem("turned"), s.sem("ct_done")
        z_out, c_out = s.sem("z_out"), s.sem("c_out")
        x_dram = io["x"].rearrange("(t u) l d -> t (u l) d", u=2)
        c_dram = io["ctx_2048"].rearrange("(t u) l d -> t (u l) d", u=2)
        zq_w = zq.rearrange("s r a h u m -> s a h r (u m)")
        ck_w = ck.rearrange("s r a h u m -> s a h r (u m)")

        with nc.Block() as block:

            @block.sync
            def _(sp):
                def load(t, w):
                    sp.dma_start(X[:, bass.ds(t, G), :],
                                 x_dram[bass.ds(t, G)].rearrange("t p d -> p t d")).then_inc(x_in, 16)
                    sp.dma_start(C[:, w], c_dram[bass.ds(t, G)].rearrange("t p d -> p t d")).then_inc(c_in, 16)

                load(0, 0)
                def turn(h, last):
                    for w in range(2):
                        g = h * 2 + w
                        to = [held(sp, g * (G // 2) + a) for a in range(G // 2)]
                        ahead, loads, before = (held(sp, v) for v in (g * G + G, g * 16 + 16, g * 16))
                        parts = [held(sp, g * 3 + part + 1) for part in range(3)]
                        sp.wait_ge(x_in, loads)
                        sp.wait_ge(c_in, loads)
                        sp.wait_ge(c_rest, before)
                        sp.wait_ge(turned, before)
                        if w == 0 or not last:
                            load(ahead, 1 - w)
                        for part in range(3):
                            sp.wait_ge(z_part, parts[part])
                            for a in range(G // 2):
                                sp.dma_start(zq_w[part, bass.ds(to[a], 1)], ZS[:, part, 2 * a:2 * a + 2].rearrange(
                                    "p u m -> p (u m)")).then_inc(z_out, 16)
                        for part in range(3):
                            sp.wait_ge(c_part, parts[part])
                            for a in range(G // 2):
                                sp.dma_start(ck_w[part, bass.ds(to[a], 1)], CS[:, part, 2 * a:2 * a + 2].rearrange(
                                    "p u m -> p (u m)")).then_inc(c_out, 16)

                with sp.Fori(0, NG // 2 - 1) as h:
                    turn(h, False)
                turn(NG // 2 - 1, True)
                sp.wait_ge(z_out, 16 * 6 * NG)
                sp.wait_ge(c_out, 16 * 6 * NG)

            @block.gpsimd
            def _(pool):
                nc.gpsimd.memset(mhalf[:], -0.5).then_inc(ready, 1)
                nc.gpsimd.memset(eps[:], LN_EPS).then_inc(ready, 1)
                nc.gpsimd.memset(ident[:], 0.0).then_inc(ready, 1)
                pool.wait_ge(ready, 3)
                nc.gpsimd.affine_select(out=ident[:], in_=ident[:], compare_op=ALU.not_equal, fill=1.0, base=0,
                                        pattern=[[-1, P]], channel_multiplier=1).then_inc(ready, 1)
                with pool.Fori(0, NG // 2) as h:
                    for w in range(2):
                        g = h * 2 + w
                        step = Steps(pool, pool_step, 1, g)
                        pool.wait_ge(stats_done, g * G + G)
                        step(nc.gpsimd.tensor_tensor(veps[:], mv[:, :, 1], eps[:], ALU.add))
                        nc.gpsimd.tensor_tensor(rstd[:], veps[:], mhalf[:], ALU.pow).then_inc(rstd_done, 1)
                        step.end()
                        pool.wait_ge(c_part, g * 3 + 1)
                        nc.gpsimd.tensor_tensor(CR[:, 0], C[:, w], CS[:, 0], ALU.subtract).then_inc(c_rest, 8)
                        pool.wait_ge(c_part, g * 3 + 2)
                        pool.wait_ge(c_rest, g * 16 + 8)
                        nc.gpsimd.tensor_tensor(CR[:, 1], CR[:, 0], CS[:, 1], ALU.subtract).then_inc(c_rest, 8)

            @block.tensor
            def _(pe):
                pe.wait_ge(ready, 4)
                with pe.Fori(0, NG // 2) as h:
                    for w in range(2):
                        g = h * 2 + w
                        pe.wait_ge(c_in, g * 16 + 16)
                        pe.wait_ge(ct_done, g * KC)
                        for k in range(KC):
                            for j in range(G):
                                mm = nc.tensor.transpose(psC[:, k, j * P:(j + 1) * P],
                                                         C[:, w, j, k * P:(k + 1) * P], ident[:])
                        mm.then_inc(turned, 16)

            @block.scalar
            def _(act):
                with act.Fori(0, NG // 2) as h:
                    for w in range(2):
                        g = h * 2 + w
                        act.wait_ge(c_in, g * 16 + 16)
                        act.wait_ge(c_out, g * (16 * 6))
                        nc.scalar.copy(CS[:, 0], C[:, w]).then_inc(c_part, 1)
                        act.wait_ge(z_done, g * G + G)
                        act.wait_ge(z_out, g * (16 * 6))
                        nc.scalar.copy(ZS[:, 0], Z[:]).then_inc(z_part, 1)
                        act.wait_ge(turned, g * 16 + 16)
                        for k in range(KC):
                            nc.scalar.copy(CT[:, k, bass.ds(g * (G * P), G * P)], psC[:, k, :]).then_inc(ct_done, 1)
                        act.wait_ge(c_rest, g * 16 + 8)
                        nc.scalar.copy(CS[:, 1], CR[:, 0]).then_inc(c_part, 1)
                        act.wait_ge(z_rest, g * 2 + 1)
                        nc.scalar.copy(ZS[:, 1], ZR[:, 0]).then_inc(z_part, 1)
                        act.wait_ge(c_rest, g * 16 + 16)
                        nc.scalar.copy(CS[:, 2], CR[:, 1]).then_inc(c_part, 1)
                        act.wait_ge(z_rest, g * 2 + 2)
                        nc.scalar.copy(ZS[:, 2], ZR[:, 1]).then_inc(z_part, 1)

            @block.vector
            def _(dve):
                with dve.Fori(0, NG // 2) as h:
                    for w in range(2):
                        g = h * 2 + w
                        dve.wait_ge(x_in, g * 16 + 16)
                        dve.wait_ge(rstd_done, g)
                        for j in range(G):
                            nc.vector.bn_stats(stats[:, j, :], X[:, g * G + j, :])
                        dve.drain()
                        for j in range(G):
                            nc.vector.bn_aggr(mv[:, j, :], stats[:, j, :]).then_inc(stats_done, 1)
                        dve.wait_ge(rstd_done, g + 1)
                        dve.wait_ge(stats_done, g * G + G)
                        for j in range(G):
                            nc.vector.tensor_scalar(Z[:, j, :], X[:, g * G + j, :], mv[:, j, 0:1], rstd[:, j:j + 1],
                                                    ALU.subtract, ALU.mult).then_inc(z_done, 1)
                        dve.wait_ge(z_part, g * 3 + 1)
                        dve.wait_ge(z_done, g * G + G)
                        nc.vector.tensor_tensor(ZR[:, 0], Z[:], ZS[:, 0], ALU.subtract).then_inc(z_rest, 1)
                        dve.wait_ge(z_part, g * 3 + 2)
                        dve.wait_ge(z_rest, g * 2 + 1)
                        nc.vector.tensor_tensor(ZR[:, 1], ZR[:, 0], ZS[:, 1], ALU.subtract).then_inc(z_rest, 1)

def row_attention(nc, io, X, CT, identb, zq, ck, o_dram):
    R = 9 * DH0
    RM = R + 3
    H2 = 2 * NH0
    QUADS = H2 // 4
    PAIR = 16 * 4
    SCALE = float(DH0) ** -0.5
    with ExitStack() as ctx:
        s = Scope(nc, ctx, "ratt")
        Q9 = s.sb("Q9", [P, 2, H2, 2, D], BF16)
        K9 = s.sb("K9", [P, 2, H2, 2, D], BF16)
        E = s.sb("E", [P, 2, 4, KC, D])
        V9 = s.sb("V9", [P, 2, KC, NH0, 32])
        nmax = s.sb("nmax", [P, 2, 2, NH0])
        rest = s.sb("rest", [P, 2, 2, NH0])
        zero = s.sb("zero", [P, 2, NH0])
        parts = s.sb("parts", [P, 2, P], BF16)
        rows = s.sb("rows", [2 * 3 * NH0, 2, P], BF16)
        O = s.sb("O", [P, 2, QUADS, D])
        num = s.sb("num", [P, 2, D])
        den = s.sb("den", [P, 2, D])
        psS = s.ps("psS", [P, 2, 2, D])
        psT = s.ps("psT", [P, 2, 2, KC, D])
        psO = s.ps("psO", [P, 2, D])
        psM = s.ps("psM", [P, 2, 512], BF16)
        ready, ones_set = s.sem("ready"), s.sem("ones_set")
        pair_in = [s.sem(f"pair_in{b}") for b in range(2)]
        scores, maxed, pool_step, split, turned, row_out = (
            s.sem(x) for x in ("scores", "maxed", "pool_step", "split", "turned", "row_out"))
        row_in = [s.sem(f"row_in{b}") for b in range(2)]
        o_back = [s.sem(f"o_back{b}") for b in range(2)]
        shifted, exped, v_in, pv, o_out = (s.sem(x) for x in ("shifted", "exped", "v_in", "pv", "o_out"))
        to_dram, recip, scaled, added = (s.sem(x) for x in ("to_dram", "recip", "scaled", "added"))

        with nc.Block() as block:

            @block.gpsimd
            def _(pool):
                nc.gpsimd.memset(Q9[64:P], 0.0).then_inc(ready, 1)
                pool.wait_ge(ready, 1)
                nc.gpsimd.memset(zero[:], 0.0).then_inc(ready, 1)
                nc.gpsimd.memset(parts[:], 0.0).then_inc(ready, 1)
                nc.gpsimd.memset(V9[:], 0.0).then_inc(ready, 1)
                pool.wait_ge(ready, 4)
                nc.gpsimd.memset(V9[:, :, :, :, DH0:DH0 + 1], 1.0).then_inc(ready, 1)
                pool.wait_ge(ready, 5)

                def take(t, b):
                    unit = t * 2 + b
                    if not isinstance(t, int) or t > 0:
                        pool.wait_ge(pv, t * QUADS + (2 * b - 2))
                    nc.gpsimd.tensor_copy(
                        V9[:, b, :, :, 0:DH0],
                        CT[:, :, bass.ds(t * P + b * L, L)].rearrange("p k (h r) -> p k h r", r=DH0),
                    ).then_inc(v_in, 1)

                def split_max(t, b):
                    unit = t * 2 + b
                    step = Steps(pool, pool_step, 4, unit)
                    pool.wait_ge(maxed, t * H2 + (b + 1) * NH0)
                    if not isinstance(t, int) or t > 0:
                        pool.wait_ge(turned, unit - 1)
                    p = parts[:, b].rearrange("p (c q) -> p c q", c=2)[:, :, 0:3 * NH0].rearrange(
                        "p c (s h) -> p c s h", s=3)
                    step(nc.gpsimd.tensor_tensor(p[:, :, 0], nmax[:, b], zero[:], ALU.add))
                    step(nc.gpsimd.tensor_tensor(rest[:, 0], nmax[:, b], p[:, :, 0], ALU.subtract))
                    step(nc.gpsimd.tensor_tensor(p[:, :, 1], rest[:, 0], zero[:], ALU.add))
                    step(nc.gpsimd.tensor_tensor(rest[:, 1], rest[:, 0], p[:, :, 1], ALU.subtract))
                    nc.gpsimd.tensor_tensor(p[:, :, 2], rest[:, 1], zero[:], ALU.add).then_inc(split, 1)
                    step.end()

                def scale_and_add(t, par):
                    pool.wait_ge(recip, t + 1)
                    nc.gpsimd.tensor_tensor(num[:, par], num[:, par], den[:, par], ALU.mult).then_inc(scaled, 1)
                    pool.wait_ge(scaled, t + 1)
                    nc.gpsimd.tensor_tensor(X[:, t, :], X[:, t, :], num[:, par], ALU.add).then_inc(added, 16)

                def step(i, k, has_s=True, has_t=True):
                    t = i * 4 + k
                    for b in range(2):
                        if has_t:
                            take(t, b)
                        if has_s:
                            split_max(t + 1, b)
                    if has_t and (k > 0 or not isinstance(i, int) or i > 0):
                        scale_and_add(t - 1, (k + 1) % 2)

                split_max(0, 0)
                split_max(0, 1)
                step(0, 0)
                step(0, 1)
                step(0, 2)
                step(0, 3)
                with pool.Fori(1, T // 4 - 1) as i:
                    for k in range(4):
                        step(i, k)
                for k in range(4):
                    step(T // 4 - 1, k, has_s=k < 3)
                scale_and_add(T - 1, 1)

            @block.sync
            def _(sp):
                def load(pair, pb):
                    z = zq.rearrange("s r a h u m -> (s r) a (h u m)")[:, bass.ds(pair, 1), :]
                    sp.dma_start(Q9[0:R, pb].rearrange("p h u m -> p (h u m)"), spread(z, 0, 3)).then_inc(
                        pair_in[pb], 16)
                    for a in range(3):
                        k = ck[a].rearrange("r a h u m -> r a (h u m)")[:, bass.ds(pair, 1), :]
                        sp.dma_start(K9[24 * a:24 * a + 24, pb].rearrange("p h u m -> p (h u m)"),
                                     spread(k, 0, 3)).then_inc(pair_in[pb], 16)

                def bring_row(t, pb, u, b):
                    sp.wait_ge(row_out, t * 2 + b + 1)
                    for c in range(2):
                        sp.dma_start(Q9[R:RM, pb, b * NH0:(b + 1) * NH0, u, c * P:(c + 1) * P],
                                     rows[c * 24:c * 24 + 24, b, :]).then_inc(row_in[b], 16)

                def out(t, par):
                    sp.wait_ge(o_out, t * QUADS + QUADS)
                    for g in range(4):
                        sp.dma_start(o_dram.rearrange("t q g c m -> g c (t q) m")[g][:, bass.ds(t * QUADS, QUADS), :],
                                     O[32 * g:32 * g + DH0 + 1, par]).then_inc(to_dram, 16)

                def back(t, par):
                    sp.wait_ge(to_dram, t * 64 + 64)
                    if not isinstance(t, int) or t > 1:
                        sp.wait_ge(added, t * 16 - 16)
                    o = o_dram.rearrange("t q g c m -> (t q g) c m")[bass.ds(t * H2, H2)]
                    sp.dma_start(num[:, par], o[:, 0:DH0, :]).then_inc(o_back[par], 16)
                    sp.dma_start(den[:, par], spread(o[:, DH0, :], 1, DH0)).then_inc(o_back[par], 16)

                def step(i, k, has_s=True, has_t=True):
                    t = i * 4 + k
                    past = not isinstance(i, int) or i > 0
                    pb1, u1 = ((k + 1) // 2) % 2, (k + 1) % 2
                    if past or k > 0:
                        bring_row(t, (k // 2) % 2, k % 2, 1)
                        out(t - 1, (k + 1) % 2)
                        back(t - 1, (k + 1) % 2)
                    if has_s:
                        bring_row(t + 1, pb1, u1, 0)
                    if k % 2 == 1 and has_s and not (isinstance(i, int) and i == T // 4 - 1):
                        sp.wait_ge(shifted, t * 8 + 8)
                        load(i * 2 + (k + 3) // 2, (k // 2) % 2)

                sp.wait_ge(ones_set, 1)
                sp.wait_ge(ready, 1)
                load(0, 0)
                load(1, 1)
                bring_row(0, 0, 0, 0)
                bring_row(0, 0, 0, 1)
                for k in range(4):
                    step(0, k)
                with sp.Fori(1, T // 4 - 1) as i:
                    for k in range(4):
                        step(i, k)
                for k in range(4):
                    step(T // 4 - 1, k, has_s=k < 3)
                out(T - 1, 1)
                back(T - 1, 1)

            @block.tensor
            def _(pe):
                def score(t, pb, u, hh):
                    if not isinstance(t, int) or t > 0 or hh > 1:
                        pe.wait_ge(maxed, t * H2 + (hh - 1))
                    for c in range(2):
                        mm = nc.tensor.matmul(psS[:, hh % 2, c, :], Q9[0:R, pb, hh, u, c * P:(c + 1) * P],
                                              K9[0:R, pb, hh, u, :], start=True, stop=True)
                    mm.then_inc(scores, 1)

                def turn_max(t, b):
                    unit = t * 2 + b
                    pe.wait_ge(split, unit + 1)
                    pe.wait_ge(row_out, unit)
                    nc.tensor.transpose(psM[:, b, 0:P], parts[:, b, :], identb[:]).then_inc(turned, 1)

                def shift(t, pb, u, hh):
                    pair = t * 8 + hh // 2
                    if not isinstance(t, int) or t > 0 or hh > 2:
                        pe.wait_ge(exped, pair - 1)
                    for h in range(hh, hh + 2):
                        for c in range(KC):
                            mm = nc.tensor.matmul(psT[:, (hh // 2) % 2, h % 2, c, :],
                                                  K9[:, pb, h, u, c * P:(c + 1) * P],
                                                  Q9[:, pb, h, u, :], start=True, stop=True)
                    mm.then_inc(shifted, 1)

                def values(t, qd):
                    quad = t * QUADS + qd
                    pe.wait_ge(exped, t * 8 + 2 * qd + 2)
                    pe.wait_ge(v_in, t * 2 + qd // 2 + 1)
                    pe.wait_ge(o_out, quad)
                    for c in range(KC):
                        for g in range(4):
                            h = (qd * 4 + g) % NH0
                            mm = nc.tensor.matmul(psO[32 * g:32 * g + 32, qd % 2, :], V9[:, qd // 2, c, h, :],
                                                  E[:, qd % 2, g, c, :], start=(c == 0), stop=(c == KC - 1),
                                                  skip_group_check=True)
                    mm.then_inc(pv, 1)

                def step(i, k, has_s=True, has_t=True):
                    t = i * 4 + k
                    pb0, u0 = (k // 2) % 2, k % 2
                    pb1, u1 = ((k + 1) // 2) % 2, (k + 1) % 2
                    first_tile = isinstance(i, int) and i == 0 and k == 0
                    if has_s and k % 2 == 1:
                        pe.wait_ge(pair_in[pb1], (i + 1 + k // 2) * PAIR)
                    for b in range(2):
                        if has_t:
                            pe.wait_ge(row_in[b], t * 32 + 32)
                        for pr in range(4):
                            hh = b * NH0 + 2 * pr
                            if has_s:
                                score(t + 1, pb1, u1, hh)
                                score(t + 1, pb1, u1, hh + 1)
                            if pr == 1:
                                if b == 0:
                                    if not first_tile:
                                        turn_max(t, 1)
                                elif has_s:
                                    turn_max(t + 1, 0)
                            if has_t:
                                shift(t, pb0, u0, hh)
                                if pr % 2 == 1:
                                    qd = 2 * b + pr // 2
                                    if qd > 0:
                                        values(t, qd - 1)
                                    elif not first_tile:
                                        values(t - 1, QUADS - 1)

                pe.wait_ge(ready, 5)
                pe.wait_ge(pair_in[0], PAIR)
                for hh in range(H2):
                    score(0, 0, 0, hh)
                turn_max(0, 0)
                turn_max(0, 1)
                for k in range(4):
                    step(0, k)
                with pe.Fori(1, T // 4 - 1) as i:
                    for k in range(4):
                        step(i, k)
                for k in range(4):
                    step(T // 4 - 1, k, has_s=k < 3)
                values(T - 1, QUADS - 1)

            @block.scalar
            def _(act):
                def row(t, b):
                    unit = t * 2 + b
                    act.wait_ge(turned, unit + 1)
                    if not isinstance(t, int) or t > 0:
                        act.wait_ge(row_in[b], t * 32)
                    nc.scalar.copy(rows[:, b, :], psM[0:48, b, 0:P]).then_inc(row_out, 1)

                def exp(t, hh):
                    quad = t * QUADS + hh // 4
                    act.wait_ge(shifted, t * 8 + hh // 2 + 1)
                    if not isinstance(t, int) or t > 0 or hh > 7:
                        act.wait_ge(pv, quad - 1)
                    nc.scalar.activation(E[:, (hh // 4) % 2, hh % 4:hh % 4 + 2], psT[:, (hh // 2) % 2], ACT.Exp,
                                         scale=SCALE).then_inc(exped, 1)

                def leave(t, qd):
                    act.wait_ge(pv, t * QUADS + qd + 1)
                    if qd == 0 and (not isinstance(t, int) or t > 1):
                        act.wait_ge(to_dram, (t - 1) * 64)
                    par = leave.par
                    nc.scalar.copy(O[:, par, qd, :], psO[:, qd % 2, :]).then_inc(o_out, 1)

                def step(i, k, has_s=True, has_t=True):
                    t = i * 4 + k
                    first_tile = isinstance(i, int) and i == 0 and k == 0
                    for b in range(2):
                        for pr in range(4):
                            exp(t, b * NH0 + 2 * pr)
                            if pr == 1:
                                if b == 0:
                                    if not first_tile:
                                        row(t, 1)
                                elif has_s:
                                    row(t + 1, 0)
                            if pr % 2 == 1:
                                qd = 2 * b + pr // 2
                                if qd > 0:
                                    leave.par = k % 2
                                    leave(t, qd - 1)
                                elif not first_tile:
                                    leave.par = (k + 1) % 2
                                    leave(t - 1, QUADS - 1)

                row(0, 0)
                row(0, 1)
                for k in range(4):
                    step(0, k)
                with act.Fori(1, T // 4 - 1) as i:
                    for k in range(4):
                        step(i, k)
                for k in range(4):
                    step(T // 4 - 1, k, has_s=k < 3)
                leave.par = 1
                leave(T - 1, QUADS - 1)

            @block.vector
            def _(dve):
                def max_of(t, hh):
                    b = hh // NH0
                    if hh % NH0 == 0 and (not isinstance(t, int) or t > 0):
                        dve.wait_ge(split, t * 2 + b - 1)
                    dve.wait_ge(scores, t * H2 + hh + 1)
                    nc.vector.tensor_reduce(nmax[:, b, :, hh % NH0], psS[:, hh % 2], AX.X, ALU.max,
                                            negate=True).then_inc(maxed, 1)

                def invert(t, par, half):
                    dve.wait_ge(o_back[par], half * 32 + 32)
                    nc.vector.reciprocal(den[:, par], den[:, par]).then_inc(recip, 1)

                def step(i, k, has_s=True, has_t=True):
                    t = i * 4 + k
                    past = not isinstance(i, int) or i > 0
                    if has_s:
                        for hh in range(H2):
                            max_of(t + 1, hh)
                    if past or k > 0:
                        invert(t - 1, (k + 1) % 2, i * 2 + (k - 1) // 2)

                nc.vector.memset(K9[64:P], 1.0).then_inc(ones_set, 1)
                for hh in range(H2):
                    max_of(0, hh)
                for k in range(4):
                    step(0, k)
                with dve.Fori(1, T // 4 - 1) as i:
                    for k in range(4):
                        step(i, k)
                for k in range(4):
                    step(T // 4 - 1, k, has_s=k < 3)
                invert(T - 1, 1, T // 2 - 1)

def pipeline(engine, front, back):
    front(0, 0)
    front(1, 1)
    back(0, 0)
    with engine.Fori(0, NG // 2 - 1) as h:
        front(h * 2 + 2, 0)
        back(h * 2 + 1, 1)
        front(h * 2 + 3, 1)
        back(h * 2 + 2, 0)
    back(NG - 1, 1)

def rounds(engine, step, last):
    step(0, 0)
    step(1, 1)
    with engine.Fori(1, NG // 2 - 1) as h:
        step(h * 2, 0)
        step(h * 2 + 1, 1)
    for g in range(NG - 2, last + 1):
        step(g, g % 2)

def is_group(g):
    return not isinstance(g, int) or 0 <= g < NG

def later(g, rounds):
    return not isinstance(g, int) or g >= rounds

class Norm:

    def __init__(self, nc, s, X, eps=LN_EPS):
        self.nc, self.X, self.eps_value = nc, X, eps
        self.stats = s.sb("stats", [P, G, 6])
        self.mv = s.sb("mv", [P, G, 2])
        self.veps = s.sb("veps", [P, G])
        self.rstd = s.sb("rstd", [P, G])
        self.mhalf = s.sb("mhalf", [P, G])
        self.eps = s.sb("eps", [P, G])
        self.set = s.sem("norm_set")
        self.stats_done, self.veps_done = s.sem("stats_done"), s.sem("veps_done")
        self.rstd_done, self.normed = s.sem("rstd_done"), s.sem("normed")

    def constants(self, pool):
        self.nc.gpsimd.memset(self.mhalf[:], -0.5).then_inc(self.set, 1)
        self.nc.gpsimd.memset(self.eps[:], self.eps_value).then_inc(self.set, 1)
        pool.wait_ge(self.set, 2)

    def on_pool(self, pool, g):
        pool.wait_ge(self.stats_done, g * G + G)
        self.nc.gpsimd.tensor_tensor(self.veps[:], self.mv[:, :, 1], self.eps[:], ALU.add).then_inc(self.veps_done, 1)
        pool.wait_ge(self.veps_done, g + 1)
        self.nc.gpsimd.tensor_tensor(self.rstd[:], self.veps[:], self.mhalf[:], ALU.pow).then_inc(self.rstd_done, 1)

    def on_vector(self, dve, g, Z):
        self.take_stats(dve, g)
        self.normalise(dve, g, Z)

    def take_stats(self, dve, g):
        for j in range(G):
            self.nc.vector.bn_stats(self.stats[:, j, :], self.X[:, g * G + j, :])
        dve.drain()
        for j in range(G):
            self.nc.vector.bn_aggr(self.mv[:, j, :], self.stats[:, j, :]).then_inc(self.stats_done, 1)

    def normalise(self, dve, g, Z):
        dve.wait_ge(self.rstd_done, g + 1)
        dve.wait_ge(self.stats_done, g * G + G)
        for j in range(G):
            self.nc.vector.tensor_scalar(Z[:, j, :], self.X[:, g * G + j, :], self.mv[:, j, 0:1],
                                         self.rstd[:, j:j + 1], ALU.subtract, ALU.mult).then_inc(self.normed, 1)

def selected_ffn(nc, io, X, ident):
    FC = FF // P
    SL = 2 * KEEP
    with ExitStack() as ctx:
        s = Scope(nc, ctx, "sffn")
        norm = Norm(nc, s, X)
        W1 = s.sb("W1", [P, KC, FF])
        W2 = s.sb("W2", [P, FC, D])
        b1 = s.sb("b1", [P, FC])
        b2 = s.sb("b2", [P, D])
        wr = s.sb("wr", [P, D])
        br = s.sb("br", [P, 1])
        Z = s.sb("Z", [P, 2, G, D])
        zw = s.sb("zw", [P, D])
        sc = s.sb("sc", [P, 2, G])
        same = s.sb("same", [P, P])
        own = s.sb("own", [P, L])
        before = s.sb("before", [P, L])
        slot = s.sb("slot", [P, SL])
        diag = s.sb("diag", [P, G, L])
        work = s.sb("work", [P, 3, G, L])
        mine = s.sb("mine", [P, G])
        rank = s.sb("rank", [P, G])
        pick = s.sb("pick", [P, 2, G, SL])
        XS = s.sb("XS", [P, KC, G * SL])
        PT = s.sb("PT", [P, G, P])
        H = s.sb("H", [P, FC, G * SL])
        OS = s.sb("OS", [P, 2, D])
        psR = s.ps("psR", [P, G, L + L])
        psG = s.ps("psG", [P, KC, G * SL])
        psP = s.ps("psP", [P, 4, P])
        psH = s.ps("psH", [P, 2, 2, G * SL])
        psO = s.ps("psO", [P, 2, D])
        psX = s.ps("psX", [P, G, D])
        w_in, ready = s.sem("w_in"), s.sem("ready")
        steps, diag_done, rows_done, pick_done = (s.sem(x) for x in ("steps", "diag_done", "rows_done", "pick_done"))
        gathered, turned, xs_done, pt_done = (s.sem(x) for x in ("gathered", "turned", "xs_done", "pt_done"))
        hidden, gelued, put, os_done, scattered, x_done = (
            s.sem(x) for x in ("hidden", "gelued", "put", "os_done", "scattered", "x_done"))
        PER = 12

        with nc.Block() as block:

            @block.sync
            def _(sp):
                sp.dma_start(W1[:], io["L0_ffn_w1"].rearrange("(k p) f -> p k f", p=P)).then_inc(w_in, 16)
                sp.dma_start(W2[:], io["L0_ffn_w2"].rearrange("(k p) d -> p k d", p=P)).then_inc(w_in, 16)
                with nc.allow_non_contiguous_dma(reason="one column of biases for each chunk"):
                    sp.dma_start(b1[:], io["L0_ffn_b1"].rearrange("(k p) -> p k", p=P)).then_inc(w_in, 16)
                sp.dma_start(b2[:], spread(io["L0_ffn_b2"], 0, P)).then_inc(w_in, 16)
                sp.dma_start(wr[:], spread(io["L0_ffn_w_r"], 0, P)).then_inc(w_in, 16)
                sp.dma_start(br[:], spread(io["L0_ffn_b_r"], 0, P)).then_inc(w_in, 16)
                sp.wait_ge(w_in, 96)

            @block.gpsimd
            def _(pool):
                step = Steps(pool, ready, 14)
                select = lambda out, op, fill, base, cm, pattern: step(nc.gpsimd.affine_select(
                    out=out, in_=out, compare_op=op, fill=fill, base=base, pattern=pattern, channel_multiplier=cm))
                step(nc.gpsimd.memset(same[:], 1.0))
                select(same[0:L, :], ALU.is_ge, 0.0, L - 1, 0, [[-1, P]])
                select(same[L:P, :], ALU.is_ge, 0.0, -L, 0, [[1, P]])
                step(nc.gpsimd.memset(own[:], 0.0))
                select(own[0:L, :], ALU.not_equal, 1.0, 0, 1, [[-1, L]])
                select(own[L:P, :], ALU.not_equal, 1.0, 0, 1, [[-1, L]])
                step(nc.gpsimd.memset(before[:], 1.0))
                select(before[0:L, :], ALU.is_gt, 0.0, 0, 1, [[-1, L]])
                select(before[L:P, :], ALU.is_gt, 0.0, 0, 1, [[-1, L]])
                step(nc.gpsimd.iota(slot[:], pattern=[[0, 2], [1, KEEP]], base=0, channel_multiplier=0,
                                    allow_small_or_imprecise_dtypes=True))
                step(nc.gpsimd.memset(slot[0:L, KEEP:], -1.0))
                step(nc.gpsimd.memset(slot[L:P, 0:KEEP], -1.0))
                step(nc.gpsimd.memset(PT[0:L, :, :], 0.0))
                step(nc.gpsimd.memset(PT[L:P, :, :], 0.0))
                step.end()
                norm.constants(pool)
                pipeline(pool, lambda g, w: norm.on_pool(pool, g), lambda g, w: None)

            @block.vector
            def _(dve):
                def front(g, w):
                    if later(g, 2):
                        dve.wait_ge(gathered, g - 1)
                        dve.wait_ge(turned, g - 1)
                    norm.on_vector(dve, g, Z[:, w])
                    step = Steps(dve, steps, PER, g)
                    dve.wait_ge(norm.normed, g * G + G)
                    dve.wait_ge(w_in, 96)
                    dve.wait_ge(ready, 14)
                    for j in range(G):
                        step(nc.vector.tensor_tensor_reduce(zw[:], Z[:, w, j, :], wr[:], 1.0, 0.0, ALU.mult, ALU.add,
                                                            sc[:, 0, j:j + 1]))
                    step(nc.vector.tensor_scalar(sc[:, 1], sc[:, 0], br[:, 0:1], None, ALU.add))
                    nc.vector.tensor_tensor(diag[:], spread(own[:], 1, G), spread(sc[:, 1], 2, L),
                                            ALU.mult).then_inc(diag_done, 1)
                    dve.wait_ge(rows_done, g + 1)
                    R = psR[:, :, 0:L]
                    step(nc.vector.tensor_tensor(work[:, 0], R, spread(own[:], 1, G), ALU.mult))
                    step(nc.vector.tensor_reduce(mine[:], work[:, 0], AX.X, ALU.add))
                    step(nc.vector.tensor_tensor(work[:, 1], R, spread(mine[:], 2, L), ALU.is_equal))
                    step(nc.vector.tensor_tensor(work[:, 2], work[:, 1], spread(before[:], 1, G), ALU.mult))
                    step(nc.vector.tensor_tensor(work[:, 0], R, spread(mine[:], 2, L), ALU.is_gt))
                    step(nc.vector.tensor_tensor(work[:, 1], work[:, 0], work[:, 2], ALU.add))
                    step(nc.vector.tensor_reduce(rank[:], work[:, 1], AX.X, ALU.add))
                    nc.vector.tensor_tensor(pick[:, w], spread(slot[:], 1, G), spread(rank[:], 2, SL),
                                            ALU.is_equal).then_inc(pick_done, 1)
                    step.end()

                def back(g, w):
                    dve.wait_ge(put, g + 1)
                    dve.wait_ge(w_in, 96)
                    dve.wait_ge(scattered, g)
                    nc.vector.tensor_tensor(OS[:], psO[:], spread(b2[:], 1, 2), ALU.add).then_inc(os_done, 1)
                    dve.wait_ge(scattered, g + 1)
                    nc.vector.tensor_tensor(X[:, bass.ds(g * G, G), :], X[:, bass.ds(g * G, G), :], psX[:],
                                            ALU.add).then_inc(x_done, 1)

                pipeline(dve, front, back)

            @block.tensor
            def _(pe):
                def front(g, w):
                    pe.wait_ge(diag_done, g + 1)
                    pe.wait_ge(pick_done, g)
                    nc.tensor.matmul(psR[:, :, 0:L], same[:], diag[:], start=True, stop=True).then_inc(rows_done, 1)

                def back(g, w):
                    pe.wait_ge(pick_done, g + 1)
                    pe.wait_ge(xs_done, g)
                    for k in range(KC):
                        for j in range(G):
                            mm = nc.tensor.matmul(psG[:, k, j * SL:(j + 1) * SL], Z[:, w, j, k * P:(k + 1) * P],
                                                  pick[:, w, j, :], start=True, stop=True)
                    mm.then_inc(gathered, 1)
                    pe.wait_ge(pt_done, g * 2)
                    for jj in range(2):
                        mm = nc.tensor.transpose(psP[:, jj, :], pick[:, w, 2 * jj:2 * jj + 2, :].rearrange(
                            "p j s -> p (j s)"), ident[:])
                    mm.then_inc(turned, 1)
                    pe.wait_ge(xs_done, g + 1)
                    pe.wait_ge(w_in, 96)
                    for f in range(FC // 2):
                        if later(g, 1) or f > 1:
                            pe.wait_ge(gelued, g * FC + 2 * f - 2)
                        for ff in range(2):
                            c = 2 * f + ff
                            for k in range(KC):
                                mm = nc.tensor.matmul(psH[:, f % 2, ff, :], W1[:, k, c * P:(c + 1) * P], XS[:, k, :],
                                                      start=(k == 0), stop=(k == KC - 1))
                        mm.then_inc(hidden, 1)
                    pe.wait_ge(gelued, g * FC + FC)
                    pe.wait_ge(os_done, g)
                    for b in range(2):
                        for c in range(FC):
                            mm = nc.tensor.matmul(psO[:, b, :], H[:, c, b * P:(b + 1) * P], W2[:, c, :],
                                                  start=(c == 0), stop=(c == FC - 1))
                    mm.then_inc(put, 1)
                    pe.wait_ge(os_done, g + 1)
                    pe.wait_ge(pt_done, g * 2 + 2)
                    pe.wait_ge(x_done, g)
                    for j in range(G):
                        mm = nc.tensor.matmul(psX[:, j, :], PT[:, j, :], OS[:, j // 2, :], start=True, stop=True)
                    mm.then_inc(scattered, 1)

                pe.wait_ge(ready, 14)
                pipeline(pe, front, back)

            @block.scalar
            def _(act):
                def back(g, w):
                    act.wait_ge(gathered, g + 1)
                    nc.scalar.copy(XS[:], psG[:]).then_inc(xs_done, 1)
                    act.wait_ge(turned, g + 1)
                    act.wait_ge(scattered, g)
                    nc.scalar.copy(PT[0:SL, 0:G:2, :], psP[0:SL, 0:2, :]).then_inc(pt_done, 1)
                    nc.scalar.copy(PT[SL:P, 1:G:2, :], psP[SL:P, 0:2, :]).then_inc(pt_done, 1)
                    for c in range(FC):
                        act.wait_ge(hidden, g * (FC // 2) + c // 2 + 1)
                        if c == 0:
                            act.wait_ge(put, g)
                        nc.scalar.activation(H[:, c, :], psH[:, (c // 2) % 2, c % 2, :], ACT.Gelu_apprx_tanh,
                                             bias=b1[:, c:c + 1]).then_inc(gelued, 1)

                act.wait_ge(w_in, 96)
                act.wait_ge(ready, 14)
                pipeline(act, lambda g, w: None, back)

HC = NH // KC
NP = NH // 2
VW = DH + 1
BG = 2 * G
HG = G * P // 2

def turn_weights(nc, name, ident, matrices):
    with ExitStack() as ctx:
        s = Scope(nc, ctx, name)
        M = len(matrices)
        W = s.sb("W", [P, M, KC, D])
        psT = s.ps("psT", [P, M, KC, D])
        w_in, turned, taken = (s.sem(x) for x in ("w_in", "turned", "taken"))
        with nc.Block() as block:

            @block.sync
            def _(sp):
                for m, (dram, WT) in enumerate(matrices):
                    sp.dma_start(W[:, m], dram.rearrange("(k p) d -> p k d", p=P)).then_inc(w_in, 16)
                sp.wait_ge(w_in, 16 * M)

            @block.tensor
            def _(pe):
                pe.wait_ge(w_in, 16 * M)
                for m in range(M):
                    for k in range(KC):
                        for c in range(KC):
                            mm = nc.tensor.transpose(psT[:, m, k, c * P:(c + 1) * P], W[:, m, c, k * P:(k + 1) * P],
                                                     ident[:])
                    mm.then_inc(turned, 1)

            @block.scalar
            def _(act):
                for m, (dram, WT) in enumerate(matrices):
                    act.wait_ge(turned, m + 1)
                    nc.scalar.copy(WT[:], psT[:, m]).then_inc(taken, 1)

class Heads:

    def __init__(self, nc, s, ident):
        self.nc, self.ident = nc, ident
        self.KX = s.sb("KX", [P, 2, KC, HC, HG])
        self.VB = s.sb("VB", [P, 2, BG, NP, 2, VW])
        self.QT = s.sb("QT", [P, 2, KC, G * P])
        self.PB = s.sb("PB", [P, 2, NH, L])
        self.PT = s.sb("PT", [P, 2, NP, P])
        self.psS = s.ps("psS", [P, KC, HC * L])
        self.psP = s.ps("psP", [P, 2, NP // 2, P])
        self.psO = s.ps("psO", [P, 512])
        self.set = s.sem("h_set")
        self.kx_in = [s.sem(f"kx_in{w}") for w in range(2)]
        self.scored, self.s_taken, self.weighted, self.turned, self.pt_done, self.valued, self.o_taken = (
            s.sem(x) for x in ("scored", "s_taken", "weighted", "p_turned", "pt_done", "valued", "o_taken"))

    def constants(self, pool):
        gp = self.nc.gpsimd
        gp.memset(self.KX[:], 0.0).then_inc(self.set, 1)
        gp.memset(self.VB[:], 0.0).then_inc(self.set, 1)
        pool.wait_ge(self.set, 2)
        gp.memset(self.VB[0:L, :, :, :, 0, DH:], 1.0).then_inc(self.set, 1)
        gp.memset(self.VB[L:P, :, :, :, 1, DH:], 1.0).then_inc(self.set, 1)
        pool.wait_ge(self.set, 4)

    def expand(self, sp, g, keys, free):
        for half in range(2):
            if free[half] is not None:
                sp.wait_ge(self.scored, free[half])
            for c in range(KC):
                for h in range(HC):
                    rows = slice(h * DH, (h + 1) * DH)
                    sp.dma_start(self.KX[rows, half, c, h, :], keys(rows, c, half)).then_inc(self.kx_in[half], 16)

    def free_after(self, sp, g):
        return [held(sp, g * G - 2) if later(g, 1) else None, held(sp, g * G)]

    def scores(self, pe, g, w, j):
        pe.wait_ge(self.s_taken, g * G + j)
        if j % 2 == 0:
            pe.wait_ge(self.kx_in[j // 2], g * 256 + 256)
        for c in range(KC):
            for b in range(2):
                at, key = (2 * j + b) * L, (2 * (j % 2) + b) * L
                mm = self.nc.tensor.matmul(self.psS[b * L:(b + 1) * L, c, :], self.QT[:, w, c, at:at + L],
                                           self.KX[:, j // 2, c, :, key:key + L], start=True, stop=True,
                                           skip_group_check=True)
        mm.then_inc(self.scored, 1)

    def turn(self, pe, g, j):
        t = g * G + j
        pe.wait_ge(self.weighted, t + 1)
        pe.wait_ge(self.pt_done, t * 2)
        for i in range(NP):
            mm = self.nc.tensor.transpose(self.psP[:, i // (NP // 2), i % (NP // 2), :],
                                          self.PB[:, j % 2, 2 * i:2 * i + 2, :].rearrange("p h t -> p (h t)"),
                                          self.ident[:])
            if i % (NP // 2) == NP // 2 - 1:
                mm.then_inc(self.turned, 1)

    def copy_turned(self, act, g, j):
        t = g * G + j
        for half in range(2):
            act.wait_ge(self.turned, 2 * t + half + 1)
            if later(g, 1) or j > 1:
                act.wait_ge(self.valued, t - 1)
            self.nc.scalar.copy(self.PT[:, j % 2, half * (NP // 2):(half + 1) * (NP // 2), :],
                                self.psP[:, half]).then_inc(self.pt_done, 1)

    def values(self, pe, g, w, j):
        t = g * G + j
        pe.wait_ge(self.pt_done, 2 * t + 2)
        pe.wait_ge(self.o_taken, t)
        for i in range(NP):
            for b in range(2):
                mm = self.nc.tensor.matmul(self.psO[b * L:(b + 1) * L, i * 2 * VW:(i + 1) * 2 * VW],
                                           self.PT[:, j % 2, i, b * L:(b + 1) * L],
                                           self.VB[:, w, 2 * j + b, i].rearrange("p h d -> p (h d)"), start=True,
                                           stop=True, skip_group_check=True)
        mm.then_inc(self.valued, 1)

    def out(self):
        return self.psO[:, 0:NH * VW].rearrange("p (h d) -> p h d", d=VW)

def gated_attention(nc, io, X, CT, ident, identb):
    NG2 = 2 * NH
    with ExitStack() as ctx:
        s = Scope(nc, ctx, "gatt")
        norm = Norm(nc, s, X)
        heads = Heads(nc, s, ident)
        heads.s_taken = heads.weighted
        WZ, WK_, WV_, WC = (s.sb(x, [P, KC, NG2]) for x in ("WZ", "WK", "WV", "WC"))
        gbias = s.sb("gbias", [P, NG2])
        lscale = s.sb("lscale", [P, D])
        same, tri = s.sb("same", [P, P]), s.sb("tri", [P, P])
        own = s.sb("own", [P, L])
        mask = s.sb("mask", [P, HC, L], BF16)
        one = s.sb("one", [P, 1])
        Z = s.sb("Z", [P, G, D])
        CG = s.sb("CG", [P, KC, G * P])
        V2 = s.sb("V2", [P, BG, D])
        gates = s.sb("gates", [P, G, NG2])
        fw = s.sb("fw", [P, 5, G, NH])
        cum = s.sb("cum", [P, 2, G, NH])
        a = s.sb("a", [P, 2, G, NH])
        DA = s.sb("DA", [P, 2, NH, L])
        DB = s.sb("DB", [P, 2, NH, L])
        mx = s.sb("mx", [P, 2, G, NH])
        OG = s.sb("OG", [P, 2, G, NH, VW])
        cen = s.sb("cen", [P, G, NH, DH])
        sq = s.sb("sq", [P, G, NH, DH])
        tw = s.sb("tw", [P, 13, G, NH])
        psA = s.ps("psA", [P, 2, HC * L])
        psG = s.ps("psG", [P, 512])
        (w_in, ready, wc_steps, cg_in, v_in, used, g_used, taken, v_copied, f_steps, f_exp, f_ln, da_done,
         a_spread, maxed, a_taken, d_done, t_steps, e_done, sq_done, v_ln, r_done, scaled, x_done) = (
             s.sem(x) for x in (
                 "w_in", "ready", "wc_steps", "cg_in", "v_in", "used", "g_used", "taken", "v_copied", "f_steps",
                 "f_exp", "f_ln", "da_done", "a_spread", "maxed", "a_taken", "d_done", "t_steps", "e_done",
                 "sq_done", "v_ln", "r_done", "scaled", "x_done"))
        READY = 15
        FPER, TPER = 6, 19
        TAIL_AT = (0, 1, 3)

        with nc.Block() as block:

            @block.sync
            def _(sp):
                with nc.allow_non_contiguous_dma(reason="16 gates for each feature"):
                    for part, W in enumerate((WZ, WK_, WV_)):
                        for n, name in enumerate(("Wi", "Wf")):
                            sp.dma_start(W[:, :, n * NH:(n + 1) * NH],
                                         io["L1_xattn_" + name][part * D:(part + 1) * D, :].rearrange(
                                             "(k p) h -> p k h", p=P)).then_inc(w_in, 16)
                sp.dma_start(gbias[:, 0:NH], spread(io["L1_xattn_bi"], 0, P)).then_inc(w_in, 16)
                sp.dma_start(gbias[:, NH:NG2], spread(io["L1_xattn_bf"], 0, P)).then_inc(w_in, 16)
                sp.dma_start(lscale[:], spread(io["L1_xattn_ln_scale"], 0, P)).then_inc(w_in, 16)
                sp.wait_ge(w_in, 144)
                sp.wait_ge(heads.set, 4)
                c_dram = io["ctx_2048"].rearrange("b t d -> t b d")

                def front(g, w):
                    at, b0, vc = (held(sp, v) for v in (g * (G * P), g * BG, g * 2))
                    free = heads.free_after(sp, g)
                    sp.wait_ge(v_copied, vc)
                    for hp in range(2):
                        sp.dma_start(V2[hp * L:(hp + 1) * L], c_dram[:, bass.ds(b0, BG), :]).then_inc(v_in, 16)
                    sp.wait_ge(g_used, vc)
                    sp.dma_start(CG[:], CT[:, :, bass.ds(at, G * P)]).then_inc(cg_in, 16)
                    starts = [at, held(sp, at + HG)]
                    heads.expand(sp, g, lambda rows, c, half: CT[rows, c, bass.ds(starts[half], HG)], free)

                rounds(sp, lambda g, w: front(g, w) if is_group(g) else None, NG)

            @block.gpsimd
            def _(pool):
                gp = nc.gpsimd
                heads.constants(pool)
                norm.constants(pool)
                step = Steps(pool, ready, READY)
                select = lambda out, op, fill, base, cm, pattern: step(gp.affine_select(
                    out=out, in_=out, compare_op=op, fill=fill, base=base, pattern=pattern, channel_multiplier=cm))
                step(gp.memset(same[:], 1.0))
                select(same[0:L, :], ALU.is_ge, 0.0, L - 1, 0, [[-1, P]])
                select(same[L:P, :], ALU.is_ge, 0.0, -L, 0, [[1, P]])
                step(gp.memset(tri[:], 1.0))
                select(tri[0:L, :], ALU.is_ge, 0.0, L - 1, 0, [[-1, P]])
                select(tri[0:L, :], ALU.is_ge, 0.0, 0, -1, [[1, P]])
                select(tri[L:P, :], ALU.is_ge, 0.0, -L, -1, [[1, P]])
                step(gp.memset(own[:], 0.0))
                select(own[0:L, :], ALU.not_equal, 1.0, 0, 1, [[-1, L]])
                select(own[L:P, :], ALU.not_equal, 1.0, 0, 1, [[-1, L]])
                step(gp.memset(mask[:], 0.0))
                select(mask[0:L], ALU.is_ge, -BIG, 0, 1, [[0, HC], [-1, L]])
                select(mask[L:P], ALU.is_ge, -BIG, 0, 1, [[0, HC], [-1, L]])
                step(gp.memset(one[:], 1.0))
                step(gp.memset(OG[:], 0.0))
                step.end()
                pool.wait_ge(w_in, 144)

                def spread_of(g, w, i):
                    t = g * G + i
                    pool.wait_ge(f_steps, g * FPER + FPER)
                    if later(g, 1) or i > 1:
                        pool.wait_ge(a_spread, t - 1)
                    gp.tensor_tensor(DA[:, i % 2], spread(own[:], 1, NH), spread(a[:, w, i], 2, L),
                                     ALU.mult).then_inc(da_done, 1)

                flat = cen[:].rearrange("p j h d -> p j (h d)")

                def add(g):
                    pool.wait_ge(t_steps, g * TPER + TPER)
                    gp.tensor_tensor(flat, flat, spread(lscale[:], 1, G), ALU.mult).then_inc(scaled, 1)
                    pool.wait_ge(scaled, g + 1)
                    xs = X[:, bass.ds(g * G, G), :]
                    gp.tensor_tensor(xs, xs, flat, ALU.add).then_inc(x_done, 1)

                def step(g, w):
                    if is_group(g - 1):
                        spread_of(g - 1, 1 - w, 2)
                        spread_of(g - 1, 1 - w, 3)
                    if is_group(g + 1):
                        norm.on_pool(pool, g + 1)
                    if is_group(g):
                        spread_of(g, w, 0)
                        spread_of(g, w, 1)
                    if is_group(g - 2):
                        add(g - 2)

                norm.on_pool(pool, 0)
                rounds(pool, step, NG + 1)

            @block.vector
            def _(dve):
                v = nc.vector
                dve.wait_ge(w_in, 144)
                v.tensor_tensor(WC[:], WK_[:], WV_[:], ALU.add).then_inc(wc_steps, 1)
                dve.wait_ge(heads.set, 4)
                dve.wait_ge(ready, READY)

                def front(g, w, i):
                    step = Steps(dve, f_steps, FPER, g)
                    f = gates[:, :, NH:NG2]
                    if i == 1:
                        dve.wait_ge(g_used, g * 2 + 1)
                        step(v.tensor_tensor(gates[:], psG[:, 0:G * NG2].rearrange("p (j n) -> p j n", n=NG2),
                                             spread(gbias[:], 1, G), ALU.add))
                        step(v.scalar_tensor_tensor(fw[:, 0], f, -1.0, f, ALU.mult, ALU.min))
                        step(v.tensor_scalar(fw[:, 3], f, 0.0, None, ALU.min))
                    step.n = 3
                    if i == 3:
                        dve.wait_ge(f_ln, g + 1)
                        step(v.tensor_tensor(fw[:, 4], fw[:, 3], fw[:, 2], ALU.subtract))
                    step.n = 4
                    if i == 4:
                        dve.wait_ge(g_used, g * 2 + 2)
                        step(v.tensor_copy(cum[:, w].rearrange("p j h -> p (j h)"), psG[:, 0:G * NH]))
                        step(v.tensor_tensor(a[:, w], gates[:, :, 0:NH], cum[:, w], ALU.subtract))
                        step.end()

                def max_and_shift(g, w, i):
                    t = g * G + i
                    A = psA[:].rearrange("p c (h t) -> p (c h) t", t=L)
                    dve.wait_ge(a_spread, t + 1)
                    v.tensor_reduce(mx[:, w, i], A, AX.X, ALU.max).then_inc(maxed, 1)
                    dve.wait_ge(maxed, t + 1)
                    v.tensor_tensor(DB[:, i % 2], A, spread(mx[:, w, i], 2, L), ALU.subtract).then_inc(a_taken, 1)

                def weigh(g, i):
                    t = g * G + i
                    p = i % 2
                    dve.wait_ge(heads.scored, t + 1)
                    dve.wait_ge(d_done, t + 1)
                    if later(g, 1) or i > 1:
                        dve.wait_ge(heads.turned, 2 * t - 2)
                    v.scalar_tensor_tensor(heads.PB[:, p], heads.psS[:].rearrange("p c (h t) -> p (c h) t", t=L),
                                           float(DH) ** -0.5, DB[:, p], ALU.mult, ALU.mult).then_inc(
                                               heads.weighted, 1)

                def tail(g, w, part):
                    step = Steps(dve, t_steps, TPER, g)
                    O = OG[:, w, :, :, 0:DH]
                    if part == 0:
                        dve.wait_ge(heads.o_taken, g * G + G)
                        step(v.tensor_tensor(tw[:, 0], mx[:, w], cum[:, w], ALU.add))
                        step(v.tensor_reduce(tw[:, 1], O, AX.X, ALU.add))
                        step(v.tensor_scalar(tw[:, 2], tw[:, 1], 1.0 / DH, None, ALU.mult))
                        dve.wait_ge(x_done, g)
                        step(v.tensor_tensor(cen[:], O, spread(tw[:, 2], 3, DH), ALU.subtract))
                    step.n = 4
                    if part == 1:
                        dve.wait_ge(e_done, g + 1)
                        S = OG[:, w, :, :, DH]
                        step(v.scalar_tensor_tensor(tw[:, 4], S, -1.0, S, ALU.mult, ALU.max))
                        step(v.tensor_tensor(tw[:, 5], tw[:, 4], tw[:, 3], ALU.max))
                        step(v.tensor_scalar(tw[:, 6], tw[:, 5], 1e-6, None, ALU.add))
                        step(v.reciprocal(tw[:, 7], tw[:, 6]))
                        step(v.tensor_tensor(tw[:, 10], tw[:, 7], tw[:, 7], ALU.mult))
                        dve.wait_ge(sq_done, g + 1)
                        step(v.tensor_reduce(tw[:, 11], sq[:], AX.X, ALU.add))
                        step(v.tensor_tensor(tw[:, 12], tw[:, 10], tw[:, 11], ALU.mult))
                        step(v.tensor_scalar(tw[:, 1], tw[:, 12], 1.0 / DH, None, ALU.mult))
                        step(v.tensor_scalar(tw[:, 8], tw[:, 1], 1e-6, None, ALU.add))
                    step.n = 13
                    if part == 2:
                        dve.wait_ge(r_done, g + 1)
                        step(v.tensor_tensor(tw[:, 4], tw[:, 9], tw[:, 9], ALU.mult))
                        step(v.tensor_tensor(tw[:, 5], tw[:, 4], tw[:, 8], ALU.mult))
                        step(v.tensor_scalar(tw[:, 6], tw[:, 5], -0.5, 1.5, ALU.mult, ALU.add))
                        step(v.tensor_tensor(tw[:, 11], tw[:, 6], tw[:, 9], ALU.mult))
                        step(v.tensor_tensor(tw[:, 10], tw[:, 11], tw[:, 7], ALU.mult))
                        step(v.tensor_tensor(cen[:], cen[:], spread(tw[:, 10], 3, DH), ALU.mult))
                        step.end()

                def step(g, w):
                    for i in range(G + 2):
                        if is_group(g - 1) and i < G:
                            max_and_shift(g - 1, 1 - w, i)
                        if is_group(g) and i in (1, 3, 4):
                            front(g, w, i)
                        if is_group(g - 1) and 1 <= i <= G:
                            weigh(g - 1, i - 1)
                        if is_group(g - 2) and i in TAIL_AT:
                            tail(g - 2, w, TAIL_AT.index(i))
                        if is_group(g + 1) and i == 3:
                            norm.take_stats(dve, g + 1)
                        if is_group(g + 1) and i == 4:
                            dve.wait_ge(used, g * 2 + 2)
                            norm.normalise(dve, g + 1, Z)

                norm.on_vector(dve, 0, Z)
                rounds(dve, step, NG + 1)

            @block.tensor
            def _(pe):
                pe.wait_ge(heads.set, 4)
                pe.wait_ge(ready, READY)
                pe.wait_ge(w_in, 144)
                pe.wait_ge(wc_steps, 1)

                def z_turned(g):
                    pe.wait_ge(norm.normed, g * G + G)
                    pe.wait_ge(f_steps, g * FPER)
                    for k in range(KC):
                        pe.wait_ge(taken, g * 2 + k)
                        for j in range(G):
                            mm = nc.tensor.transpose(psG[:, j * P:(j + 1) * P], Z[:, j, k * P:(k + 1) * P], ident[:])
                        mm.then_inc(used, 1)

                def gates_of(g, w):
                    pe.wait_ge(taken, g * 2 + 2)
                    pe.wait_ge(cg_in, g * 16 + 16)
                    for j in range(G):
                        tile = slice(j * P, (j + 1) * P)
                        for n, (src, W) in enumerate([(heads.QT[:, w, k, tile], WZ[:, k, :]) for k in range(KC)]
                                                     + [(CG[:, k, tile], WC[:, k, :]) for k in range(KC)]):
                            mm = nc.tensor.matmul(psG[:, j * NG2:(j + 1) * NG2], src, W, start=(n == 0),
                                                  stop=(n == 2 * KC - 1))
                    mm.then_inc(g_used, 1)

                def running_sums(g):
                    pe.wait_ge(f_steps, g * FPER + 4)
                    nc.tensor.matmul(psG[:, 0:G * NH], tri[:], fw[:, 4].rearrange("p j h -> p (j h)"), start=True,
                                     stop=True).then_inc(g_used, 1)

                def spread_a(g, i):
                    t = g * G + i
                    pe.wait_ge(da_done, t + 1)
                    pe.wait_ge(a_taken, t)
                    for half in range(2):
                        nc.tensor.matmul(psA[:, half, :], same[:],
                                         DA[:, i % 2, half * HC:(half + 1) * HC, :].rearrange("p h t -> p (h t)"),
                                         start=True, stop=False)
                        mm = nc.tensor.matmul(psA[:, half, :], identb[:], mask[:].rearrange("p h t -> p (h t)"),
                                              start=False, stop=True)
                    mm.then_inc(a_spread, 1)

                def step(g, w):
                    bg, bw = g - 1, 1 - w
                    for i in range(G + 2):
                        if is_group(bg) and i >= 2:
                            heads.turn(pe, bg, i - 2)
                        if is_group(bg) and i < G:
                            spread_a(bg, i)
                        if is_group(g) and i == 0:
                            z_turned(g)
                        if is_group(g) and i == 1:
                            gates_of(g, w)
                        if is_group(g) and i == 4:
                            running_sums(g)
                        if is_group(bg) and 1 <= i <= G:
                            heads.scores(pe, bg, bw, i - 1)
                        if is_group(bg) and i >= 2:
                            if i == 2:
                                pe.wait_ge(v_copied, bg * 2 + 2)
                            heads.values(pe, bg, bw, i - 2)

                rounds(pe, step, NG + 1)

            @block.scalar
            def _(act):
                sc = nc.scalar
                act.wait_ge(ready, READY)
                act.wait_ge(heads.set, 4)

                def queries(g, w):
                    if later(g, 2):
                        act.wait_ge(heads.scored, g * G - G)
                    for k in range(KC):
                        act.wait_ge(used, g * 2 + k + 1)
                        sc.copy(heads.QT[:, w, k, :], psG[:]).then_inc(taken, 1)

                def place_values(g, w):
                    act.wait_ge(v_in, g * 32 + 32)
                    if later(g, 2):
                        act.wait_ge(heads.valued, g * G - G)
                    for hp in range(2):
                        rows = slice(hp * L, (hp + 1) * L)
                        sc.copy(heads.VB[rows, w, :, :, hp, 0:DH],
                                V2[rows].rearrange("p b (i h d) -> p b i h d", h=2, d=DH)[:, :, :, hp, :]).then_inc(
                                    v_copied, 1)

                def softplus(g):
                    act.wait_ge(f_steps, g * FPER + 2)
                    sc.activation(fw[:, 1], fw[:, 0], ACT.Exp).then_inc(f_exp, 1)

                def logarithms(g):
                    if is_group(g):
                        act.wait_ge(f_exp, g + 1)
                        sc.activation(fw[:, 2], fw[:, 1], ACT.Ln, bias=one[:, 0:1]).then_inc(f_ln, 1)
                    if is_group(g - 2):
                        act.wait_ge(t_steps, (g - 2) * TPER + 13)
                        sc.activation(tw[:, 12], tw[:, 8], ACT.Ln).then_inc(v_ln, 1)
                        act.wait_ge(v_ln, g - 1)
                        sc.activation(tw[:, 9], tw[:, 12], ACT.Exp, scale=-0.5).then_inc(r_done, 1)

                def step(g, w):
                    bg, bw = g - 1, 1 - w
                    for i in range(G + 2):
                        if is_group(bg) and i >= 2:
                            heads.copy_turned(act, bg, i - 2)
                        if is_group(bg) and i < G:
                            act.wait_ge(a_taken, bg * G + i + 1)
                            sc.activation(DB[:, i % 2], DB[:, i % 2], ACT.Exp).then_inc(d_done, 1)
                        if is_group(g) and i == 0:
                            queries(g, w)
                        if is_group(g) and i == 1:
                            softplus(g)
                        if is_group(bg) and i >= 2:
                            act.wait_ge(heads.valued, bg * G + i - 1)
                            sc.copy(OG[:, bw, i - 2], heads.out()).then_inc(heads.o_taken, 1)
                        if is_group(g - 2) and i == TAIL_AT[0]:
                            act.wait_ge(t_steps, (g - 2) * TPER + 1)
                            sc.activation(tw[:, 3], tw[:, 0], ACT.Exp, scale=-1.0).then_inc(e_done, 1)
                            act.wait_ge(t_steps, (g - 2) * TPER + 4)
                            sc.activation(sq[:], cen[:], ACT.Square).then_inc(sq_done, 1)
                        if i == 2:
                            logarithms(g)
                        if is_group(g) and i == 4:
                            place_values(g, w)

                rounds(act, step, NG + 1)

def ternary(nc, name, identb, matrices):
    NB = 8
    with ExitStack() as ctx:
        s = Scope(nc, ctx, name)
        M = len(matrices)
        W = s.sb("W", [P, M, FF * D // P])
        R = s.sb("R", [P, M, FF * D // P], BF16)
        ones = s.sb("ones", [P, P])
        rowsum = s.sb("rowsum", [P, M])
        inv = s.sb("inv", [P, M])
        psum = s.ps("psum", [P, M])
        psT = s.ps("psT", [P, 2, NB, P], BF16)
        w_in, set_, steps, summed, totalled, ternary_done, turned, taken = (
            s.sem(x) for x in ("w_in", "set", "steps", "summed", "totalled", "ternary", "turned", "taken"))
        with nc.Block() as block:

            @block.sync
            def _(sp):
                for m, (dram, WT, scale) in enumerate(matrices):
                    I = dram.shape[1]
                    sp.dma_start(W[:, m].rearrange("p (c i) -> p c i", i=I),
                                 dram.rearrange("(c p) i -> p c i", p=P)).then_inc(w_in, 16)
                    sp.wait_ge(w_in, 16 * m + 16)

            @block.gpsimd
            def _(pool):
                nc.gpsimd.memset(ones[:], 1.0).then_inc(set_, 1)

            @block.vector
            def _(dve):
                step = Steps(dve, steps, 4 * M)
                for m, (dram, WT, scale) in enumerate(matrices):
                    dve.wait_ge(w_in, 16 * m + 16)
                    nc.vector.tensor_reduce(rowsum[:, m:m + 1], W[:, m], AX.X, ALU.add,
                                            apply_absolute_value=True).then_inc(summed, 1)
                for m, (dram, WT, scale) in enumerate(matrices):
                    dve.wait_ge(totalled, m + 1)
                    if m == 0:
                        dve.wait_ge(totalled, M)
                    step(nc.vector.tensor_scalar(scale[:, 0:1], psum[:, m:m + 1], 1.0 / (FF * D), 1e-5, ALU.mult,
                                                 ALU.max))
                    step(nc.vector.reciprocal(inv[:, m:m + 1], scale[:, 0:1]))
                    step(nc.vector.tensor_scalar(W[:, m], W[:, m], inv[:, m:m + 1], MAGIC, ALU.mult, ALU.add))
                    step(nc.vector.tensor_scalar(W[:, m], W[:, m], MAGIC, 1.0, ALU.subtract, ALU.min))
                    nc.vector.tensor_scalar(R[:, m], W[:, m], -1.0, None, ALU.max).then_inc(ternary_done, 1)
                step.end()

            @block.tensor
            def _(pe):
                pe.wait_ge(set_, 1)
                for m in range(M):
                    pe.wait_ge(summed, m + 1)
                    nc.tensor.matmul(psum[:, m:m + 1], ones[:], rowsum[:, m:m + 1], start=True,
                                     stop=True).then_inc(totalled, 1)
                for m, (dram, WT, scale) in enumerate(matrices):
                    O, I = dram.shape
                    pe.wait_ge(ternary_done, m + 1)
                    blocks = [(k, c) for k in range(I // P) for c in range(O // P)]
                    for half in range(2):
                        if m > 0:
                            pe.wait_ge(taken, 2 * m - 1 + half)
                        for n, (k, c) in enumerate(blocks[half * NB:half * NB + NB]):
                            mm = nc.tensor.transpose(psT[:, half, n, :], R[:, m, c * I + k * P:c * I + (k + 1) * P],
                                                     identb[:])
                        mm.then_inc(turned, 1)

            @block.scalar
            def _(act):
                for m, (dram, WT, scale) in enumerate(matrices):
                    flat = WT[:].rearrange("p k o -> p (k o)")
                    for half in range(2):
                        act.wait_ge(turned, 2 * m + half + 1)
                        nc.scalar.copy(flat[:, half * NB * P:(half + 1) * NB * P],
                                       psT[:, half].rearrange("p n q -> p (n q)")).then_inc(taken, 1)

class Rounded:

    def __init__(self, nc, s, X, ident, rms_eps, floor):
        self.nc, self.ident, self.rms_eps, self.floor = nc, ident, rms_eps, floor
        self.norm = Norm(nc, s, X)
        self.Z = s.sb("Z", [P, G, D])
        self.ZM = s.sb("ZM", [P, G, D])
        self.QT = s.sb("QT", [P, 2, KC, G * P], BF16)
        self.amax = s.sb("amax", [P, G])
        self.am = s.sb("am", [P, G])
        self.unit = s.sb("unit", [P, 2, G])
        self.inv = s.sb("inv", [P, G])
        self.qs = s.sb("qs", [P, G])
        self.u = s.sb("u", [P, 3, G])
        self.r = s.sb("r", [P, G])
        self.rms_e = s.sb("rms_e", [P, G])
        self.neg = s.sb("neg", [P, 1])
        self.psT = s.ps("psT", [P, KC, G * P])
        self.steps, self.rounded, self.turned, self.qt_done = (
            s.sem(x) for x in ("q_steps", "rounded", "q_turned", "qt_done"))
        self.set, self.rms_steps, self.r_done = s.sem("q_set"), s.sem("rms_steps"), s.sem("r_done")
        self.PER = 5 if rms_eps else 3

    def constants(self, pool):
        self.nc.gpsimd.memset(self.neg[:], -MAGIC).then_inc(self.set, 1)
        self.nc.gpsimd.memset(self.rms_e[:], self.rms_eps or 0.0).then_inc(self.set, 1)
        pool.wait_ge(self.set, 2)
        self.norm.constants(pool)

    def on_pool(self, pool, g):
        self.norm.on_pool(pool, g)
        if self.rms_eps:
            gp, n = self.nc.gpsimd, self.norm
            step = Steps(pool, self.rms_steps, 3, g)
            pool.wait_ge(n.rstd_done, g + 1)
            step(gp.tensor_tensor(self.u[:, 0], n.mv[:, :, 1], n.rstd[:], ALU.mult))
            step(gp.tensor_tensor(self.u[:, 1], self.u[:, 0], n.rstd[:], ALU.mult))
            step(gp.tensor_tensor(self.u[:, 2], self.u[:, 1], self.rms_e[:], ALU.add))
            gp.tensor_tensor(self.r[:], self.u[:, 2], n.mhalf[:], ALU.pow).then_inc(self.r_done, 1)
            step.end()

    def on_vector(self, dve, g, w):
        v, Z = self.nc.vector, self.Z
        self.norm.on_vector(dve, g, Z)
        step = Steps(dve, self.steps, self.PER, g)
        dve.wait_ge(self.norm.normed, g * G + G)
        step(v.tensor_reduce(self.amax[:], Z[:], AX.X, ALU.max, apply_absolute_value=True))
        am, qs = self.amax, self.inv
        if self.rms_eps:
            dve.wait_ge(self.r_done, g + 1)
            step(v.tensor_tensor(self.am[:], self.amax[:], self.r[:], ALU.mult))
            am, qs = self.am, self.qs
        step(v.tensor_scalar(self.unit[:, w], am[:], self.floor, 1.0 / 127.0, ALU.max, ALU.mult))
        step(v.reciprocal(self.inv[:], self.unit[:, w]))
        if self.rms_eps:
            step(v.tensor_tensor(self.qs[:], self.inv[:], self.r[:], ALU.mult))
        step.end()
        dve.wait_ge(self.turned, g * KC)
        for j in range(G):
            v.tensor_scalar(self.ZM[:, j, :], Z[:, j, :], qs[:, j:j + 1], MAGIC, ALU.mult,
                            ALU.add).then_inc(self.rounded, 1)

    def on_tensor(self, pe, g):
        pe.wait_ge(self.rounded, g * G + G)
        pe.wait_ge(self.qt_done, g * KC)
        for k in range(KC):
            for j in range(G):
                mm = self.nc.tensor.transpose(self.psT[:, k, j * P:(j + 1) * P], self.ZM[:, j, k * P:(k + 1) * P],
                                              self.ident[:])
            mm.then_inc(self.turned, 1)

    def on_scalar(self, act, g, w):
        for k in range(KC):
            act.wait_ge(self.turned, g * KC + k + 1)
            self.nc.scalar.activation(self.QT[:, w, k, :], self.psT[:, k, :], ACT.Identity,
                                      bias=self.neg[:, 0:1]).then_inc(self.qt_done, 1)

class Down:

    def __init__(self, nc, s, X, identb, W2, w2_unit, eps):
        self.nc, self.X, self.identb, self.W2, self.w2_unit, self.eps = nc, X, identb, W2, w2_unit, eps
        self.square = s.sb("square", [P, 2, FF], BF16)
        self.ms = s.sb("ms", [P, 2, G])
        self.me = s.sb("me", [P, G])
        self.r = s.sb("d_r", [P, G])
        self.mhalf = s.sb("d_mhalf", [P, G])
        self.amax = s.sb("d_amax", [P, 2, G])
        self.am = s.sb("d_am", [P, G])
        self.unit = s.sb("d_unit", [P, G])
        self.inv = s.sb("d_inv", [P, G])
        self.qs = s.sb("d_qs", [P, G])
        self.uw = s.sb("d_uw", [P, G])
        self.magic = s.sb("magic", [P, 1])
        self.HM = s.sb("HM", [P, 2, FF])
        self.HB = s.sb("HB", [P, 2, FF], BF16)
        self.HT = s.sb("HT", [P, 2, FF // P, P], BF16)
        self.psV = s.ps("psV", [P, FF // P, P], BF16)
        self.psO = s.ps("psO", [P, D])
        self.set = s.sem("d_set")
        (self.squared, self.maxed, self.steps, self.r_done, self.hm_done, self.hb_done, self.turned, self.ht_done,
         self.out, self.x_done) = (s.sem(x) for x in (
             "squared", "d_maxed", "d_steps", "d_r_done", "hm_done", "hb_done", "d_turned", "ht_done", "out",
             "x_done"))

    def constants(self, pool):
        self.nc.gpsimd.memset(self.magic[:], MAGIC).then_inc(self.set, 1)
        self.nc.gpsimd.memset(self.mhalf[:], -0.5).then_inc(self.set, 1)
        pool.wait_ge(self.set, 2)

    def power(self, pool, g):
        pool.wait_ge(self.steps, g * 6 + 1)
        self.nc.gpsimd.tensor_tensor(self.r[:], self.me[:], self.mhalf[:], ALU.pow).then_inc(self.r_done, 1)

    def squares(self, act, g, w, j, Hj):
        if later(g, 1) or j > 1:
            act.wait_ge(self.squared, g * G + j - 1)
        if j == 0 and later(g, 2):
            act.wait_ge(self.steps, g * 6 - 6)
        self.nc.scalar.activation(self.square[:, j % 2], Hj, ACT.Square,
                                  accum_out=self.ms[:, w, j:j + 1]).then_inc(self.squared, 1)

    def maximum(self, w, j, Hj):
        self.nc.vector.tensor_reduce(self.amax[:, w, j:j + 1], Hj, AX.X, ALU.max,
                                     apply_absolute_value=True).then_inc(self.maxed, 1)

    def scales(self, dve, g, w):
        v = self.nc.vector
        step = Steps(dve, self.steps, 6, g)
        dve.wait_ge(self.squared, g * G + G)
        step(v.tensor_scalar(self.me[:], self.ms[:, w], 1.0 / FF, self.eps, ALU.mult, ALU.add))
        dve.wait_ge(self.r_done, g + 1)
        dve.wait_ge(self.maxed, g * G + G)
        step(v.tensor_tensor(self.am[:], self.amax[:, w], self.r[:], ALU.mult))
        step(v.tensor_scalar(self.unit[:], self.am[:], 1e-5, 1.0 / 127.0, ALU.max, ALU.mult))
        step(v.reciprocal(self.inv[:], self.unit[:]))
        dve.wait_ge(self.hm_done, g * G)
        step(v.tensor_tensor(self.qs[:], self.inv[:], self.r[:], ALU.mult))
        step(v.tensor_scalar(self.uw[:], self.unit[:], self.w2_unit[:, 0:1], None, ALU.mult))
        step.end()

    def scale_and_round(self, act, g, j, Hj):
        if j == 0:
            act.wait_ge(self.steps, g * 6 + 6)
        if later(g, 1) or j > 1:
            act.wait_ge(self.hb_done, g * G + j - 1)
        self.nc.scalar.activation(self.HM[:, j % 2], Hj, ACT.Identity, bias=self.magic[:, 0:1],
                                  scale=self.qs[:, j:j + 1]).then_inc(self.hm_done, 1)

    def integers(self, dve, g, j):
        dve.wait_ge(self.hm_done, g * G + j + 1)
        if later(g, 1) or j > 1:
            dve.wait_ge(self.turned, g * G + j - 1)
        self.nc.vector.tensor_scalar(self.HB[:, j % 2], self.HM[:, j % 2], MAGIC, None, ALU.subtract).then_inc(
            self.hb_done, 1)

    def turn(self, pe, g, j):
        t = g * G + j
        pe.wait_ge(self.hb_done, t + 1)
        pe.wait_ge(self.ht_done, t)
        for c in range(FF // P):
            mm = self.nc.tensor.transpose(self.psV[:, c, :], self.HB[:, j % 2, c * P:(c + 1) * P], self.identb[:])
        mm.then_inc(self.turned, 1)

    def copy_turned(self, act, g, j):
        t = g * G + j
        act.wait_ge(self.turned, t + 1)
        if later(g, 1) or j > 1:
            act.wait_ge(self.out, t - 1)
        self.nc.scalar.copy(self.HT[:, j % 2], self.psV[:]).then_inc(self.ht_done, 1)

    def product(self, pe, g, j):
        t = g * G + j
        pe.wait_ge(self.ht_done, t + 1)
        pe.wait_ge(self.x_done, t)
        for c in range(FF // P):
            mm = self.nc.tensor.matmul(self.psO[:], self.HT[:, j % 2, c, :], self.W2[:, c, :], start=(c == 0),
                                       stop=(c == FF // P - 1))
        mm.then_inc(self.out, 1)

    def add(self, dve, g, j):
        t = g * G + j
        x = self.X[:, t, :]
        dve.wait_ge(self.out, t + 1)
        self.nc.vector.scalar_tensor_tensor(x, self.psO[:], self.uw[:, j:j + 1], x, ALU.mult, ALU.add).then_inc(
            self.x_done, 1)

def interleave(engine, both):
    both(0, 0, True, False)
    both(1, 1, True, True)
    with engine.Fori(1, NG // 2) as h:
        both(h * 2, 0, True, True)
        both(h * 2 + 1, 1, True, True)
    both(NG, 0, False, True)

HALF = FF // 2

def normed_ffn(nc, io, X, ident, identb):
    with ExitStack() as ctx:
        s = Scope(nc, ctx, "nffn")
        W1 = s.sb("W1", [P, KC, FF], BF16)
        W2 = s.sb("W2", [P, FF // P, D], BF16)
        u1, u2 = s.sb("u1", [P, 1]), s.sb("u2", [P, 1])
        ternary(nc, "nffn_weights", identb, [(io["L1_ffn_w1"], W1, u1), (io["L1_ffn_w2"], W2, u2)])
        b1, gam, bet, b2 = s.sb("b1", [P, FF]), s.sb("gam", [P, FF]), s.sb("bet", [P, FF]), s.sb("b2", [P, D])
        H = s.sb("H", [P, 2, G, FF])
        q = Rounded(nc, s, X, ident, 1e-5, 1e-5)
        down = Down(nc, s, X, identb, W2, u2, 1e-5)
        uw = s.sb("uw", [P, G])
        stats = s.sb("stats2", [P, G, 2, 6])
        mv = s.sb("mv2", [P, G, 2])
        rstd = s.sb("rstd2", [P, G])
        veps = s.sb("veps2", [P, G])
        psH = s.ps("psH", [P, 2, HALF])
        (b_in, uw_done, up, affined, silued, gelued, agg, veps_done, rstd_done, normed, gained, shifted, b2_added) = (
            s.sem(x) for x in ("b_in", "uw_done", "up", "affined", "silued", "gelued", "agg2", "veps2_done",
                               "rstd2_done", "normed2", "gained", "shifted", "b2_added"))

        with nc.Block() as block:

            @block.sync
            def _(sp):
                for tile, name in ((b1, "b1"), (gam, "ln_g"), (bet, "ln_b"), (b2, "b2")):
                    sp.dma_start(tile[:], spread(io["L1_ffn_" + name], 0, P)).then_inc(b_in, 16)
                sp.wait_ge(b_in, 64)

            @block.gpsimd
            def _(pool):
                q.constants(pool)
                down.constants(pool)
                pool.wait_ge(b_in, 64)

                def both(g, w, front, back):
                    if front:
                        q.on_pool(pool, g)
                    if back:
                        g, w = g - 1, 1 - w
                        pool.wait_ge(agg, g * G + G)
                        nc.gpsimd.tensor_tensor(veps[:], mv[:, :, 1], q.norm.eps[:], ALU.add).then_inc(veps_done, 1)
                        pool.wait_ge(veps_done, g + 1)
                        nc.gpsimd.tensor_tensor(rstd[:], veps[:], q.norm.mhalf[:], ALU.pow).then_inc(rstd_done, 1)
                        for j in range(G):
                            pool.wait_ge(normed, g * G + j + 1)
                            nc.gpsimd.tensor_tensor(H[:, w, j], H[:, w, j], gam[:], ALU.mult).then_inc(gained, 1)
                        down.power(pool, g)
                        pool.wait_ge(down.x_done, g * G + G)
                        xs = X[:, bass.ds(g * G, G), :]
                        nc.gpsimd.tensor_tensor(xs, xs, spread(b2[:], 1, G), ALU.add).then_inc(b2_added, 1)

                interleave(pool, both)

            @block.vector
            def _(dve):
                v = nc.vector
                dve.wait_ge(b_in, 64)

                def both(g, w, front, back):
                    if front:
                        q.on_vector(dve, g, w)
                        v.tensor_scalar(uw[:], q.unit[:, w], u1[:, 0:1], None, ALU.mult).then_inc(uw_done, 1)
                    b, bw = g - 1, 1 - w
                    if back:
                        dve.wait_ge(gelued, b + 1)
                        for j in range(G):
                            for h in range(2):
                                v.bn_stats(stats[:, j, h, :], H[:, bw, j, h * HALF:(h + 1) * HALF])
                        dve.drain()
                        for j in range(G):
                            v.bn_aggr(mv[:, j, :], stats[:, j].rearrange("p h s -> p (h s)")).then_inc(agg, 1)
                        dve.wait_ge(rstd_done, b + 1)
                        dve.wait_ge(agg, b * G + G)
                        for j in range(G):
                            v.tensor_scalar(H[:, bw, j], H[:, bw, j], mv[:, j, 0:1], rstd[:, j:j + 1],
                                            ALU.subtract, ALU.mult).then_inc(normed, 1)
                    if front:
                        dve.wait_ge(uw_done, g + 1)
                    for j in range(G):
                        if front:
                            for h in range(2):
                                half = slice(h * HALF, (h + 1) * HALF)
                                dve.wait_ge(up, (g * G + j) * 2 + h + 1)
                                v.scalar_tensor_tensor(H[:, w, j, half], psH[:, h, :], uw[:, j:j + 1], b1[:, half],
                                                       ALU.mult, ALU.add).then_inc(affined, 1)
                        if back:
                            dve.wait_ge(gained, b * G + j + 1)
                            v.tensor_tensor(H[:, bw, j], H[:, bw, j], bet[:], ALU.add).then_inc(shifted, 1)
                            dve.wait_ge(shifted, b * G + j + 1)
                            down.maximum(bw, j, H[:, bw, j])
                    if back:
                        down.scales(dve, b, bw)
                        for j in range(G):
                            down.integers(dve, b, j)
                            if j > 0:
                                down.add(dve, b, j - 1)
                        down.add(dve, b, G - 1)

                interleave(dve, both)

            @block.tensor
            def _(pe):
                def both(g, w, front, back):
                    if front:
                        q.on_tensor(pe, g)
                        pe.wait_ge(q.qt_done, g * KC + KC)
                        for j in range(G):
                            for h in range(2):
                                if later(g, 1) or j > 0:
                                    pe.wait_ge(affined, (g * G + j) * 2 + h - 1)
                                for k in range(KC):
                                    mm = nc.tensor.matmul(psH[:, h, :], q.QT[:, w, k, j * P:(j + 1) * P],
                                                          W1[:, k, h * HALF:(h + 1) * HALF], start=(k == 0),
                                                          stop=(k == KC - 1))
                                mm.then_inc(up, 1)
                    if back:
                        down.turn(pe, g - 1, 0)
                        for j in range(G):
                            down.product(pe, g - 1, j)
                            if j + 1 < G:
                                down.turn(pe, g - 1, j + 1)

                interleave(pe, both)

            @block.scalar
            def _(act):
                def both(g, w, front, back):
                    if front:
                        q.on_scalar(act, g, w)
                    b, bw = g - 1, 1 - w
                    for j in range(G):
                        if front:
                            act.wait_ge(affined, (g * G + j) * 2 + 2)
                            nc.scalar.activation(H[:, w, j], H[:, w, j], ACT.Silu).then_inc(silued, 1)
                        if back:
                            act.wait_ge(shifted, b * G + j + 1)
                            down.squares(act, b, bw, j, H[:, bw, j])
                    if back:
                        for j in range(G):
                            down.scale_and_round(act, b, j, H[:, bw, j])
                            if j > 0:
                                down.copy_turned(act, b, j - 1)
                        down.copy_turned(act, b, G - 1)
                    if front:
                        act.wait_ge(silued, g * G + G)
                        nc.scalar.activation(H[:, w], H[:, w], ACT.Gelu).then_inc(gelued, 1)

                interleave(act, both)

def softmax_attention(nc, io, X, CT, ident):
    V_AT = [[], [], [], [0, 1, 2], [3, 4, 5], [6, 7]]
    with ExitStack() as ctx:
        s = Scope(nc, ctx, "satt")
        WQ, WK, WV, WO = (s.sb(x, [P, KC, D]) for x in ("WQ", "WK", "WV", "WO"))
        turn_weights(nc, "satt_wqk", ident, [(io["L2_xattn_Wq"], WQ), (io["L2_xattn_Wk"], WK)])
        turn_weights(nc, "satt_wvo", ident, [(io["L2_xattn_Wv"], WV), (io["L2_xattn_Wo"], WO)])
        norm = Norm(nc, s, X)
        heads = Heads(nc, s, ident)
        bq, bk = s.sb("bq", [P, KC]), s.sb("bk", [P, KC])
        bv, bo = s.sb("bv", [P, D]), s.sb("bo", [P, D])
        Z = s.sb("Z", [P, G, D])
        ZT = s.sb("ZT", [P, KC, G * P])
        KT = s.sb("KT", [P, KC, G * P])
        CG = s.sb("CG", [P, KC, G * P])
        mx = s.sb("mx", [P, 2, NH])
        rs = s.sb("rs", [P, 2, NH])
        AO = s.sb("AO", [P, 2, NH, DH])
        AT = s.sb("AT", [P, 2, KC, P])
        psG = s.ps("psG", [P, 2, 512])
        psF = s.ps("psF", [P, 512])
        (b_in, c_in, used, taken, v_used, v_taken, maxed, subbed, inverted, ao_done, ao_turned, at_done, projected,
         x_done, bo_added) = (s.sem(x) for x in (
             "b_in", "c_in", "used", "taken", "v_used", "v_taken", "maxed", "subbed", "inverted", "ao_done",
             "ao_turned", "at_done", "projected", "x_done", "bo_added"))

        with nc.Block() as block:

            @block.sync
            def _(sp):
                with nc.allow_non_contiguous_dma(reason="one column of biases for each chunk"):
                    sp.dma_start(bq[:], io["L2_xattn_bq"].rearrange("(k p) -> p k", p=P)).then_inc(b_in, 16)
                    sp.dma_start(bk[:], io["L2_xattn_bk"].rearrange("(k p) -> p k", p=P)).then_inc(b_in, 16)
                sp.dma_start(bv[:], spread(io["L2_xattn_bv"], 0, P)).then_inc(b_in, 16)
                sp.dma_start(bo[:], spread(io["L2_xattn_bo"], 0, P)).then_inc(b_in, 16)
                sp.wait_ge(b_in, 64)
                sp.wait_ge(heads.set, 4)

                def front(g, w):
                    at, vs, ks = (held(sp, v) for v in (g * (G * P), g * BG, g * 6 + 6))
                    free = heads.free_after(sp, g)
                    sp.wait_ge(v_used, vs)
                    sp.dma_start(CG[:], CT[:, :, bass.ds(at, G * P)]).then_inc(c_in, 16)
                    sp.wait_ge(taken, ks)
                    heads.expand(sp, g, lambda rows, c, half: KT[rows, c, half * HG:(half + 1) * HG], free)

                rounds(sp, lambda g, w: front(g, w) if is_group(g) else None, NG)

            @block.gpsimd
            def _(pool):
                heads.constants(pool)
                norm.constants(pool)
                pool.wait_ge(b_in, 64)

                def back(g, w):
                    pool.wait_ge(x_done, g * G + G)
                    xs = X[:, bass.ds(g * G, G), :]
                    nc.gpsimd.tensor_tensor(xs, xs, spread(bo[:], 1, G), ALU.add).then_inc(bo_added, 1)

                def step(g, w):
                    if is_group(g + 1):
                        norm.on_pool(pool, g + 1)
                    if is_group(g - 1):
                        back(g - 1, 1 - w)

                norm.on_pool(pool, 0)
                rounds(pool, step, NG)

            @block.vector
            def _(dve):
                v = nc.vector
                dve.wait_ge(heads.set, 4)
                dve.wait_ge(b_in, 64)

                def values_of(g, w, b):
                    dve.wait_ge(v_used, g * BG + b + 1)
                    if b == 0 and later(g, 2):
                        dve.wait_ge(heads.valued, g * G - G)
                    for hp in range(2):
                        rows = slice(hp * L, (hp + 1) * L)
                        take = lambda x: x.rearrange("p (i h d) -> p i h d", h=2, d=DH)[:, :, hp, :]
                        v.tensor_tensor(heads.VB[rows, w, b, :, hp, 0:DH], take(psG[rows, b % 2, 0:D]),
                                        take(bv[rows, :]), ALU.add).then_inc(v_taken, 1)

                def step(g, w):
                    bg = g - 1
                    for i in range(G + 2):
                        if is_group(bg) and i < G:
                            t = bg * G + i
                            p = i % 2
                            S = heads.psS[:].rearrange("p c (h t) -> p (c h) t", t=L)
                            dve.wait_ge(heads.scored, t + 1)
                            v.tensor_reduce(mx[:, p], S, AX.X, ALU.max).then_inc(maxed, 1)
                            if later(bg, 1) or i > 1:
                                dve.wait_ge(heads.turned, 2 * t - 2)
                            dve.wait_ge(maxed, t + 1)
                            v.tensor_tensor(heads.PB[:, p], S, spread(mx[:, p], 2, L), ALU.subtract).then_inc(
                                heads.s_taken, 1)
                        if is_group(g):
                            for b in V_AT[i]:
                                values_of(g, w, b)
                        if is_group(bg) and 1 <= i <= G:
                            t = bg * G + i - 1
                            p = (i - 1) % 2
                            dve.wait_ge(heads.valued, t + 1)
                            v.reciprocal(rs[:, p], heads.out()[:, :, DH]).then_inc(inverted, 1)
                            dve.wait_ge(inverted, t + 1)
                            if later(bg, 1) or i > 2:
                                dve.wait_ge(ao_turned, t - 1)
                            v.tensor_tensor(AO[:, p], heads.out()[:, :, 0:DH], spread(rs[:, p], 2, DH),
                                            ALU.mult).then_inc(heads.o_taken, 1)
                        if is_group(bg) and i >= 2:
                            t = bg * G + i - 2
                            dve.wait_ge(projected, t + 1)
                            v.tensor_tensor(X[:, t, :], psF[:, 0:D], X[:, t, :], ALU.add).then_inc(x_done, 1)
                        if is_group(g + 1) and i == 2:
                            norm.take_stats(dve, g + 1)
                        if is_group(g + 1) and i == 3:
                            dve.wait_ge(used, g * 6 + 2)
                            norm.normalise(dve, g + 1, Z)

                norm.on_vector(dve, 0, Z)
                rounds(dve, step, NG)

            @block.tensor
            def _(pe):
                pe.wait_ge(heads.set, 4)

                def z_turned(g):
                    pe.wait_ge(norm.normed, g * G + G)
                    for k in range(KC):
                        pe.wait_ge(v_taken, g * 2 * BG)
                        for j in range(G):
                            mm = nc.tensor.transpose(psG[:, k, j * P:(j + 1) * P], Z[:, j, k * P:(k + 1) * P], ident[:])
                        mm.then_inc(used, 1)

                def project(g, m, W, src):
                    for e in range(KC):
                        pe.wait_ge(taken, g * 6 + (2 if m == 0 else e + 3))
                        for k in range(KC):
                            mm = nc.tensor.matmul(psG[:, e, :], W[:, k, e * P:(e + 1) * P], src[:, k, :],
                                                  start=(k == 0), stop=(k == KC - 1))
                        mm.then_inc(used, 1)

                def values_of(g, b):
                    if b < 2:
                        pe.wait_ge(taken, g * 6 + 5 + b)
                    else:
                        pe.wait_ge(v_taken, g * 2 * BG + 2 * (b - 1))
                    for k in range(KC):
                        for hp in range(2):
                            mm = nc.tensor.matmul(psG[hp * L:(hp + 1) * L, b % 2, 0:D],
                                                  CG[:, k, b * L:(b + 1) * L], WV[:, k, :], start=(k == 0),
                                                  stop=(k == KC - 1), skip_group_check=True)
                    mm.then_inc(v_used, 1)

                def turn_out(g, j):
                    t = g * G + j
                    pe.wait_ge(heads.o_taken, t + 1)
                    pe.wait_ge(x_done, t)
                    for c in range(KC):
                        mm = nc.tensor.transpose(psF[:, c * P:(c + 1) * P],
                                                 AO[:, j % 2, c * HC:(c + 1) * HC, :].rearrange("p h d -> p (h d)"),
                                                 ident[:])
                    mm.then_inc(ao_turned, 1)

                def project_out(g, j):
                    t = g * G + j
                    pe.wait_ge(at_done, t + 1)
                    for c in range(KC):
                        mm = nc.tensor.matmul(psF[:, 0:D], AT[:, j % 2, c, :], WO[:, c, :], start=(c == 0),
                                              stop=(c == KC - 1))
                    mm.then_inc(projected, 1)

                def step(g, w):
                    bg, bw = g - 1, 1 - w
                    if is_group(bg):
                        pe.wait_ge(taken, bg * 6 + 4)
                        pe.wait_ge(v_taken, (bg + 1) * 2 * BG)
                    for i in range(G + 2):
                        if is_group(bg) and i < G:
                            heads.scores(pe, bg, bw, i)
                        if is_group(bg) and i >= 2:
                            turn_out(bg, i - 2)
                        if is_group(bg) and 1 <= i <= G:
                            heads.turn(pe, bg, i - 1)
                        if is_group(g):
                            if i == 0:
                                z_turned(g)
                            if i == 1:
                                project(g, 0, WQ, ZT)
                            if i == 2:
                                pe.wait_ge(c_in, g * 16 + 16)
                                project(g, 1, WK, CG)
                            for b in V_AT[i]:
                                values_of(g, b)
                        if is_group(bg) and 1 <= i <= G:
                            heads.values(pe, bg, bw, i - 1)
                        if is_group(bg) and i >= 2:
                            project_out(bg, i - 2)

                rounds(pe, step, NG)

            @block.scalar
            def _(act):
                act.wait_ge(b_in, 64)
                SCALE = float(DH) ** -0.5

                def step(g, w):
                    bg = g - 1
                    for i in range(G + 2):
                        if is_group(bg) and i >= 2:
                            j = i - 2
                            t = bg * G + j
                            act.wait_ge(ao_turned, t + 1)
                            if later(bg, 1) or j > 1:
                                act.wait_ge(projected, t - 1)
                            nc.scalar.copy(AT[:, j % 2].rearrange("p c t -> p (c t)"), psF[:, 0:D]).then_inc(
                                at_done, 1)
                        if is_group(bg) and 1 <= i <= G:
                            heads.copy_turned(act, bg, i - 1)
                        if is_group(g) and i == 0:
                            for k in range(KC):
                                act.wait_ge(used, g * 6 + k + 1)
                                nc.scalar.copy(ZT[:, k, :], psG[:, k, :]).then_inc(taken, 1)
                        if is_group(g) and i == 1:
                            if later(g, 2):
                                act.wait_ge(heads.scored, g * G - G)
                            for e in range(KC):
                                act.wait_ge(used, g * 6 + 3 + e)
                                nc.scalar.activation(heads.QT[:, w, e, :], psG[:, e, :], ACT.Identity,
                                                     bias=bq[:, e:e + 1]).then_inc(taken, 1)
                        if is_group(g) and i == 2:
                            for half in range(2):
                                act.wait_ge(heads.kx_in[half], g * 256)
                            for e in range(KC):
                                act.wait_ge(used, g * 6 + 5 + e)
                                nc.scalar.activation(KT[:, e, :], psG[:, e, :], ACT.Identity,
                                                     bias=bk[:, e:e + 1]).then_inc(taken, 1)
                        if is_group(bg) and i < G:
                            act.wait_ge(heads.s_taken, bg * G + i + 1)
                            nc.scalar.activation(heads.PB[:, i % 2], heads.PB[:, i % 2], ACT.Exp,
                                                 scale=SCALE).then_inc(heads.weighted, 1)

                rounds(act, step, NG)

def gated_ffn(nc, io, X, ident, identb):
    with ExitStack() as ctx:
        s = Scope(nc, ctx, "gffn")
        WG = s.sb("WG", [P, KC, FF], BF16)
        WU = s.sb("WU", [P, KC, FF], BF16)
        W2 = s.sb("W2", [P, FF // P, D], BF16)
        ug, uu, u2 = s.sb("ug", [P, 1]), s.sb("uu", [P, 1]), s.sb("u2", [P, 1])
        ternary(nc, "gffn_weights", identb, [(io["L2_ffn_w_gate"], WG, ug), (io["L2_ffn_w_up"], WU, uu),
                                       (io["L2_ffn_w_down"], W2, u2)])
        H = s.sb("H", [P, 2, G, FF])
        S = s.sb("S", [P, 2, HALF])
        q = Rounded(nc, s, X, ident, 1e-6, 1e-5)
        down = Down(nc, s, X, identb, W2, u2, 1e-6)
        uwg, uwu = s.sb("uwg", [P, 2, G]), s.sb("uwu", [P, 2, G])
        psG = s.ps("psG", [P, 2, HALF])
        psU = s.ps("psU", [P, 2, HALF])
        uw_done, up, gated, taken = (s.sem(x) for x in ("uw_done", "up", "gated", "taken"))

        with nc.Block() as block:

            @block.gpsimd
            def _(pool):
                q.constants(pool)
                down.constants(pool)

                def both(g, w, front, back):
                    if back:
                        down.power(pool, g - 1)
                    if front:
                        q.on_pool(pool, g)

                interleave(pool, both)

            @block.vector
            def _(dve):
                v = nc.vector

                def both(g, w, front, back):
                    if back:
                        down.scales(dve, g - 1, 1 - w)
                    if front:
                        q.on_vector(dve, g, w)
                        v.tensor_scalar(uwg[:, w], q.unit[:, w], ug[:, 0:1], None, ALU.mult).then_inc(uw_done, 1)
                        v.tensor_scalar(uwu[:, w], q.unit[:, w], uu[:, 0:1], None, ALU.mult).then_inc(uw_done, 1)
                        dve.wait_ge(uw_done, g * 2 + 2)
                    for j in range(G):
                        if back:
                            down.integers(dve, g - 1, j)
                        if front:
                            t = g * G + j
                            for h in range(2):
                                dve.wait_ge(gated, t * 2 + h + 1)
                                v.scalar_tensor_tensor(H[:, w, j, h * HALF:(h + 1) * HALF], psU[:, h, :],
                                                       uwu[:, w, j:j + 1], S[:, h, :], ALU.mult,
                                                       ALU.mult).then_inc(taken, 1)
                            if back and j > 0:
                                down.add(dve, g - 1, j - 1)
                            dve.wait_ge(taken, t * 2 + 2)
                            down.maximum(w, j, H[:, w, j])
                        elif j > 0:
                            down.add(dve, g - 1, j - 1)
                    if back:
                        down.add(dve, g - 1, G - 1)

                interleave(dve, both)

            @block.tensor
            def _(pe):
                def up_(g, w, j):
                    for h in range(2):
                        if later(g, 1) or j > 0:
                            pe.wait_ge(taken, (g * G + j) * 2 + h - 1)
                        for bank, W in ((psG, WG), (psU, WU)):
                            for k in range(KC):
                                mm = nc.tensor.matmul(bank[:, h, :], q.QT[:, w, k, j * P:(j + 1) * P],
                                                      W[:, k, h * HALF:(h + 1) * HALF], start=(k == 0),
                                                      stop=(k == KC - 1))
                        mm.then_inc(up, 1)

                def both(g, w, front, back):
                    if front:
                        q.on_tensor(pe, g)
                        pe.wait_ge(q.qt_done, g * KC + KC)
                        up_(g, w, 0)
                    for j in range(G):
                        if back:
                            down.turn(pe, g - 1, j)
                        if front and j + 1 < G:
                            up_(g, w, j + 1)
                        if back:
                            down.product(pe, g - 1, j)

                interleave(pe, both)

            @block.scalar
            def _(act):
                def both(g, w, front, back):
                    if front:
                        q.on_scalar(act, g, w)
                        act.wait_ge(uw_done, g * 2 + 2)
                    for j in range(G):
                        t = g * G + j
                        if back:
                            down.scale_and_round(act, g - 1, j, H[:, 1 - w, j])
                        if front:
                            for h in range(2):
                                act.wait_ge(up, t * 2 + h + 1)
                                if later(g, 1) or j > 0:
                                    act.wait_ge(taken, t * 2 + h - 1)
                                nc.scalar.activation(S[:, h, :], psG[:, h, :], ACT.Silu,
                                                     scale=uwg[:, w, j:j + 1]).then_inc(gated, 1)
                        if back:
                            down.copy_turned(act, g - 1, j)
                        if front:
                            act.wait_ge(taken, t * 2 + 2)
                            down.squares(act, g, w, j, H[:, w, j])

                interleave(act, both)

def quantized_ffn(nc, io, X, ident, out):
    with ExitStack() as ctx:
        s = Scope(nc, ctx, "qffn")
        K = s.sb("K", [P, KC, D])
        KT = s.sb("KT", [P, KC, D])
        W = s.sb("W", [P, KC, D], BF16)
        cols = s.sb("cols", [P, KC, 4])
        unit_w = s.sb("unit_w", [P, D])
        bias = s.sb("bias", [P, D])
        bq = s.sb("bq", [P, D])
        bs = s.sb("bs", [P, 4])
        diag = s.sb("diag", [P, KC, P])
        ones = s.sb("ones", [P, P])
        Y = s.sb("Y", [P, 2, G, D])
        YR = s.sb("YR", [P, G, D])
        q = Rounded(nc, s, X, ident, None, 1e-35)
        ymax, yunit, yinv = s.sb("ymax", [P, G]), s.sb("yunit", [P, G]), s.sb("yinv", [P, G])
        psK = s.ps("psK", [P, KC, D])
        psW = s.ps("psW", [P, D])
        psU = s.ps("psU", [P, D])
        psY = s.ps("psY", [P, 2, 512])
        (w_in, set_, k_steps, turned, back_turned, spread_out, up, scaled, y_steps,
         x_done, stored) = (s.sem(x) for x in ("w_in", "set", "k_steps", "turned", "back_turned", "spread_out",
                                               "up", "scaled", "y_steps", "x_done",
                                               "stored"))
        SETUP = 20

        with nc.Block() as block:

            @block.sync
            def _(sp):
                sp.dma_start(K[:], io["L3_ffn_kernel"].rearrange("(k p) f -> p k f", p=P)).then_inc(w_in, 16)
                sp.dma_start(bias[:], spread(io["L3_ffn_bias"], 0, P)).then_inc(w_in, 16)
                sp.wait_ge(w_in, 32)
                o = out.rearrange("(t u) l d -> (u l) t d", u=2)
                with sp.Fori(0, NG) as g:
                    sp.wait_ge(x_done, g + 1)
                    sp.dma_start(o[:, bass.ds(g * G, G), :], X[:, bass.ds(g * G, G), :]).then_inc(stored, 16)
                sp.wait_ge(stored, 16 * NG)

            @block.gpsimd
            def _(pool):
                nc.gpsimd.memset(ones[:], 1.0).then_inc(set_, 1)
                q.constants(pool)
                pipeline(pool, lambda g, w: q.on_pool(pool, g), lambda g, w: None)

            @block.vector
            def _(dve):
                v = nc.vector
                step = Steps(dve, k_steps, SETUP)
                dve.wait_ge(w_in, 32)
                dve.wait_ge(turned, 2)
                for k in range(KC):
                    step(v.tensor_reduce(cols[:, k, 0:1], psK[:, k, :], AX.X, ALU.max, apply_absolute_value=True))
                    step(v.tensor_scalar(cols[:, k, 1:2], cols[:, k, 0:1], 1e-35, 1.0 / 127.0, ALU.max, ALU.mult))
                    step(v.reciprocal(cols[:, k, 2:3], cols[:, k, 1:2]))
                    step(v.tensor_scalar(KT[:, k, :], psK[:, k, :], cols[:, k, 2:3], MAGIC, ALU.mult, ALU.add))
                    step(v.tensor_scalar(KT[:, k, :], KT[:, k, :], MAGIC, None, ALU.subtract))
                    step(v.tensor_scalar(diag[:, k, :], ident[:], cols[:, k, 1:2], None, ALU.mult))
                step(v.tensor_reduce(bs[:, 0:1], bias[:], AX.X, ALU.max, apply_absolute_value=True))
                step(v.tensor_scalar(bs[:, 1:2], bs[:, 0:1], 1e-35, 1.0 / 127.0, ALU.max, ALU.mult))
                step(v.reciprocal(bs[:, 2:3], bs[:, 1:2]))
                step(v.tensor_scalar(bq[:], bias[:], bs[:, 2:3], MAGIC, ALU.mult, ALU.add))
                step(v.tensor_scalar(bq[:], bq[:], MAGIC, bs[:, 1:2], ALU.subtract, ALU.mult))
                dve.wait_ge(spread_out, 1)
                step(v.tensor_copy(unit_w[:], psU[:]))
                dve.wait_ge(back_turned, 1)
                step(v.tensor_copy(W[:, 0, :], psW[:]))
                dve.wait_ge(back_turned, 2)
                step(v.tensor_copy(W[:, 1, :], psW[:]))
                step.end()

                def back(g, w):
                    for j in range(G):
                        t = g * G + j
                        dve.wait_ge(up, t + 1)
                        v.scalar_tensor_tensor(Y[:, w, j], psY[:, j % 2, 0:D], q.unit[:, w, j:j + 1], unit_w[:],
                                               ALU.mult, ALU.mult).then_inc(scaled, 1)
                    dve.wait_ge(scaled, g * G + G)
                    step = Steps(dve, y_steps, 7, g)
                    y = Y[:, w]
                    step(v.tensor_tensor(y, y, spread(bq[:], 1, G), ALU.add))
                    step(v.tensor_scalar(y, y, 0.0, None, ALU.max))
                    step(v.tensor_reduce(ymax[:], y, AX.X, ALU.max))
                    step(v.tensor_scalar(yunit[:], ymax[:], 1e-35, 1.0 / 127.0, ALU.max, ALU.mult))
                    step(v.reciprocal(yinv[:], yunit[:]))
                    step(v.tensor_tensor(YR[:], y, spread(yinv[:], 2, D), ALU.mult))
                    step(v.tensor_scalar(YR[:], YR[:], MAGIC, MAGIC, ALU.add, ALU.subtract))
                    step.end()
                    for j in range(G):
                        x = X[:, g * G + j, :]
                        m = v.scalar_tensor_tensor(x, YR[:, j], yunit[:, j:j + 1], x, ALU.mult, ALU.add)
                    m.then_inc(x_done, 1)

                pipeline(dve, lambda g, w: q.on_vector(dve, g, w), back)

            @block.tensor
            def _(pe):
                pe.wait_ge(w_in, 32)
                for f in range(KC):
                    for k in range(KC):
                        mm = nc.tensor.transpose(psK[:, f, k * P:(k + 1) * P], K[:, k, f * P:(f + 1) * P], ident[:])
                    mm.then_inc(turned, 1)
                pe.wait_ge(k_steps, 12)
                pe.wait_ge(set_, 1)
                for f in range(KC):
                    mm = nc.tensor.matmul(psU[:, f * P:(f + 1) * P], ones[:], diag[:, f, :], start=True, stop=True)
                mm.then_inc(spread_out, 1)
                for k in range(KC):
                    if k == 1:
                        pe.wait_ge(k_steps, SETUP - 1)
                    for f in range(KC):
                        mm = nc.tensor.transpose(psW[:, f * P:(f + 1) * P], KT[:, f, k * P:(k + 1) * P], ident[:])
                    mm.then_inc(back_turned, 1)
                pe.wait_ge(k_steps, SETUP)

                def back(g, w):
                    pe.wait_ge(q.qt_done, g * KC + KC)
                    for j in range(G):
                        t = g * G + j
                        if later(g, 1) or j > 1:
                            pe.wait_ge(scaled, t - 1)
                        for k in range(KC):
                            mm = nc.tensor.matmul(psY[:, j % 2, 0:D], q.QT[:, w, k, j * P:(j + 1) * P], W[:, k, :],
                                                  start=(k == 0), stop=(k == KC - 1))
                        mm.then_inc(up, 1)

                pipeline(pe, lambda g, w: q.on_tensor(pe, g), back)

            @block.scalar
            def _(act):
                def front(g, w):
                    if later(g, 2):
                        act.wait_ge(up, g * G - G)
                    q.on_scalar(act, g, w)

                pipeline(act, front, lambda g, w: None)

def summary_mix(nc, io, X, CT, ident, sums):
    with ExitStack() as ctx:
        s = Scope(nc, ctx, "mix")
        norm = Norm(nc, s, X)
        WI, WO = s.sb("WI", [P, KC, D]), s.sb("WO", [P, KC, D])
        WIT, WOT = s.sb("WIT", [P, KC, D]), s.sb("WOT", [P, KC, D])
        bi = s.sb("bi", [P, KC])
        bo = s.sb("bo", [L, D])
        gam, bet = s.sb("gam", [P, D]), s.sb("bet", [P, D])
        decay, k = s.sb("decay", [P, 1]), s.sb("k", [P, 3])
        ones = s.sb("ones", [P, L])
        powers, weights, wsum = s.sb("powers", [P, L]), s.sb("weights", [P, L]), s.sb("wsum", [P, 1])
        flip, flipped = s.sb("flip", [L, L]), s.sb("flipped", [L, L])
        col, diag, all1 = s.sb("col", [L, 1]), s.sb("diag", [L, L]), s.sb("all1", [L, P])
        weighted = s.sb("weighted", [P, 2, B // 2, L])
        ST = s.sb("ST", [P, KC, B])
        bw = s.sb("bw", [P, KC])
        HT = s.sb("HT", [P, KC, B])
        SUM = s.sb("SUM", [B, D])
        SM = s.sb("SM", [P, T, D])
        Y = s.sb("Y", [P, 2, G, D])
        stats, mv = s.sb("stats2", [P, G, 6]), s.sb("mv2", [P, G, 2])
        veps, rstd = s.sb("veps2", [P, G]), s.sb("rstd2", [P, G])
        psW = s.ps("psW", [P, 2, KC, D])
        psB = s.ps("psB", [P, 512])
        psH = s.ps("psH", [P, KC, 512])
        psS = s.ps("psS", [B, 512])
        (w_in, ready, steps, expd, w_turned, w_copied, wide, hid, summed, sum_out, sum_in, added, stats_done,
         veps_done, rstd_done, normed, gained, y_steps) = (s.sem(x) for x in (
             "w_in", "ready", "steps", "expd", "w_turned", "w_copied", "wide", "hid", "summed", "sum_out", "sum_in",
             "added", "stats2_done", "veps2_done", "rstd2_done", "normed2", "gained", "y_steps"))
        SETUP = 21

        with nc.Block() as block:

            @block.sync
            def _(sp):
                sp.dma_start(decay[:], spread(io["L3_xattn_decay"], 0, P)).then_inc(w_in, 16)
                sp.dma_start(WI[:], io["L3_xattn_W_in"].rearrange("(k p) d -> p k d", p=P)).then_inc(w_in, 16)
                sp.dma_start(WO[:], io["L3_xattn_W_out"].rearrange("(k p) d -> p k d", p=P)).then_inc(w_in, 16)
                with nc.allow_non_contiguous_dma(reason="one column of biases for each chunk"):
                    sp.dma_start(bi[:], io["L3_xattn_b_in"].rearrange("(k p) -> p k", p=P)).then_inc(w_in, 16)
                sp.dma_start(bo[:], spread(io["L3_xattn_b_out"], 0, L)).then_inc(w_in, 16)
                sp.dma_start(gam[:], spread(io["L3_xattn_gamma"], 0, P)).then_inc(w_in, 16)
                sp.dma_start(bet[:], spread(io["L3_xattn_beta"], 0, P)).then_inc(w_in, 16)
                sp.wait_ge(w_in, 112)
                sp.wait_ge(steps, SETUP)
                sp.dma_start(sums, SUM[:]).then_inc(sum_out, 16)
                sp.wait_ge(sum_out, 16)
                for u in range(2):
                    sp.dma_start(SM[u * L:(u + 1) * L],
                                 spread(sums.rearrange("(t u) d -> u t d", u=2)[u], 0, L)).then_inc(sum_in, 16)

            @block.gpsimd
            def _(pool):
                nc.gpsimd.memset(ones[:], 1.0).then_inc(ready, 1)
                nc.gpsimd.memset(all1[:], 1.0).then_inc(ready, 1)
                nc.gpsimd.memset(flip[:], 0.0).then_inc(ready, 1)
                pool.wait_ge(ready, 3)
                nc.gpsimd.affine_select(out=flip[:], in_=flip[:], compare_op=ALU.not_equal, fill=1.0, base=1 - L,
                                        pattern=[[1, L]], channel_multiplier=1).then_inc(ready, 1)
                norm.constants(pool)
                pool.wait_ge(w_in, 112)

                def front(g, w):
                    norm.on_pool(pool, g)
                    pool.wait_ge(norm.normed, g * G + G)
                    if not later(g, 1):
                        pool.wait_ge(sum_in, 32)
                    nc.gpsimd.tensor_tensor(Y[:, w], Y[:, w], SM[:, bass.ds(g * G, G), :], ALU.add).then_inc(added, 1)

                def back(g, w):
                    pool.wait_ge(stats_done, g * G + G)
                    nc.gpsimd.tensor_tensor(veps[:], mv[:, :, 1], norm.eps[:], ALU.add).then_inc(veps_done, 1)
                    pool.wait_ge(veps_done, g + 1)
                    nc.gpsimd.tensor_tensor(rstd[:], veps[:], norm.mhalf[:], ALU.pow).then_inc(rstd_done, 1)
                    pool.wait_ge(normed, g * G + G)
                    nc.gpsimd.tensor_tensor(Y[:, w], Y[:, w], spread(gam[:], 1, G), ALU.mult).then_inc(gained, 1)

                pipeline(pool, front, back)

            @block.vector
            def _(dve):
                v = nc.vector
                step = Steps(dve, steps, SETUP)
                dve.wait_ge(ready, 4)
                dve.wait_ge(expd, 1)
                step(v.tensor_scalar(k[:, 1:2], k[:, 0:1], 1.0, None, ALU.add))
                step(v.reciprocal(k[:, 2:3], k[:, 1:2]))
                step(v.tensor_scalar(weights[:], ones[:], k[:, 2:3], None, ALU.mult))
                step(v.tensor_tensor_scan(powers[:], weights[:], ones[:], 0.0, ALU.mult, ALU.add))
                step(v.tensor_tensor(flipped[:], powers[0:L, :], flip[:], ALU.mult))
                step(v.tensor_reduce(col[:], flipped[:], AX.X, ALU.add))
                step(v.tensor_scalar(diag[:], ident[0:L, 0:L], col[:, 0:1], None, ALU.mult))
                dve.wait_ge(wide, 1)
                step(v.tensor_copy(weights[:], psB[:, 0:L]))
                step(v.tensor_reduce(wsum[:], weights[:], AX.X, ALU.add))
                dve.wait_ge(w_in, 112)
                step(v.tensor_scalar(bw[:], bi[:], wsum[:, 0:1], None, ALU.mult))
                for c in range(KC):
                    for half in range(2):
                        seg = CT[:, c, half * (N // 2):(half + 1) * (N // 2)].rearrange("p (b l) -> p b l", l=L)
                        step(v.tensor_tensor(weighted[:, half], seg, spread(weights[:], 1, B // 2), ALU.mult))
                        step(v.tensor_reduce(ST[:, c, half * (B // 2):(half + 1) * (B // 2)], weighted[:, half], AX.X,
                                             ALU.add))
                for c in range(KC):
                    dve.wait_ge(hid, c + 1)
                    step(v.tensor_scalar(HT[:, c, :], psH[:, c, 0:B], bw[:, c:c + 1], None, ALU.add))
                dve.wait_ge(summed, 1)
                step(v.scalar_tensor_tensor(SUM[:], psS[:, 0:D], 1.0 / L, bo[:], ALU.mult, ALU.add))
                step.end()

                def back(g, w):
                    dve.wait_ge(added, g + 1)
                    for j in range(G):
                        v.bn_stats(stats[:, j, :], Y[:, w, j, :])
                    dve.drain()
                    for j in range(G):
                        v.bn_aggr(mv[:, j, :], stats[:, j, :]).then_inc(stats_done, 1)
                    dve.wait_ge(rstd_done, g + 1)
                    dve.wait_ge(stats_done, g * G + G)
                    for j in range(G):
                        v.tensor_scalar(Y[:, w, j], Y[:, w, j], mv[:, j, 0:1], rstd[:, j:j + 1], ALU.subtract,
                                        ALU.mult).then_inc(normed, 1)
                    dve.wait_ge(gained, g + 1)
                    step = Steps(dve, y_steps, 2, g)
                    step(v.tensor_tensor(Y[:, w], Y[:, w], spread(bet[:], 1, G), ALU.add))
                    xs = X[:, bass.ds(g * G, G), :]
                    step(v.tensor_tensor(xs, xs, Y[:, w], ALU.add))
                    step.end()

                pipeline(dve, lambda g, w: norm.on_vector(dve, g, Y[:, w]), back)

            @block.tensor
            def _(pe):
                pe.wait_ge(w_in, 112)
                for m, W in enumerate((WI, WO)):
                    for k_ in range(KC):
                        for c in range(KC):
                            mm = nc.tensor.transpose(psW[:, m, k_, c * P:(c + 1) * P], W[:, c, k_ * P:(k_ + 1) * P],
                                                     ident[:])
                    mm.then_inc(w_turned, 1)
                pe.wait_ge(steps, 7)
                nc.tensor.matmul(psB[:, 0:L], all1[:], diag[:], start=True, stop=True).then_inc(wide, 1)
                pe.wait_ge(steps, 18)
                pe.wait_ge(w_copied, 1)
                for e in range(KC):
                    for c in range(KC):
                        mm = nc.tensor.matmul(psH[:, e, 0:B], WIT[:, c, e * P:(e + 1) * P], ST[:, c, :],
                                              start=(c == 0), stop=(c == KC - 1))
                    mm.then_inc(hid, 1)
                pe.wait_ge(steps, 20)
                pe.wait_ge(w_copied, 2)
                for e in range(KC):
                    mm = nc.tensor.matmul(psS[:, 0:D], HT[:, e, :], WOT[:, e, :], start=(e == 0), stop=(e == KC - 1))
                mm.then_inc(summed, 1)

            @block.scalar
            def _(act):
                act.wait_ge(w_in, 112)
                nc.scalar.activation(k[:, 0:1], decay[:], ACT.Exp, scale=-1.0).then_inc(expd, 1)
                for m, WT in enumerate((WIT, WOT)):
                    act.wait_ge(w_turned, m + 1)
                    nc.scalar.copy(WT[:], psW[:, m]).then_inc(w_copied, 1)

def mk_xattn_ffn_d4(nc, io, out):
    zq = nc.dram_tensor("z_parts", (3, DH0, T // 2, 2 * NH0, 2, D), BF16, kind="Internal").ap()
    ck = nc.dram_tensor("context_parts", (3, DH0, T // 2, 2 * NH0, 2, D), BF16, kind="Internal").ap()
    o_dram = nc.dram_tensor("head_sums", (T, 4, 4, DH0 + 1, D), F32, kind="Internal").ap()
    sums = nc.dram_tensor("summaries", (B, D), F32, kind="Internal").ap()
    with ExitStack() as ctx:
        s = Scope(nc, ctx, "all")
        X = s.sb("X", [P, T, D])
        CT = s.sb("CT", [P, KC, N])
        ident = s.sb("ident", [P, P])
        identb = s.sb("identb", [P, P], BF16)
        prepare(nc, io, X, CT, ident, zq, ck)
        with nc.Block() as block:

            @block.vector
            def _(dve):
                nc.vector.tensor_copy(identb[:], ident[:])

        row_attention(nc, io, X, CT, identb, zq, ck, o_dram)
        selected_ffn(nc, io, X, ident)
        gated_attention(nc, io, X, CT, ident, identb)
        normed_ffn(nc, io, X, ident, identb)
        softmax_attention(nc, io, X, CT, ident)
        gated_ffn(nc, io, X, ident, identb)
        summary_mix(nc, io, X, CT, ident, sums)
        quantized_ffn(nc, io, X, ident, out)

_INS = ["x", "ctx_2048", "L0_ffn_w_r", "L0_ffn_b_r", "L0_ffn_w1", "L0_ffn_b1", "L0_ffn_w2", "L0_ffn_b2",
        "L1_xattn_Wi", "L1_xattn_bi", "L1_xattn_Wf", "L1_xattn_bf", "L1_xattn_ln_scale", "L1_ffn_w1", "L1_ffn_b1",
        "L1_ffn_ln_g", "L1_ffn_ln_b", "L1_ffn_w2", "L1_ffn_b2", "L2_xattn_Wq", "L2_xattn_bq", "L2_xattn_Wk",
        "L2_xattn_bk", "L2_xattn_Wv", "L2_xattn_bv", "L2_xattn_Wo", "L2_xattn_bo", "L2_ffn_w_gate", "L2_ffn_w_up",
        "L2_ffn_w_down", "L3_xattn_decay", "L3_xattn_W_in", "L3_xattn_b_in", "L3_xattn_W_out", "L3_xattn_b_out",
        "L3_xattn_gamma", "L3_xattn_beta", "L3_ffn_kernel", "L3_ffn_bias"]

def kernel(**inputs):
    import numpy as _np
    import concourse.bacc as _bacc
    from concourse import mybir as _mybir
    from concourse.bass_utils import run_bass_kernel_spmd as _run

    nc = _bacc.Bacc("TRN2", target_bir_lowering=False, num_devices=1)
    arrays, io = {}, {}
    for name in _INS:
        a = _np.ascontiguousarray(inputs[name])
        if a.ndim == 0:
            a = a.reshape(1)
        arrays[f"in_{name}_dram"] = a
        io[name] = nc.dram_tensor(f"in_{name}_dram", a.shape, _mybir.dt.from_np(a.dtype), kind="ExternalInput").ap()
    out = nc.dram_tensor("out_0_dram", (B, L, D), F32, kind="ExternalOutput").ap()
    mk_xattn_ffn_d4(nc, io, out)
    r = _run(nc, [arrays], core_ids=[0])
    return r.results[0]["out_0_dram"]
```

```python
from contextlib import ExitStack

import numpy as np

import concourse.bass as bass
from concourse import mybir

ALU = mybir.AluOpType
ACT = mybir.ActivationFunctionType
AX = mybir.AxisListType
F32 = mybir.dt.float32
BF16 = mybir.dt.bfloat16

P = 128
B, L, D = 64, 64, 256
N = B * L
T = N // P
G = 4
NG = T // G
KC = D // P
FF = 4 * D
NH0, DH0 = 8, 8
BH = B * NH0
NH, DH = 16, 16
KEEP = L // 2
LN_EPS = 1e-5
MAGIC = 12582912.0
BIG = 1.0e30

class Scope:

    def __init__(self, nc, ctx, name):
        self.nc, self.ctx, self.name, self.sems = nc, ctx, name, []
        ctx.callback(self.close)

    def sb(self, name, shape, dt=F32):
        return self.ctx.enter_context(self.nc.sbuf_tensor(f"{self.name}_{name}", shape, dt))

    def ps(self, name, shape, dt=F32):
        return self.ctx.enter_context(self.nc.psum_tensor(f"{self.name}_{name}", shape, dt))

    def sem(self, name):
        self.sems.append(self.nc.alloc_semaphore(name=f"{self.name}_{name}"))
        return self.sems[-1]

    def close(self):
        if self.sems:
            self.nc.clear_and_free_semaphores(self.sems)
            self.nc.all_engine_barrier()

class Steps:

    def __init__(self, engine, done, per, i=0):
        self.engine, self.done, self.per, self.i, self.n = engine, done, per, i, 0

    def __call__(self, instruction):
        self.n += 1
        instruction.then_inc(self.done, 1)
        self.engine.wait_ge(self.done, self.i * self.per + self.n)

    def end(self):
        assert self.n == self.per, (self.n, self.per)

def held(engine, value):
    return value if isinstance(value, int) else engine.snap(value)

def spread(ap, dim, n):
    return ap.unsqueeze(dim).to_broadcast(list(ap.shape[:dim]) + [n] + list(ap.shape[dim:]))

def prepare(nc, io, X, CT, ident, zq, ck):
    with ExitStack() as ctx:
        s = Scope(nc, ctx, "prep")
        C = s.sb("C", [P, 2, G, D])
        Z = s.sb("Z", [P, G, D])
        ZR = s.sb("ZR", [P, 2, G, D])
        CR = s.sb("CR", [P, 2, G, D])
        ZS = s.sb("ZS", [P, 2, 3, G, D], BF16)
        CS = s.sb("CS", [P, 2, 3, G, D], BF16)
        stats = s.sb("stats", [P, G, 6])
        mv = s.sb("mv", [P, G, 2])
        veps = s.sb("veps", [P, G])
        rstd = s.sb("rstd", [P, G])
        mhalf = s.sb("mhalf", [P, G])
        eps = s.sb("eps", [P, G])
        psC = s.ps("psC", [P, KC, G * P])
        ready = s.sem("ready")
        x_in, c_in = s.sem("x_in"), s.sem("c_in")
        stats_done, rstd_done, pool_step = s.sem("stats_done"), s.sem("rstd_done"), s.sem("pool_step")
        z_done = s.sem("z_done")
        z_part, z_rest, c_part, c_rest = s.sem("z_part"), s.sem("z_rest"), s.sem("c_part"), s.sem("c_rest")
        turned, ct_done = s.sem("turned"), s.sem("ct_done")
        z_out = [s.sem(f"z_out{w}") for w in range(2)]
        c_out = [s.sem(f"c_out{w}") for w in range(2)]
        x_dram = io["x"].rearrange("(t u) l d -> t (u l) d", u=2)
        c_dram = io["ctx_2048"].rearrange("(t u) l d -> t (u l) d", u=2)
        zq_w = zq.rearrange("s r a h u m -> s a h r (u m)")
        ck_w = ck.rearrange("s r a h u m -> s a h r (u m)")

        OUT = 16 * 3 * (G // 2)

        def pairs(engine, body):
            for w in range(2):
                body(0, w)
            with engine.Fori(1, NG // 2) as h:
                for w in range(2):
                    body(h, w)

        with nc.Block() as block:

            @block.sync
            def _(sp):
                def load(t, w):
                    sp.dma_start(X[:, bass.ds(t, G), :],
                                 x_dram[bass.ds(t, G)].rearrange("t p d -> p t d")).then_inc(x_in, 16)
                    sp.dma_start(C[:, w], c_dram[bass.ds(t, G)].rearrange("t p d -> p t d")).then_inc(c_in, 16)

                load(0, 0)
                def turn(h, last):
                    for w in range(2):
                        g = h * 2 + w
                        to = [held(sp, g * (G // 2) + a) for a in range(G // 2)]
                        ahead, loads, before = (held(sp, v) for v in (g * G + G, g * 16 + 16, g * 16))
                        parts = [held(sp, g * 3 + part + 1) for part in range(3)]
                        sp.wait_ge(x_in, loads)
                        sp.wait_ge(c_in, loads)
                        sp.wait_ge(c_rest, before)
                        sp.wait_ge(turned, before)
                        if w == 0 or not last:
                            load(ahead, 1 - w)
                        for part in range(3):
                            sp.wait_ge(z_part, parts[part])
                            for a in range(G // 2):
                                sp.dma_start(zq_w[part, bass.ds(to[a], 1)], ZS[:, w, part, 2 * a:2 * a + 2].rearrange(
                                    "p u m -> p (u m)")).then_inc(z_out[w], 16)
                        for part in range(3):
                            sp.wait_ge(c_part, parts[part])
                            for a in range(G // 2):
                                sp.dma_start(ck_w[part, bass.ds(to[a], 1)], CS[:, w, part, 2 * a:2 * a + 2].rearrange(
                                    "p u m -> p (u m)")).then_inc(c_out[w], 16)

                turn(0, False)
                with sp.Fori(1, NG // 2 - 1) as h:
                    turn(h, False)
                turn(NG // 2 - 1, True)
                for w in range(2):
                    sp.wait_ge(z_out[w], OUT * (NG // 2))
                    sp.wait_ge(c_out[w], OUT * (NG // 2))

            @block.gpsimd
            def _(pool):
                nc.gpsimd.memset(mhalf[:], -0.5).then_inc(ready, 1)
                nc.gpsimd.memset(eps[:], LN_EPS).then_inc(ready, 1)
                nc.gpsimd.memset(ident[:], 0.0).then_inc(ready, 1)
                pool.wait_ge(ready, 3)
                nc.gpsimd.affine_select(out=ident[:], in_=ident[:], compare_op=ALU.not_equal, fill=1.0, base=0,
                                        pattern=[[-1, P]], channel_multiplier=1).then_inc(ready, 1)
                def body(h, w):
                    g = h * 2 + w
                    step = Steps(pool, pool_step, 1, g)
                    pool.wait_ge(stats_done, g * G + G)
                    step(nc.gpsimd.tensor_tensor(veps[:], mv[:, :, 1], eps[:], ALU.add))
                    nc.gpsimd.tensor_tensor(rstd[:], veps[:], mhalf[:], ALU.pow).then_inc(rstd_done, 1)
                    step.end()
                    pool.wait_ge(c_part, g * 3 + 1)
                    nc.gpsimd.tensor_tensor(CR[:, 0], C[:, w], CS[:, w, 0], ALU.subtract).then_inc(c_rest, 8)
                    pool.wait_ge(c_part, g * 3 + 2)
                    pool.wait_ge(c_rest, g * 16 + 8)
                    nc.gpsimd.tensor_tensor(CR[:, 1], CR[:, 0], CS[:, w, 1], ALU.subtract).then_inc(c_rest, 8)

                pairs(pool, body)

            @block.tensor
            def _(pe):
                pe.wait_ge(ready, 4)
                def body(h, w):
                    g = h * 2 + w
                    pe.wait_ge(c_in, g * 16 + 16)
                    pe.wait_ge(ct_done, g * KC)
                    for k in range(KC):
                        for j in range(G):
                            mm = nc.tensor.transpose(psC[:, k, j * P:(j + 1) * P],
                                                     C[:, w, j, k * P:(k + 1) * P], ident[:])
                    mm.then_inc(turned, 16)

                pairs(pe, body)

            @block.scalar
            def _(act):
                def body(h, w):
                    g = h * 2 + w
                    act.wait_ge(c_in, g * 16 + 16)
                    act.wait_ge(c_out[w], h * OUT)
                    nc.scalar.copy(CS[:, w, 0], C[:, w]).then_inc(c_part, 1)
                    act.wait_ge(z_done, g * G + G)
                    act.wait_ge(z_out[w], h * OUT)
                    nc.scalar.copy(ZS[:, w, 0], Z[:]).then_inc(z_part, 1)
                    act.wait_ge(turned, g * 16 + 16)
                    for k in range(KC):
                        nc.scalar.copy(CT[:, k, bass.ds(g * (G * P), G * P)], psC[:, k, :]).then_inc(ct_done, 1)
                    act.wait_ge(c_rest, g * 16 + 8)
                    nc.scalar.copy(CS[:, w, 1], CR[:, 0]).then_inc(c_part, 1)
                    act.wait_ge(z_rest, g * 2 + 1)
                    nc.scalar.copy(ZS[:, w, 1], ZR[:, 0]).then_inc(z_part, 1)
                    act.wait_ge(c_rest, g * 16 + 16)
                    nc.scalar.copy(CS[:, w, 2], CR[:, 1]).then_inc(c_part, 1)
                    act.wait_ge(z_rest, g * 2 + 2)
                    nc.scalar.copy(ZS[:, w, 2], ZR[:, 1]).then_inc(z_part, 1)

                pairs(act, body)

            @block.vector
            def _(dve):
                def body(h, w):
                    g = h * 2 + w
                    dve.wait_ge(x_in, g * 16 + 16)
                    dve.wait_ge(rstd_done, g)
                    for j in range(G):
                        nc.vector.bn_stats(stats[:, j, :], X[:, g * G + j, :])
                    dve.drain()
                    for j in range(G):
                        nc.vector.bn_aggr(mv[:, j, :], stats[:, j, :]).then_inc(stats_done, 1)
                    dve.wait_ge(rstd_done, g + 1)
                    dve.wait_ge(stats_done, g * G + G)
                    for j in range(G):
                        nc.vector.tensor_scalar(Z[:, j, :], X[:, g * G + j, :], mv[:, j, 0:1], rstd[:, j:j + 1],
                                                ALU.subtract, ALU.mult).then_inc(z_done, 1)
                    dve.wait_ge(z_part, g * 3 + 1)
                    dve.wait_ge(z_done, g * G + G)
                    nc.vector.tensor_tensor(ZR[:, 0], Z[:], ZS[:, w, 0], ALU.subtract).then_inc(z_rest, 1)
                    dve.wait_ge(z_part, g * 3 + 2)
                    dve.wait_ge(z_rest, g * 2 + 1)
                    nc.vector.tensor_tensor(ZR[:, 1], ZR[:, 0], ZS[:, w, 1], ALU.subtract).then_inc(z_rest, 1)

                pairs(dve, body)

def row_attention(nc, io, X, CT, identb, zq, ck, o_dram):
    R = 9 * DH0
    RM = R + 3
    H2 = 2 * NH0
    QUADS = H2 // 4
    PAIR = 16 * 4
    SCALE = float(DH0) ** -0.5
    with ExitStack() as ctx:
        s = Scope(nc, ctx, "ratt")
        Q9 = s.sb("Q9", [P, 2, H2, 2, D], BF16)
        K9 = s.sb("K9", [P, 2, H2, 2, D], BF16)
        E = s.sb("E", [P, 2, 4, KC, D])
        V9 = s.sb("V9", [P, 2, KC, NH0, 32])
        nmax = s.sb("nmax", [P, 2, 2, NH0])
        rest = s.sb("rest", [P, 2, 2, NH0])
        zero = s.sb("zero", [P, 2, NH0])
        parts = s.sb("parts", [P, 2, P], BF16)
        rows = s.sb("rows", [2 * 3 * NH0, 2, P], BF16)
        O = s.sb("O", [P, 2, QUADS, D])
        num = s.sb("num", [P, 2, D])
        den = s.sb("den", [P, 2, D])
        psS = s.ps("psS", [P, 2, 2, D])
        psT = s.ps("psT", [P, 2, 2, KC, D])
        psO = s.ps("psO", [P, 2, D])
        psM = s.ps("psM", [P, 2, 512], BF16)
        ready, ones_set = s.sem("ready"), s.sem("ones_set")
        pair_in = [s.sem(f"pair_in{b}") for b in range(2)]
        scores, maxed, pool_step, split, turned, row_out = (
            s.sem(x) for x in ("scores", "maxed", "pool_step", "split", "turned", "row_out"))
        row_in = [s.sem(f"row_in{b}") for b in range(2)]
        o_back = [s.sem(f"o_back{b}") for b in range(2)]
        shifted, exped, v_in, pv, o_out = (s.sem(x) for x in ("shifted", "exped", "v_in", "pv", "o_out"))
        to_dram, recip, scaled, added = (s.sem(x) for x in ("to_dram", "recip", "scaled", "added"))

        with nc.Block() as block:

            @block.gpsimd
            def _(pool):
                nc.gpsimd.memset(Q9[64:P], 0.0).then_inc(ready, 1)
                pool.wait_ge(ready, 1)
                nc.gpsimd.memset(zero[:], 0.0).then_inc(ready, 1)
                nc.gpsimd.memset(parts[:], 0.0).then_inc(ready, 1)
                nc.gpsimd.memset(V9[:], 0.0).then_inc(ready, 1)
                pool.wait_ge(ready, 4)
                nc.gpsimd.memset(V9[:, :, :, :, DH0:DH0 + 1], 1.0).then_inc(ready, 1)
                pool.wait_ge(ready, 5)

                def take(t, b):
                    unit = t * 2 + b
                    if not isinstance(t, int) or t > 0:
                        pool.wait_ge(pv, t * QUADS + (2 * b - 2))
                    nc.gpsimd.tensor_copy(
                        V9[:, b, :, :, 0:DH0],
                        CT[:, :, bass.ds(t * P + b * L, L)].rearrange("p k (h r) -> p k h r", r=DH0),
                    ).then_inc(v_in, 1)

                def split_max(t, b):
                    unit = t * 2 + b
                    step = Steps(pool, pool_step, 4, unit)
                    pool.wait_ge(maxed, t * H2 + (b + 1) * NH0)
                    if not isinstance(t, int) or t > 0:
                        pool.wait_ge(turned, unit - 1)
                    p = parts[:, b].rearrange("p (c q) -> p c q", c=2)[:, :, 0:3 * NH0].rearrange(
                        "p c (s h) -> p c s h", s=3)
                    step(nc.gpsimd.tensor_tensor(p[:, :, 0], nmax[:, b], zero[:], ALU.add))
                    step(nc.gpsimd.tensor_tensor(rest[:, 0], nmax[:, b], p[:, :, 0], ALU.subtract))
                    step(nc.gpsimd.tensor_tensor(p[:, :, 1], rest[:, 0], zero[:], ALU.add))
                    step(nc.gpsimd.tensor_tensor(rest[:, 1], rest[:, 0], p[:, :, 1], ALU.subtract))
                    nc.gpsimd.tensor_tensor(p[:, :, 2], rest[:, 1], zero[:], ALU.add).then_inc(split, 1)
                    step.end()

                def scale_and_add(t, par):
                    pool.wait_ge(recip, t + 1)
                    nc.gpsimd.tensor_tensor(num[:, par], num[:, par], den[:, par], ALU.mult).then_inc(scaled, 1)
                    pool.wait_ge(scaled, t + 1)
                    nc.gpsimd.tensor_tensor(X[:, t, :], X[:, t, :], num[:, par], ALU.add).then_inc(added, 16)

                def step(i, k, has_s=True, has_t=True):
                    t = i * 4 + k
                    for b in range(2):
                        if has_t:
                            take(t, b)
                        if has_s:
                            split_max(t + 1, b)
                    if has_t and (k > 0 or not isinstance(i, int) or i > 0):
                        scale_and_add(t - 1, (k + 1) % 2)

                split_max(0, 0)
                split_max(0, 1)
                step(0, 0)
                step(0, 1)
                step(0, 2)
                step(0, 3)
                with pool.Fori(1, T // 4 - 1) as i:
                    for k in range(4):
                        step(i, k)
                for k in range(4):
                    step(T // 4 - 1, k, has_s=k < 3)
                scale_and_add(T - 1, 1)

            @block.sync
            def _(sp):
                def load(pair, pb):
                    z = zq.rearrange("s r a h u m -> (s r) a (h u m)")[:, bass.ds(pair, 1), :]
                    sp.dma_start(Q9[0:R, pb].rearrange("p h u m -> p (h u m)"), spread(z, 0, 3)).then_inc(
                        pair_in[pb], 16)
                    for a in range(3):
                        k = ck[a].rearrange("r a h u m -> r a (h u m)")[:, bass.ds(pair, 1), :]
                        sp.dma_start(K9[24 * a:24 * a + 24, pb].rearrange("p h u m -> p (h u m)"),
                                     spread(k, 0, 3)).then_inc(pair_in[pb], 16)

                def bring_row(t, pb, u, b):
                    sp.wait_ge(row_out, t * 2 + b + 1)
                    for c in range(2):
                        sp.dma_start(Q9[R:RM, pb, b * NH0:(b + 1) * NH0, u, c * P:(c + 1) * P],
                                     rows[c * 24:c * 24 + 24, b, :]).then_inc(row_in[b], 16)

                def out(t, par):
                    sp.wait_ge(o_out, t * QUADS + QUADS)
                    for g in range(4):
                        sp.dma_start(o_dram.rearrange("t q g c m -> g c (t q) m")[g][:, bass.ds(t * QUADS, QUADS), :],
                                     O[32 * g:32 * g + DH0 + 1, par]).then_inc(to_dram, 16)

                def back(t, par):
                    sp.wait_ge(to_dram, t * 64 + 64)
                    if not isinstance(t, int) or t > 1:
                        sp.wait_ge(added, t * 16 - 16)
                    o = o_dram.rearrange("t q g c m -> (t q g) c m")[bass.ds(t * H2, H2)]
                    sp.dma_start(num[:, par], o[:, 0:DH0, :]).then_inc(o_back[par], 16)
                    sp.dma_start(den[:, par], spread(o[:, DH0, :], 1, DH0)).then_inc(o_back[par], 16)

                def step(i, k, has_s=True, has_t=True):
                    t = i * 4 + k
                    past = not isinstance(i, int) or i > 0
                    pb1, u1 = ((k + 1) // 2) % 2, (k + 1) % 2
                    if past or k > 0:
                        bring_row(t, (k // 2) % 2, k % 2, 1)
                        out(t - 1, (k + 1) % 2)
                        back(t - 1, (k + 1) % 2)
                    if has_s:
                        bring_row(t + 1, pb1, u1, 0)
                    if k % 2 == 1 and has_s and not (isinstance(i, int) and i == T // 4 - 1):
                        sp.wait_ge(shifted, t * 8 + 8)
                        load(i * 2 + (k + 3) // 2, (k // 2) % 2)

                sp.wait_ge(ones_set, 1)
                sp.wait_ge(ready, 1)
                load(0, 0)
                load(1, 1)
                bring_row(0, 0, 0, 0)
                bring_row(0, 0, 0, 1)
                for k in range(4):
                    step(0, k)
                with sp.Fori(1, T // 4 - 1) as i:
                    for k in range(4):
                        step(i, k)
                for k in range(4):
                    step(T // 4 - 1, k, has_s=k < 3)
                out(T - 1, 1)
                back(T - 1, 1)

            @block.tensor
            def _(pe):
                def score(t, pb, u, hh):
                    if not isinstance(t, int) or t > 0 or hh > 1:
                        pe.wait_ge(maxed, t * H2 + (hh - 1))
                    for c in range(2):
                        mm = nc.tensor.matmul(psS[:, hh % 2, c, :], Q9[0:R, pb, hh, u, c * P:(c + 1) * P],
                                              K9[0:R, pb, hh, u, :], start=True, stop=True)
                    mm.then_inc(scores, 1)

                def turn_max(t, b):
                    unit = t * 2 + b
                    pe.wait_ge(split, unit + 1)
                    pe.wait_ge(row_out, unit)
                    nc.tensor.transpose(psM[:, b, 0:P], parts[:, b, :], identb[:]).then_inc(turned, 1)

                def shift(t, pb, u, hh):
                    pair = t * 8 + hh // 2
                    if not isinstance(t, int) or t > 0 or hh > 2:
                        pe.wait_ge(exped, pair - 1)
                    for h in range(hh, hh + 2):
                        for c in range(KC):
                            mm = nc.tensor.matmul(psT[:, (hh // 2) % 2, h % 2, c, :],
                                                  K9[:, pb, h, u, c * P:(c + 1) * P],
                                                  Q9[:, pb, h, u, :], start=True, stop=True)
                    mm.then_inc(shifted, 1)

                def values(t, qd):
                    quad = t * QUADS + qd
                    pe.wait_ge(exped, t * 8 + 2 * qd + 2)
                    pe.wait_ge(v_in, t * 2 + qd // 2 + 1)
                    pe.wait_ge(o_out, quad)
                    for c in range(KC):
                        for g in range(4):
                            h = (qd * 4 + g) % NH0
                            mm = nc.tensor.matmul(psO[32 * g:32 * g + 32, qd % 2, :], V9[:, qd // 2, c, h, :],
                                                  E[:, qd % 2, g, c, :], start=(c == 0), stop=(c == KC - 1),
                                                  skip_group_check=True)
                    mm.then_inc(pv, 1)

                def step(i, k, has_s=True, has_t=True):
                    t = i * 4 + k
                    pb0, u0 = (k // 2) % 2, k % 2
                    pb1, u1 = ((k + 1) // 2) % 2, (k + 1) % 2
                    first_tile = isinstance(i, int) and i == 0 and k == 0
                    if has_s and k % 2 == 1:
                        pe.wait_ge(pair_in[pb1], (i + 1 + k // 2) * PAIR)
                    for b in range(2):
                        if has_t:
                            pe.wait_ge(row_in[b], t * 32 + 32)
                        for pr in range(4):
                            hh = b * NH0 + 2 * pr
                            if has_s:
                                score(t + 1, pb1, u1, hh)
                                score(t + 1, pb1, u1, hh + 1)
                            if pr == 1:
                                if b == 0:
                                    if not first_tile:
                                        turn_max(t, 1)
                                elif has_s:
                                    turn_max(t + 1, 0)
                            if has_t:
                                shift(t, pb0, u0, hh)
                                if pr % 2 == 1:
                                    qd = 2 * b + pr // 2
                                    if qd > 0:
                                        values(t, qd - 1)
                                    elif not first_tile:
                                        values(t - 1, QUADS - 1)

                pe.wait_ge(ready, 5)
                pe.wait_ge(pair_in[0], PAIR)
                for hh in range(H2):
                    score(0, 0, 0, hh)
                turn_max(0, 0)
                turn_max(0, 1)
                for k in range(4):
                    step(0, k)
                with pe.Fori(1, T // 4 - 1) as i:
                    for k in range(4):
                        step(i, k)
                for k in range(4):
                    step(T // 4 - 1, k, has_s=k < 3)
                values(T - 1, QUADS - 1)

            @block.scalar
            def _(act):
                def row(t, b):
                    unit = t * 2 + b
                    act.wait_ge(turned, unit + 1)
                    if not isinstance(t, int) or t > 0:
                        act.wait_ge(row_in[b], t * 32)
                    nc.scalar.copy(rows[:, b, :], psM[0:48, b, 0:P]).then_inc(row_out, 1)

                def exp(t, hh):
                    quad = t * QUADS + hh // 4
                    act.wait_ge(shifted, t * 8 + hh // 2 + 1)
                    if not isinstance(t, int) or t > 0 or hh > 7:
                        act.wait_ge(pv, quad - 1)
                    nc.scalar.activation(E[:, (hh // 4) % 2, hh % 4:hh % 4 + 2], psT[:, (hh // 2) % 2], ACT.Exp,
                                         scale=SCALE).then_inc(exped, 1)

                def leave(t, qd):
                    act.wait_ge(pv, t * QUADS + qd + 1)
                    if qd == 0 and (not isinstance(t, int) or t > 1):
                        act.wait_ge(to_dram, (t - 1) * 64)
                    par = leave.par
                    nc.scalar.copy(O[:, par, qd, :], psO[:, qd % 2, :]).then_inc(o_out, 1)

                def step(i, k, has_s=True, has_t=True):
                    t = i * 4 + k
                    first_tile = isinstance(i, int) and i == 0 and k == 0
                    for b in range(2):
                        for pr in range(4):
                            exp(t, b * NH0 + 2 * pr)
                            if pr == 1:
                                if b == 0:
                                    if not first_tile:
                                        row(t, 1)
                                elif has_s:
                                    row(t + 1, 0)
                            if pr % 2 == 1:
                                qd = 2 * b + pr // 2
                                if qd > 0:
                                    leave.par = k % 2
                                    leave(t, qd - 1)
                                elif not first_tile:
                                    leave.par = (k + 1) % 2
                                    leave(t - 1, QUADS - 1)

                row(0, 0)
                row(0, 1)
                for k in range(4):
                    step(0, k)
                with act.Fori(1, T // 4 - 1) as i:
                    for k in range(4):
                        step(i, k)
                for k in range(4):
                    step(T // 4 - 1, k, has_s=k < 3)
                leave.par = 1
                leave(T - 1, QUADS - 1)

            @block.vector
            def _(dve):
                def max_of(t, hh):
                    b = hh // NH0
                    if hh % NH0 == 0 and (not isinstance(t, int) or t > 0):
                        dve.wait_ge(split, t * 2 + b - 1)
                    dve.wait_ge(scores, t * H2 + hh + 1)
                    nc.vector.tensor_reduce(nmax[:, b, :, hh % NH0], psS[:, hh % 2], AX.X, ALU.max,
                                            negate=True).then_inc(maxed, 1)

                def invert(t, par, half):
                    dve.wait_ge(o_back[par], half * 32 + 32)
                    nc.vector.reciprocal(den[:, par], den[:, par]).then_inc(recip, 1)

                def step(i, k, has_s=True, has_t=True):
                    t = i * 4 + k
                    past = not isinstance(i, int) or i > 0
                    if has_s:
                        for hh in range(H2):
                            max_of(t + 1, hh)
                    if past or k > 0:
                        invert(t - 1, (k + 1) % 2, i * 2 + (k - 1) // 2)

                nc.vector.memset(K9[64:P], 1.0).then_inc(ones_set, 1)
                for hh in range(H2):
                    max_of(0, hh)
                for k in range(4):
                    step(0, k)
                with dve.Fori(1, T // 4 - 1) as i:
                    for k in range(4):
                        step(i, k)
                for k in range(4):
                    step(T // 4 - 1, k, has_s=k < 3)
                invert(T - 1, 1, T // 2 - 1)

def pipeline(engine, front, back):
    front(0, 0)
    front(1, 1)
    back(0, 0)
    with engine.Fori(0, NG // 2 - 1) as h:
        front(h * 2 + 2, 0)
        back(h * 2 + 1, 1)
        front(h * 2 + 3, 1)
        back(h * 2 + 2, 0)
    back(NG - 1, 1)

def rounds(engine, step, last):
    step(0, 0)
    step(1, 1)
    with engine.Fori(1, NG // 2 - 1) as h:
        step(h * 2, 0)
        step(h * 2 + 1, 1)
    for g in range(NG - 2, last + 1):
        step(g, g % 2)

def is_group(g):
    return not isinstance(g, int) or 0 <= g < NG

def later(g, rounds):
    return not isinstance(g, int) or g >= rounds

class Norm:

    def __init__(self, nc, s, X, eps=LN_EPS):
        self.nc, self.X, self.eps_value = nc, X, eps
        self.stats = s.sb("stats", [P, G, 6])
        self.mv = s.sb("mv", [P, G, 2])
        self.veps = s.sb("veps", [P, G])
        self.rstd = s.sb("rstd", [P, G])
        self.mhalf = s.sb("mhalf", [P, G])
        self.eps = s.sb("eps", [P, G])
        self.set = s.sem("norm_set")
        self.stats_done, self.veps_done = s.sem("stats_done"), s.sem("veps_done")
        self.rstd_done, self.normed = s.sem("rstd_done"), s.sem("normed")

    def constants(self, pool):
        self.nc.gpsimd.memset(self.mhalf[:], -0.5).then_inc(self.set, 1)
        self.nc.gpsimd.memset(self.eps[:], self.eps_value).then_inc(self.set, 1)
        pool.wait_ge(self.set, 2)

    def on_pool(self, pool, g):
        pool.wait_ge(self.stats_done, g * G + G)
        self.nc.gpsimd.tensor_tensor(self.veps[:], self.mv[:, :, 1], self.eps[:], ALU.add).then_inc(self.veps_done, 1)
        pool.wait_ge(self.veps_done, g + 1)
        self.nc.gpsimd.tensor_tensor(self.rstd[:], self.veps[:], self.mhalf[:], ALU.pow).then_inc(self.rstd_done, 1)

    def on_vector(self, dve, g, Z):
        self.take_stats(dve, g)
        self.normalise(dve, g, Z)

    def take_stats(self, dve, g):
        for j in range(G):
            self.nc.vector.bn_stats(self.stats[:, j, :], self.X[:, g * G + j, :])
        dve.drain()
        for j in range(G):
            self.nc.vector.bn_aggr(self.mv[:, j, :], self.stats[:, j, :]).then_inc(self.stats_done, 1)

    def normalise(self, dve, g, Z):
        dve.wait_ge(self.rstd_done, g + 1)
        dve.wait_ge(self.stats_done, g * G + G)
        for j in range(G):
            self.nc.vector.tensor_scalar(Z[:, j, :], self.X[:, g * G + j, :], self.mv[:, j, 0:1],
                                         self.rstd[:, j:j + 1], ALU.subtract, ALU.mult).then_inc(self.normed, 1)

def selected_ffn(nc, io, X, ident):
    FC = FF // P
    SL = 2 * KEEP
    with ExitStack() as ctx:
        s = Scope(nc, ctx, "sffn")
        norm = Norm(nc, s, X)
        W1 = s.sb("W1", [P, KC, FF])
        W2 = s.sb("W2", [P, FC, D])
        b1 = s.sb("b1", [P, FC])
        b2 = s.sb("b2", [P, D])
        wr = s.sb("wr", [P, D])
        br = s.sb("br", [P, 1])
        Z = s.sb("Z", [P, 2, G, D])
        zw = s.sb("zw", [P, D])
        sc = s.sb("sc", [P, 2, G])
        same = s.sb("same", [P, P])
        own = s.sb("own", [P, L])
        before = s.sb("before", [P, L])
        slot = s.sb("slot", [P, SL])
        diag = s.sb("diag", [P, G, L])
        work = s.sb("work", [P, 3, G, L])
        mine = s.sb("mine", [P, G])
        rank = s.sb("rank", [P, G])
        pick = s.sb("pick", [P, 2, G, SL])
        XS = s.sb("XS", [P, KC, G * SL])
        PT = s.sb("PT", [P, G, P])
        H = s.sb("H", [P, FC, G * SL])
        OS = s.sb("OS", [P, 2, D])
        psR = s.ps("psR", [P, G, L + L])
        psG = s.ps("psG", [P, KC, G * SL])
        psP = s.ps("psP", [P, 4, P])
        psH = s.ps("psH", [P, 2, 2, G * SL])
        psO = s.ps("psO", [P, 2, D])
        psX = s.ps("psX", [P, G, D])
        w_in, ready = s.sem("w_in"), s.sem("ready")
        steps, diag_done, rows_done, pick_done = (s.sem(x) for x in ("steps", "diag_done", "rows_done", "pick_done"))
        gathered, turned, xs_done, pt_done = (s.sem(x) for x in ("gathered", "turned", "xs_done", "pt_done"))
        hidden, gelued, put, os_done, scattered, x_done = (
            s.sem(x) for x in ("hidden", "gelued", "put", "os_done", "scattered", "x_done"))
        PER = 12

        with nc.Block() as block:

            @block.sync
            def _(sp):
                sp.dma_start(W1[:], io["L0_ffn_w1"].rearrange("(k p) f -> p k f", p=P)).then_inc(w_in, 16)
                sp.dma_start(W2[:], io["L0_ffn_w2"].rearrange("(k p) d -> p k d", p=P)).then_inc(w_in, 16)
                with nc.allow_non_contiguous_dma(reason="one column of biases for each chunk"):
                    sp.dma_start(b1[:], io["L0_ffn_b1"].rearrange("(k p) -> p k", p=P)).then_inc(w_in, 16)
                sp.dma_start(b2[:], spread(io["L0_ffn_b2"], 0, P)).then_inc(w_in, 16)
                sp.dma_start(wr[:], spread(io["L0_ffn_w_r"], 0, P)).then_inc(w_in, 16)
                sp.dma_start(br[:], spread(io["L0_ffn_b_r"], 0, P)).then_inc(w_in, 16)
                sp.wait_ge(w_in, 96)

            @block.gpsimd
            def _(pool):
                step = Steps(pool, ready, 14)
                select = lambda out, op, fill, base, cm, pattern: step(nc.gpsimd.affine_select(
                    out=out, in_=out, compare_op=op, fill=fill, base=base, pattern=pattern, channel_multiplier=cm))
                step(nc.gpsimd.memset(same[:], 1.0))
                select(same[0:L, :], ALU.is_ge, 0.0, L - 1, 0, [[-1, P]])
                select(same[L:P, :], ALU.is_ge, 0.0, -L, 0, [[1, P]])
                step(nc.gpsimd.memset(own[:], 0.0))
                select(own[0:L, :], ALU.not_equal, 1.0, 0, 1, [[-1, L]])
                select(own[L:P, :], ALU.not_equal, 1.0, 0, 1, [[-1, L]])
                step(nc.gpsimd.memset(before[:], 1.0))
                select(before[0:L, :], ALU.is_gt, 0.0, 0, 1, [[-1, L]])
                select(before[L:P, :], ALU.is_gt, 0.0, 0, 1, [[-1, L]])
                step(nc.gpsimd.iota(slot[:], pattern=[[0, 2], [1, KEEP]], base=0, channel_multiplier=0,
                                    allow_small_or_imprecise_dtypes=True))
                step(nc.gpsimd.memset(slot[0:L, KEEP:], -1.0))
                step(nc.gpsimd.memset(slot[L:P, 0:KEEP], -1.0))
                step(nc.gpsimd.memset(PT[0:L, :, :], 0.0))
                step(nc.gpsimd.memset(PT[L:P, :, :], 0.0))
                step.end()
                norm.constants(pool)
                pipeline(pool, lambda g, w: norm.on_pool(pool, g), lambda g, w: None)

            @block.vector
            def _(dve):
                def front(g, w):
                    if later(g, 2):
                        dve.wait_ge(gathered, g - 1)
                        dve.wait_ge(turned, g - 1)
                    norm.on_vector(dve, g, Z[:, w])
                    step = Steps(dve, steps, PER, g)
                    dve.wait_ge(norm.normed, g * G + G)
                    dve.wait_ge(w_in, 96)
                    dve.wait_ge(ready, 14)
                    for j in range(G):
                        step(nc.vector.tensor_tensor_reduce(zw[:], Z[:, w, j, :], wr[:], 1.0, 0.0, ALU.mult, ALU.add,
                                                            sc[:, 0, j:j + 1]))
                    step(nc.vector.tensor_scalar(sc[:, 1], sc[:, 0], br[:, 0:1], None, ALU.add))
                    nc.vector.tensor_tensor(diag[:], spread(own[:], 1, G), spread(sc[:, 1], 2, L),
                                            ALU.mult).then_inc(diag_done, 1)
                    dve.wait_ge(rows_done, g + 1)
                    R = psR[:, :, 0:L]
                    step(nc.vector.tensor_tensor(work[:, 0], R, spread(own[:], 1, G), ALU.mult))
                    step(nc.vector.tensor_reduce(mine[:], work[:, 0], AX.X, ALU.add))
                    step(nc.vector.tensor_tensor(work[:, 1], R, spread(mine[:], 2, L), ALU.is_equal))
                    step(nc.vector.tensor_tensor(work[:, 2], work[:, 1], spread(before[:], 1, G), ALU.mult))
                    step(nc.vector.tensor_tensor(work[:, 0], R, spread(mine[:], 2, L), ALU.is_gt))
                    step(nc.vector.tensor_tensor(work[:, 1], work[:, 0], work[:, 2], ALU.add))
                    step(nc.vector.tensor_reduce(rank[:], work[:, 1], AX.X, ALU.add))
                    nc.vector.tensor_tensor(pick[:, w], spread(slot[:], 1, G), spread(rank[:], 2, SL),
                                            ALU.is_equal).then_inc(pick_done, 1)
                    step.end()

                def back(g, w):
                    dve.wait_ge(put, g + 1)
                    dve.wait_ge(w_in, 96)
                    dve.wait_ge(scattered, g)
                    nc.vector.tensor_tensor(OS[:], psO[:], spread(b2[:], 1, 2), ALU.add).then_inc(os_done, 1)
                    dve.wait_ge(scattered, g + 1)
                    nc.vector.tensor_tensor(X[:, bass.ds(g * G, G), :], X[:, bass.ds(g * G, G), :], psX[:],
                                            ALU.add).then_inc(x_done, 1)

                pipeline(dve, front, back)

            @block.tensor
            def _(pe):
                def front(g, w):
                    pe.wait_ge(diag_done, g + 1)
                    pe.wait_ge(pick_done, g)
                    nc.tensor.matmul(psR[:, :, 0:L], same[:], diag[:], start=True, stop=True).then_inc(rows_done, 1)

                def gather_and_widen(g, w):
                    pe.wait_ge(pick_done, g + 1)
                    pe.wait_ge(xs_done, g)
                    for k in range(KC):
                        for j in range(G):
                            mm = nc.tensor.matmul(psG[:, k, j * SL:(j + 1) * SL], Z[:, w, j, k * P:(k + 1) * P],
                                                  pick[:, w, j, :], start=True, stop=True)
                    mm.then_inc(gathered, 1)
                    pe.wait_ge(pt_done, g * 2)
                    for jj in range(2):
                        mm = nc.tensor.transpose(psP[:, jj, :], pick[:, w, 2 * jj:2 * jj + 2, :].rearrange(
                            "p j s -> p (j s)"), ident[:])
                    mm.then_inc(turned, 1)
                    pe.wait_ge(xs_done, g + 1)
                    pe.wait_ge(w_in, 96)
                    for f in range(FC // 2):
                        if later(g, 1) or f > 1:
                            pe.wait_ge(gelued, g * FC + 2 * f - 2)
                        for ff in range(2):
                            c = 2 * f + ff
                            for k in range(KC):
                                mm = nc.tensor.matmul(psH[:, f % 2, ff, :], W1[:, k, c * P:(c + 1) * P], XS[:, k, :],
                                                      start=(k == 0), stop=(k == KC - 1))
                        mm.then_inc(hidden, 1)

                def narrow_and_scatter(g):
                    pe.wait_ge(gelued, g * FC + FC)
                    pe.wait_ge(os_done, g)
                    for b in range(2):
                        for c in range(FC):
                            mm = nc.tensor.matmul(psO[:, b, :], H[:, c, b * P:(b + 1) * P], W2[:, c, :],
                                                  start=(c == 0), stop=(c == FC - 1))
                    mm.then_inc(put, 1)
                    pe.wait_ge(os_done, g + 1)
                    pe.wait_ge(pt_done, g * 2 + 2)
                    pe.wait_ge(x_done, g)
                    for j in range(G):
                        mm = nc.tensor.matmul(psX[:, j, :], PT[:, j, :], OS[:, j // 2, :], start=True, stop=True)
                    mm.then_inc(scattered, 1)

                def step(g, w):
                    if is_group(g - 1):
                        gather_and_widen(g - 1, 1 - w)
                    if is_group(g):
                        front(g, w)
                    if is_group(g - 1):
                        narrow_and_scatter(g - 1)

                pe.wait_ge(ready, 14)
                rounds(pe, step, NG)

            @block.scalar
            def _(act):
                def back(g, w):
                    act.wait_ge(gathered, g + 1)
                    nc.scalar.copy(XS[:], psG[:]).then_inc(xs_done, 1)
                    act.wait_ge(turned, g + 1)
                    act.wait_ge(scattered, g)
                    nc.scalar.copy(PT[0:SL, 0:G:2, :], psP[0:SL, 0:2, :]).then_inc(pt_done, 1)
                    nc.scalar.copy(PT[SL:P, 1:G:2, :], psP[SL:P, 0:2, :]).then_inc(pt_done, 1)
                    for c in range(FC):
                        act.wait_ge(hidden, g * (FC // 2) + c // 2 + 1)
                        if c == 0:
                            act.wait_ge(put, g)
                        nc.scalar.activation(H[:, c, :], psH[:, (c // 2) % 2, c % 2, :], ACT.Gelu_apprx_tanh,
                                             bias=b1[:, c:c + 1]).then_inc(gelued, 1)

                act.wait_ge(w_in, 96)
                act.wait_ge(ready, 14)
                pipeline(act, lambda g, w: None, back)

HC = NH // KC
NP = NH // 2
VW = DH + 1
BG = 2 * G
HG = G * P // 2

def turn_weights(nc, name, ident, matrices, loads=()):
    with ExitStack() as ctx:
        s = Scope(nc, ctx, name)
        M = len(matrices)
        W = s.sb("W", [P, M, KC, D])
        psT = s.ps("psT", [P, M, KC, D])
        w_in, turned, taken, side_in = (s.sem(x) for x in ("w_in", "turned", "taken", "side_in"))
        with nc.Block() as block:

            @block.sync
            def _(sp):
                for m, (dram, WT) in enumerate(matrices):
                    sp.dma_start(W[:, m], dram.rearrange("(k p) d -> p k d", p=P)).then_inc(w_in, 16)
                sp.wait_ge(w_in, 16 * M)
                with nc.allow_non_contiguous_dma(reason="one column of biases for each chunk"):
                    for tile, source in loads:
                        sp.dma_start(tile[:], source).then_inc(side_in, 16)
                if loads:
                    sp.wait_ge(side_in, 16 * len(loads))

            @block.tensor
            def _(pe):
                pe.wait_ge(w_in, 16 * M)
                for m in range(M):
                    for k in range(KC):
                        for c in range(KC):
                            mm = nc.tensor.transpose(psT[:, m, k, c * P:(c + 1) * P], W[:, m, c, k * P:(k + 1) * P],
                                                     ident[:])
                    mm.then_inc(turned, 1)

            @block.scalar
            def _(act):
                for m, (dram, WT) in enumerate(matrices):
                    act.wait_ge(turned, m + 1)
                    nc.scalar.copy(WT[:], psT[:, m]).then_inc(taken, 1)

class Heads:

    def __init__(self, nc, s, ident, KX, VB):
        self.nc, self.ident, self.KX, self.VB = nc, ident, KX, VB
        self.QT = s.sb("QT", [P, 2, KC, G * P])
        self.PB = s.sb("PB", [P, 2, NH, L])
        self.PT = s.sb("PT", [P, 2, NP, P])
        self.psS = s.ps("psS", [P, KC, HC * L])
        self.psP = s.ps("psP", [P, 2, NP // 2, P])
        self.psO = s.ps("psO", [P, 512])
        self.set = s.sem("h_set")
        self.kx_in = [s.sem(f"kx_in{w}") for w in range(2)]
        self.scored, self.s_taken, self.weighted, self.turned, self.pt_done, self.valued, self.o_taken = (
            s.sem(x) for x in ("scored", "s_taken", "weighted", "p_turned", "pt_done", "valued", "o_taken"))

    def zeros_and_ones(self, pool):
        gp = self.nc.gpsimd
        gp.memset(self.VB[:], 0.0).then_inc(self.set, 1)
        pool.wait_ge(self.set, 1)
        gp.memset(self.VB[0:L, :, :, :, 0, DH:], 1.0).then_inc(self.set, 1)
        gp.memset(self.VB[L:P, :, :, :, 1, DH:], 1.0).then_inc(self.set, 1)
        pool.wait_ge(self.set, 3)
        gp.memset(self.KX[:, 0], 0.0).then_inc(self.set, 1)
        pool.wait_ge(self.set, 4)

    def expand(self, sp, g, keys, free):
        for half in range(2):
            if free[half] is not None:
                sp.wait_ge(self.scored, free[half])
            for c in range(KC):
                for h in range(HC):
                    rows = slice(h * DH, (h + 1) * DH)
                    sp.dma_start(self.KX[rows, half, c, h, :], keys(rows, c, half)).then_inc(self.kx_in[half], 16)

    def free_after(self, sp, g):
        return [held(sp, g * G - 2) if later(g, 1) else None, held(sp, g * G)]

    def scores(self, pe, g, w, j):
        pe.wait_ge(self.s_taken, g * G + j)
        if j % 2 == 0:
            pe.wait_ge(self.kx_in[j // 2], g * 256 + 256)
        for c in range(KC):
            for b in range(2):
                at, key = (2 * j + b) * L, (2 * (j % 2) + b) * L
                mm = self.nc.tensor.matmul(self.psS[b * L:(b + 1) * L, c, :], self.QT[:, w, c, at:at + L],
                                           self.KX[:, j // 2, c, :, key:key + L], start=True, stop=True,
                                           skip_group_check=True)
        mm.then_inc(self.scored, 1)

    def turn(self, pe, g, j):
        t = g * G + j
        pe.wait_ge(self.weighted, t + 1)
        pe.wait_ge(self.pt_done, t * 2)
        for i in range(NP):
            mm = self.nc.tensor.transpose(self.psP[:, i // (NP // 2), i % (NP // 2), :],
                                          self.PB[:, j % 2, 2 * i:2 * i + 2, :].rearrange("p h t -> p (h t)"),
                                          self.ident[:])
            if i % (NP // 2) == NP // 2 - 1:
                mm.then_inc(self.turned, 1)

    def copy_turned(self, act, g, j):
        t = g * G + j
        for half in range(2):
            act.wait_ge(self.turned, 2 * t + half + 1)
            if later(g, 1) or j > 1:
                act.wait_ge(self.valued, t - 1)
            self.nc.scalar.copy(self.PT[:, j % 2, half * (NP // 2):(half + 1) * (NP // 2), :],
                                self.psP[:, half]).then_inc(self.pt_done, 1)

    def values(self, pe, g, w, j):
        t = g * G + j
        pe.wait_ge(self.pt_done, 2 * t + 2)
        pe.wait_ge(self.o_taken, t)
        for i in range(NP):
            for b in range(2):
                mm = self.nc.tensor.matmul(self.psO[b * L:(b + 1) * L, i * 2 * VW:(i + 1) * 2 * VW],
                                           self.PT[:, j % 2, i, b * L:(b + 1) * L],
                                           self.VB[:, w, 2 * j + b, i].rearrange("p h d -> p (h d)"), start=True,
                                           stop=True, skip_group_check=True)
        mm.then_inc(self.valued, 1)

    def out(self):
        return self.psO[:, 0:NH * VW].rearrange("p (h d) -> p h d", d=VW)

def gated_attention(nc, io, X, CT, ident, identb, KX, VB):
    NG2 = 2 * NH
    with ExitStack() as ctx:
        s = Scope(nc, ctx, "gatt")
        norm = Norm(nc, s, X)
        heads = Heads(nc, s, ident, KX, VB)
        heads.s_taken = heads.weighted
        WZ, WK_, WV_, WC = (s.sb(x, [P, KC, NG2]) for x in ("WZ", "WK", "WV", "WC"))
        gbias = s.sb("gbias", [P, NG2])
        lscale = s.sb("lscale", [P, D])
        same, tri = s.sb("same", [P, P]), s.sb("tri", [P, P])
        own = s.sb("own", [P, L])
        mask = s.sb("mask", [P, HC, L], BF16)
        one = s.sb("one", [P, 1])
        Z = s.sb("Z", [P, G, D])
        CG = s.sb("CG", [P, KC, G * P])
        V2 = s.sb("V2", [P, BG, D])
        gates = s.sb("gates", [P, G, NG2])
        fw = s.sb("fw", [P, 5, G, NH])
        cum = s.sb("cum", [P, 2, G, NH])
        a = s.sb("a", [P, 2, G, NH])
        DA = s.sb("DA", [P, 2, NH, L])
        DB = s.sb("DB", [P, 2, NH, L])
        mx = s.sb("mx", [P, 2, G, NH])
        OG = s.sb("OG", [P, 2, G, NH, VW])
        cen = s.sb("cen", [P, G, NH, DH])
        sq = s.sb("sq", [P, G, NH, DH])
        tw = s.sb("tw", [P, 13, G, NH])
        psA = s.ps("psA", [P, 2, HC * L])
        psG = s.ps("psG", [P, 512])
        (w_in, ready, wc_steps, cg_in, v_in, used, g_used, taken, v_copied, f_steps, f_exp, f_ln, da_done,
         a_spread, maxed, a_taken, d_done, t_steps, e_done, sq_done, v_ln, r_done, scaled, x_done, kx_set) = (
             s.sem(x) for x in (
                 "w_in", "ready", "wc_steps", "cg_in", "v_in", "used", "g_used", "taken", "v_copied", "f_steps",
                 "f_exp", "f_ln", "da_done", "a_spread", "maxed", "a_taken", "d_done", "t_steps", "e_done",
                 "sq_done", "v_ln", "r_done", "scaled", "x_done", "kx_set"))
        READY = 15
        FPER, TPER = 6, 19
        TAIL_AT = (0, 1, 3)

        with nc.Block() as block:

            @block.sync
            def _(sp):
                with nc.allow_non_contiguous_dma(reason="16 gates for each feature"):
                    for part, W in enumerate((WZ, WK_, WV_)):
                        for n, name in enumerate(("Wi", "Wf")):
                            sp.dma_start(W[:, :, n * NH:(n + 1) * NH],
                                         io["L1_xattn_" + name][part * D:(part + 1) * D, :].rearrange(
                                             "(k p) h -> p k h", p=P)).then_inc(w_in, 16)
                sp.dma_start(gbias[:, 0:NH], spread(io["L1_xattn_bi"], 0, P)).then_inc(w_in, 16)
                sp.dma_start(gbias[:, NH:NG2], spread(io["L1_xattn_bf"], 0, P)).then_inc(w_in, 16)
                sp.dma_start(lscale[:], spread(io["L1_xattn_ln_scale"], 0, P)).then_inc(w_in, 16)
                sp.wait_ge(w_in, 144)
                sp.wait_ge(heads.set, 4)
                sp.wait_ge(kx_set, 1)
                c_dram = io["ctx_2048"].rearrange("b t d -> t b d")

                def context(at):
                    sp.dma_start(CG[:], CT[:, :, bass.ds(at, G * P)]).then_inc(cg_in, 16)

                def rows_of_context(b0):
                    for hp in range(2):
                        sp.dma_start(V2[hp * L:(hp + 1) * L], c_dram[:, bass.ds(b0, BG), :]).then_inc(v_in, 16)

                def step(g, w):
                    if not is_group(g):
                        return
                    starts = [held(sp, g * (G * P)), held(sp, g * (G * P) + HG)]
                    free = heads.free_after(sp, g)
                    if is_group(g + 1):
                        at, b0, gs, vs = (held(sp, v) for v in (
                            g * (G * P) + G * P, g * BG + BG, g * 2 + 1, g * 2 + 2))
                        sp.wait_ge(g_used, gs)
                        context(at)
                    heads.expand(sp, g, lambda rows, c, half: CT[rows, c, bass.ds(starts[half], HG)], free)
                    if is_group(g + 1):
                        sp.wait_ge(v_copied, vs)
                        rows_of_context(b0)

                context(0)
                rows_of_context(0)
                rounds(sp, step, NG)

            @block.gpsimd
            def _(pool):
                gp = nc.gpsimd
                heads.zeros_and_ones(pool)
                norm.constants(pool)
                step = Steps(pool, ready, READY)
                select = lambda out, op, fill, base, cm, pattern: step(gp.affine_select(
                    out=out, in_=out, compare_op=op, fill=fill, base=base, pattern=pattern, channel_multiplier=cm))
                step(gp.memset(same[:], 1.0))
                select(same[0:L, :], ALU.is_ge, 0.0, L - 1, 0, [[-1, P]])
                select(same[L:P, :], ALU.is_ge, 0.0, -L, 0, [[1, P]])
                step(gp.memset(tri[:], 1.0))
                select(tri[0:L, :], ALU.is_ge, 0.0, L - 1, 0, [[-1, P]])
                select(tri[0:L, :], ALU.is_ge, 0.0, 0, -1, [[1, P]])
                select(tri[L:P, :], ALU.is_ge, 0.0, -L, -1, [[1, P]])
                step(gp.memset(own[:], 0.0))
                select(own[0:L, :], ALU.not_equal, 1.0, 0, 1, [[-1, L]])
                select(own[L:P, :], ALU.not_equal, 1.0, 0, 1, [[-1, L]])
                step(gp.memset(mask[:], 0.0))
                select(mask[0:L], ALU.is_ge, -BIG, 0, 1, [[0, HC], [-1, L]])
                select(mask[L:P], ALU.is_ge, -BIG, 0, 1, [[0, HC], [-1, L]])
                step(gp.memset(one[:], 1.0))
                step(gp.memset(OG[:], 0.0))
                step.end()
                pool.wait_ge(w_in, 144)

                def spread_of(g, w, i):
                    t = g * G + i
                    pool.wait_ge(f_steps, g * FPER + FPER)
                    if later(g, 1) or i > 1:
                        pool.wait_ge(a_spread, t - 1)
                    gp.tensor_tensor(DA[:, i % 2], spread(own[:], 1, NH), spread(a[:, w, i], 2, L),
                                     ALU.mult).then_inc(da_done, 1)

                flat = cen[:].rearrange("p j h d -> p j (h d)")

                def add(g):
                    pool.wait_ge(t_steps, g * TPER + TPER)
                    gp.tensor_tensor(flat, flat, spread(lscale[:], 1, G), ALU.mult).then_inc(scaled, 1)
                    pool.wait_ge(scaled, g + 1)
                    xs = X[:, bass.ds(g * G, G), :]
                    gp.tensor_tensor(xs, xs, flat, ALU.add).then_inc(x_done, 1)

                def step(g, w):
                    if is_group(g - 1):
                        spread_of(g - 1, 1 - w, 2)
                        spread_of(g - 1, 1 - w, 3)
                    if is_group(g + 1):
                        norm.on_pool(pool, g + 1)
                    if is_group(g):
                        spread_of(g, w, 0)
                        spread_of(g, w, 1)
                    if is_group(g - 2):
                        add(g - 2)

                norm.on_pool(pool, 0)
                rounds(pool, step, NG + 1)

            @block.vector
            def _(dve):
                v = nc.vector
                v.memset(KX[:, 1], 0.0).then_inc(kx_set, 1)
                dve.wait_ge(w_in, 144)
                v.tensor_tensor(WC[:], WK_[:], WV_[:], ALU.add).then_inc(wc_steps, 1)
                dve.wait_ge(heads.set, 4)
                dve.wait_ge(ready, READY)

                def front(g, w, i):
                    step = Steps(dve, f_steps, FPER, g)
                    f = gates[:, :, NH:NG2]
                    if i == 1:
                        dve.wait_ge(g_used, g * 2 + 1)
                        step(v.tensor_tensor(gates[:], psG[:, 0:G * NG2].rearrange("p (j n) -> p j n", n=NG2),
                                             spread(gbias[:], 1, G), ALU.add))
                        step(v.scalar_tensor_tensor(fw[:, 0], f, -1.0, f, ALU.mult, ALU.min))
                        step(v.tensor_scalar(fw[:, 3], f, 0.0, None, ALU.min))
                    step.n = 3
                    if i == 3:
                        dve.wait_ge(f_ln, g + 1)
                        step(v.tensor_tensor(fw[:, 4], fw[:, 3], fw[:, 2], ALU.subtract))
                    step.n = 4
                    if i == 4:
                        dve.wait_ge(g_used, g * 2 + 2)
                        step(v.tensor_copy(cum[:, w].rearrange("p j h -> p (j h)"), psG[:, 0:G * NH]))
                        step(v.tensor_tensor(a[:, w], gates[:, :, 0:NH], cum[:, w], ALU.subtract))
                        step.end()

                def max_and_shift(g, w, i):
                    t = g * G + i
                    A = psA[:].rearrange("p c (h t) -> p (c h) t", t=L)
                    dve.wait_ge(a_spread, t + 1)
                    v.tensor_reduce(mx[:, w, i], A, AX.X, ALU.max).then_inc(maxed, 1)
                    dve.wait_ge(maxed, t + 1)
                    v.tensor_tensor(DB[:, i % 2], A, spread(mx[:, w, i], 2, L), ALU.subtract).then_inc(a_taken, 1)

                def weigh(g, i):
                    t = g * G + i
                    p = i % 2
                    dve.wait_ge(heads.scored, t + 1)
                    dve.wait_ge(d_done, t + 1)
                    if later(g, 1) or i > 1:
                        dve.wait_ge(heads.turned, 2 * t - 2)
                    v.scalar_tensor_tensor(heads.PB[:, p], heads.psS[:].rearrange("p c (h t) -> p (c h) t", t=L),
                                           float(DH) ** -0.5, DB[:, p], ALU.mult, ALU.mult).then_inc(
                                               heads.weighted, 1)

                def tail(g, w, part):
                    step = Steps(dve, t_steps, TPER, g)
                    O = OG[:, w, :, :, 0:DH]
                    if part == 0:
                        dve.wait_ge(heads.o_taken, g * G + G)
                        step(v.tensor_tensor(tw[:, 0], mx[:, w], cum[:, w], ALU.add))
                        step(v.tensor_reduce(tw[:, 1], O, AX.X, ALU.add))
                        step(v.tensor_scalar(tw[:, 2], tw[:, 1], 1.0 / DH, None, ALU.mult))
                        dve.wait_ge(x_done, g)
                        step(v.tensor_tensor(cen[:], O, spread(tw[:, 2], 3, DH), ALU.subtract))
                    step.n = 4
                    if part == 1:
                        dve.wait_ge(e_done, g + 1)
                        S = OG[:, w, :, :, DH]
                        step(v.scalar_tensor_tensor(tw[:, 4], S, -1.0, S, ALU.mult, ALU.max))
                        step(v.tensor_tensor(tw[:, 5], tw[:, 4], tw[:, 3], ALU.max))
                        step(v.tensor_scalar(tw[:, 6], tw[:, 5], 1e-6, None, ALU.add))
                        step(v.reciprocal(tw[:, 7], tw[:, 6]))
                        step(v.tensor_tensor(tw[:, 10], tw[:, 7], tw[:, 7], ALU.mult))
                        dve.wait_ge(sq_done, g + 1)
                        step(v.tensor_reduce(tw[:, 11], sq[:], AX.X, ALU.add))
                        step(v.tensor_tensor(tw[:, 12], tw[:, 10], tw[:, 11], ALU.mult))
                        step(v.tensor_scalar(tw[:, 1], tw[:, 12], 1.0 / DH, None, ALU.mult))
                        step(v.tensor_scalar(tw[:, 8], tw[:, 1], 1e-6, None, ALU.add))
                    step.n = 13
                    if part == 2:
                        dve.wait_ge(r_done, g + 1)
                        step(v.tensor_tensor(tw[:, 4], tw[:, 9], tw[:, 9], ALU.mult))
                        step(v.tensor_tensor(tw[:, 5], tw[:, 4], tw[:, 8], ALU.mult))
                        step(v.tensor_scalar(tw[:, 6], tw[:, 5], -0.5, 1.5, ALU.mult, ALU.add))
                        step(v.tensor_tensor(tw[:, 11], tw[:, 6], tw[:, 9], ALU.mult))
                        step(v.tensor_tensor(tw[:, 10], tw[:, 11], tw[:, 7], ALU.mult))
                        step(v.tensor_tensor(cen[:], cen[:], spread(tw[:, 10], 3, DH), ALU.mult))
                        step.end()

                def step(g, w):
                    for i in range(G + 2):
                        if is_group(g - 1) and 1 <= i < G:
                            max_and_shift(g - 1, 1 - w, i)
                        if is_group(g) and i == G + 1:
                            max_and_shift(g, w, 0)
                        if is_group(g) and i in (1, 3, 4):
                            front(g, w, i)
                        if is_group(g - 1) and 1 <= i <= G:
                            weigh(g - 1, i - 1)
                        if is_group(g - 2) and i in TAIL_AT:
                            tail(g - 2, w, TAIL_AT.index(i))
                        if is_group(g + 1) and i == 2:
                            norm.take_stats(dve, g + 1)
                        if is_group(g + 1) and i == 4:
                            dve.wait_ge(used, g * 2 + 2)
                            norm.normalise(dve, g + 1, Z)

                norm.on_vector(dve, 0, Z)
                rounds(dve, step, NG + 1)

            @block.tensor
            def _(pe):
                pe.wait_ge(heads.set, 4)
                pe.wait_ge(ready, READY)
                pe.wait_ge(w_in, 144)
                pe.wait_ge(wc_steps, 1)

                def z_turned(g):
                    pe.wait_ge(norm.normed, g * G + G)
                    pe.wait_ge(f_steps, g * FPER)
                    for k in range(KC):
                        pe.wait_ge(taken, g * 2 + k)
                        for j in range(G):
                            mm = nc.tensor.transpose(psG[:, j * P:(j + 1) * P], Z[:, j, k * P:(k + 1) * P], ident[:])
                        mm.then_inc(used, 1)

                def gates_of(g, w):
                    pe.wait_ge(taken, g * 2 + 2)
                    pe.wait_ge(cg_in, g * 16 + 16)
                    for j in range(G):
                        tile = slice(j * P, (j + 1) * P)
                        for n, (src, W) in enumerate([(heads.QT[:, w, k, tile], WZ[:, k, :]) for k in range(KC)]
                                                     + [(CG[:, k, tile], WC[:, k, :]) for k in range(KC)]):
                            mm = nc.tensor.matmul(psG[:, j * NG2:(j + 1) * NG2], src, W, start=(n == 0),
                                                  stop=(n == 2 * KC - 1))
                    mm.then_inc(g_used, 1)

                def running_sums(g):
                    pe.wait_ge(f_steps, g * FPER + 4)
                    nc.tensor.matmul(psG[:, 0:G * NH], tri[:], fw[:, 4].rearrange("p j h -> p (j h)"), start=True,
                                     stop=True).then_inc(g_used, 1)

                def spread_a(g, i):
                    t = g * G + i
                    pe.wait_ge(da_done, t + 1)
                    pe.wait_ge(a_taken, t)
                    for half in range(2):
                        nc.tensor.matmul(psA[:, half, :], same[:],
                                         DA[:, i % 2, half * HC:(half + 1) * HC, :].rearrange("p h t -> p (h t)"),
                                         start=True, stop=False)
                        mm = nc.tensor.matmul(psA[:, half, :], identb[:], mask[:].rearrange("p h t -> p (h t)"),
                                              start=False, stop=True)
                    mm.then_inc(a_spread, 1)

                def step(g, w):
                    bg, bw = g - 1, 1 - w
                    for i in range(G + 2):
                        if is_group(bg) and 1 <= i < G:
                            spread_a(bg, i)
                        if is_group(bg) and i >= 2:
                            heads.turn(pe, bg, i - 2)
                        if i == G + 1:
                            if is_group(g + 1):
                                z_turned(g + 1)
                            if is_group(g):
                                spread_a(g, 0)
                            if is_group(g + 1):
                                gates_of(g + 1, 1 - w)
                        if is_group(g) and i == 4:
                            running_sums(g)
                        if is_group(bg) and 1 <= i <= G:
                            heads.scores(pe, bg, bw, i - 1)
                        if is_group(bg) and i >= 2:
                            if i == 2:
                                pe.wait_ge(v_copied, bg * 2 + 2)
                            heads.values(pe, bg, bw, i - 2)

                z_turned(0)
                gates_of(0, 0)
                rounds(pe, step, NG + 1)

            @block.scalar
            def _(act):
                sc = nc.scalar
                act.wait_ge(ready, READY)
                act.wait_ge(heads.set, 4)

                def queries(g, w):
                    if later(g, 2):
                        act.wait_ge(heads.scored, g * G - G)
                    for k in range(KC):
                        act.wait_ge(used, g * 2 + k + 1)
                        sc.copy(heads.QT[:, w, k, :], psG[:]).then_inc(taken, 1)

                def place_values(g, w):
                    act.wait_ge(v_in, g * 32 + 32)
                    if later(g, 2):
                        act.wait_ge(heads.valued, g * G - G)
                    for hp in range(2):
                        rows = slice(hp * L, (hp + 1) * L)
                        sc.copy(heads.VB[rows, w, :, :, hp, 0:DH],
                                V2[rows].rearrange("p b (i h d) -> p b i h d", h=2, d=DH)[:, :, :, hp, :]).then_inc(
                                    v_copied, 1)

                def exp(g, i):
                    act.wait_ge(a_taken, g * G + i + 1)
                    sc.activation(DB[:, i % 2], DB[:, i % 2], ACT.Exp).then_inc(d_done, 1)

                def softplus(g):
                    act.wait_ge(f_steps, g * FPER + 2)
                    sc.activation(fw[:, 1], fw[:, 0], ACT.Exp).then_inc(f_exp, 1)

                def logarithms(g):
                    if is_group(g):
                        act.wait_ge(f_exp, g + 1)
                        sc.activation(fw[:, 2], fw[:, 1], ACT.Ln, bias=one[:, 0:1]).then_inc(f_ln, 1)
                    if is_group(g - 2):
                        act.wait_ge(t_steps, (g - 2) * TPER + 13)
                        sc.activation(tw[:, 12], tw[:, 8], ACT.Ln).then_inc(v_ln, 1)
                        act.wait_ge(v_ln, g - 1)
                        sc.activation(tw[:, 9], tw[:, 12], ACT.Exp, scale=-0.5).then_inc(r_done, 1)

                def step(g, w):
                    bg, bw = g - 1, 1 - w
                    for i in range(G + 2):
                        if is_group(bg) and i >= 2:
                            heads.copy_turned(act, bg, i - 2)
                        if is_group(bg) and 1 <= i < G:
                            exp(bg, i)
                        if i == G + 1:
                            if is_group(g + 1):
                                queries(g + 1, 1 - w)
                            if is_group(g):
                                exp(g, 0)
                        if is_group(g) and i == 1:
                            softplus(g)
                        if is_group(bg) and i >= 2:
                            act.wait_ge(heads.valued, bg * G + i - 1)
                            sc.copy(OG[:, bw, i - 2], heads.out()).then_inc(heads.o_taken, 1)
                        if is_group(g - 2) and i == TAIL_AT[0]:
                            act.wait_ge(t_steps, (g - 2) * TPER + 1)
                            sc.activation(tw[:, 3], tw[:, 0], ACT.Exp, scale=-1.0).then_inc(e_done, 1)
                            act.wait_ge(t_steps, (g - 2) * TPER + 4)
                            sc.activation(sq[:], cen[:], ACT.Square).then_inc(sq_done, 1)
                        if i == 2:
                            logarithms(g)
                        if is_group(g) and i == 5:
                            place_values(g, w)

                queries(0, 0)
                rounds(act, step, NG + 1)

def ternary(nc, name, identb, matrices, loads=()):
    NB = 8
    with ExitStack() as ctx:
        s = Scope(nc, ctx, name)
        M = len(matrices)
        W = s.sb("W", [P, M, FF * D // P])
        R = s.sb("R", [P, M, FF * D // P], BF16)
        scratch = s.sb("scratch", [P, M, FF * D // P], BF16)
        ones = s.sb("ones", [P, P])
        rowsum = s.sb("rowsum", [P, M])
        inv = s.sb("inv", [P, M])
        psum = s.ps("psum", [P, M])
        psT = s.ps("psT", [P, 2, NB, P], BF16)
        set_, steps, summed, totalled, ternary_done, turned, taken, side_in = (
            s.sem(x) for x in ("set", "steps", "summed", "totalled", "ternary", "turned", "taken", "side_in"))
        w_in = [s.sem(f"w_in{m}") for m in range(M)]
        with nc.Block() as block:

            @block.sync
            def _(sp):
                for m, (dram, WT, scale) in enumerate(matrices):
                    I = dram.shape[1]
                    sp.dma_start(W[:, m].rearrange("p (c i) -> p c i", i=I),
                                 dram.rearrange("(c p) i -> p c i", p=P)).then_inc(w_in[m], 16)
                for tile, source in loads:
                    sp.dma_start(tile[:], source).then_inc(side_in, 16)
                if loads:
                    sp.wait_ge(side_in, 16 * len(loads))

            @block.gpsimd
            def _(pool):
                nc.gpsimd.memset(ones[:], 1.0).then_inc(set_, 1)

            @block.vector
            def _(dve):
                step = Steps(dve, steps, 4 * M)
                for m, (dram, WT, scale) in enumerate(matrices):
                    dve.wait_ge(totalled, M)
                    step(nc.vector.tensor_scalar(scale[:, 0:1], psum[:, m:m + 1], 1.0 / (FF * D), 1e-5, ALU.mult,
                                                 ALU.max))
                    step(nc.vector.reciprocal(inv[:, m:m + 1], scale[:, 0:1]))
                    step(nc.vector.tensor_scalar(W[:, m], W[:, m], inv[:, m:m + 1], MAGIC, ALU.mult, ALU.add))
                    step(nc.vector.tensor_scalar(W[:, m], W[:, m], MAGIC, 1.0, ALU.subtract, ALU.min))
                    nc.vector.tensor_scalar(R[:, m], W[:, m], -1.0, None, ALU.max).then_inc(ternary_done, 1)
                step.end()

            @block.tensor
            def _(pe):
                pe.wait_ge(set_, 1)
                for m in range(M):
                    pe.wait_ge(summed, m + 1)
                    nc.tensor.matmul(psum[:, m:m + 1], ones[:], rowsum[:, m:m + 1], start=True,
                                     stop=True).then_inc(totalled, 1)
                for m, (dram, WT, scale) in enumerate(matrices):
                    O, I = dram.shape
                    pe.wait_ge(ternary_done, m + 1)
                    blocks = [(k, c) for k in range(I // P) for c in range(O // P)]
                    for half in range(2):
                        if m > 0:
                            pe.wait_ge(taken, 2 * m - 1 + half)
                        for n, (k, c) in enumerate(blocks[half * NB:half * NB + NB]):
                            mm = nc.tensor.transpose(psT[:, half, n, :], R[:, m, c * I + k * P:c * I + (k + 1) * P],
                                                     identb[:])
                        mm.then_inc(turned, 1)

            @block.scalar
            def _(act):
                for m in range(M):
                    act.wait_ge(w_in[m], 16)
                    nc.scalar.activation(scratch[:, m], W[:, m], ACT.Abs, accum_out=rowsum[:, m:m + 1]).then_inc(
                        summed, 1)
                for m, (dram, WT, scale) in enumerate(matrices):
                    flat = WT[:].rearrange("p k o -> p (k o)")
                    for half in range(2):
                        act.wait_ge(turned, 2 * m + half + 1)
                        nc.scalar.copy(flat[:, half * NB * P:(half + 1) * NB * P],
                                       psT[:, half].rearrange("p n q -> p (n q)")).then_inc(taken, 1)

class Rounded:

    def __init__(self, nc, s, X, ident, rms_eps, floor):
        self.nc, self.ident, self.rms_eps, self.floor = nc, ident, rms_eps, floor
        self.norm = Norm(nc, s, X)
        self.Z = s.sb("Z", [P, G, D])
        self.ZM = s.sb("ZM", [P, G, D])
        self.QT = s.sb("QT", [P, 2, KC, G * P], BF16)
        self.amax = s.sb("amax", [P, G])
        self.am = s.sb("am", [P, G])
        self.unit = s.sb("unit", [P, 2, G])
        self.inv = s.sb("inv", [P, G])
        self.qs = s.sb("qs", [P, G])
        self.u = s.sb("u", [P, 3, G])
        self.r = s.sb("r", [P, G])
        self.rms_e = s.sb("rms_e", [P, G])
        self.neg = s.sb("neg", [P, 1])
        self.psT = s.ps("psT", [P, KC, G * P])
        self.steps, self.rounded, self.turned, self.qt_done = (
            s.sem(x) for x in ("q_steps", "rounded", "q_turned", "qt_done"))
        self.set, self.rms_steps, self.r_done = s.sem("q_set"), s.sem("rms_steps"), s.sem("r_done")
        self.PER = 5 if rms_eps else 3

    def constants(self, pool):
        self.nc.gpsimd.memset(self.neg[:], -MAGIC).then_inc(self.set, 1)
        self.nc.gpsimd.memset(self.rms_e[:], self.rms_eps or 0.0).then_inc(self.set, 1)
        pool.wait_ge(self.set, 2)
        self.norm.constants(pool)

    def on_pool(self, pool, g):
        self.norm.on_pool(pool, g)
        if self.rms_eps:
            gp, n = self.nc.gpsimd, self.norm
            step = Steps(pool, self.rms_steps, 3, g)
            pool.wait_ge(n.rstd_done, g + 1)
            step(gp.tensor_tensor(self.u[:, 0], n.mv[:, :, 1], n.rstd[:], ALU.mult))
            step(gp.tensor_tensor(self.u[:, 1], self.u[:, 0], n.rstd[:], ALU.mult))
            step(gp.tensor_tensor(self.u[:, 2], self.u[:, 1], self.rms_e[:], ALU.add))
            gp.tensor_tensor(self.r[:], self.u[:, 2], n.mhalf[:], ALU.pow).then_inc(self.r_done, 1)
            step.end()

    def on_vector(self, dve, g, w, part):
        v, Z = self.nc.vector, self.Z
        if part == 0:
            self.norm.take_stats(dve, g)
        if part == 1:
            self.norm.normalise(dve, g, Z)
        if part == 2:
            step = Steps(dve, self.steps, self.PER, g)
            dve.wait_ge(self.norm.normed, g * G + G)
            step(v.tensor_reduce(self.amax[:], Z[:], AX.X, ALU.max, apply_absolute_value=True))
            am = self.amax
            if self.rms_eps:
                dve.wait_ge(self.r_done, g + 1)
                step(v.tensor_tensor(self.am[:], self.amax[:], self.r[:], ALU.mult))
                am = self.am
            step(v.tensor_scalar(self.unit[:, w], am[:], self.floor, 1.0 / 127.0, ALU.max, ALU.mult))
            step(v.reciprocal(self.inv[:], self.unit[:, w]))
            if self.rms_eps:
                step(v.tensor_tensor(self.qs[:], self.inv[:], self.r[:], ALU.mult))
            step.end()
        if part == 3:
            qs = self.qs if self.rms_eps else self.inv
            dve.wait_ge(self.turned, g * KC)
            for j in range(G):
                v.tensor_scalar(self.ZM[:, j, :], Z[:, j, :], qs[:, j:j + 1], MAGIC, ALU.mult,
                                ALU.add).then_inc(self.rounded, 1)

    def on_tensor(self, pe, g):
        pe.wait_ge(self.rounded, g * G + G)
        pe.wait_ge(self.qt_done, g * KC)
        for k in range(KC):
            for j in range(G):
                mm = self.nc.tensor.transpose(self.psT[:, k, j * P:(j + 1) * P], self.ZM[:, j, k * P:(k + 1) * P],
                                              self.ident[:])
            mm.then_inc(self.turned, 1)

    def on_scalar(self, act, g, w):
        for k in range(KC):
            act.wait_ge(self.turned, g * KC + k + 1)
            self.nc.scalar.activation(self.QT[:, w, k, :], self.psT[:, k, :], ACT.Identity,
                                      bias=self.neg[:, 0:1]).then_inc(self.qt_done, 1)

class Down:

    def __init__(self, nc, s, X, identb, W2, w2_unit, eps):
        self.nc, self.X, self.identb, self.W2, self.w2_unit, self.eps = nc, X, identb, W2, w2_unit, eps
        self.square = s.sb("square", [P, 2, FF], BF16)
        self.ms = s.sb("ms", [P, 2, G])
        self.me = s.sb("me", [P, G])
        self.r = s.sb("d_r", [P, G])
        self.mhalf = s.sb("d_mhalf", [P, G])
        self.amax = s.sb("d_amax", [P, 2, G])
        self.am = s.sb("d_am", [P, G])
        self.unit = s.sb("d_unit", [P, G])
        self.inv = s.sb("d_inv", [P, G])
        self.qs = s.sb("d_qs", [P, G])
        self.uw = s.sb("d_uw", [P, G])
        self.magic = s.sb("magic", [P, 1])
        self.HM = s.sb("HM", [P, 2, FF])
        self.HB = s.sb("HB", [P, 2, FF], BF16)
        self.HT = s.sb("HT", [P, 2, FF // P, P], BF16)
        self.psV = s.ps("psV", [P, FF // P, P], BF16)
        self.psO = s.ps("psO", [P, D])
        self.set = s.sem("d_set")
        (self.squared, self.maxed, self.steps, self.r_done, self.hm_done, self.hb_done, self.turned, self.ht_done,
         self.out, self.x_done) = (s.sem(x) for x in (
             "squared", "d_maxed", "d_steps", "d_r_done", "hm_done", "hb_done", "d_turned", "ht_done", "out",
             "x_done"))

    def constants(self, pool):
        self.nc.gpsimd.memset(self.magic[:], MAGIC).then_inc(self.set, 1)
        self.nc.gpsimd.memset(self.mhalf[:], -0.5).then_inc(self.set, 1)
        pool.wait_ge(self.set, 2)

    def power(self, pool, g):
        pool.wait_ge(self.steps, g * 6 + 1)
        self.nc.gpsimd.tensor_tensor(self.r[:], self.me[:], self.mhalf[:], ALU.pow).then_inc(self.r_done, 1)

    def squares(self, act, g, w, j, Hj):
        if later(g, 1) or j > 1:
            act.wait_ge(self.squared, g * G + j - 1)
        if j == 0 and later(g, 2):
            act.wait_ge(self.steps, g * 6 - 6)
        self.nc.scalar.activation(self.square[:, j % 2], Hj, ACT.Square,
                                  accum_out=self.ms[:, w, j:j + 1]).then_inc(self.squared, 1)

    def maximum(self, w, j, Hj):
        self.nc.vector.tensor_reduce(self.amax[:, w, j:j + 1], Hj, AX.X, ALU.max,
                                     apply_absolute_value=True).then_inc(self.maxed, 1)

    def scales(self, dve, g, w):
        v = self.nc.vector
        step = Steps(dve, self.steps, 6, g)
        dve.wait_ge(self.squared, g * G + G)
        step(v.tensor_scalar(self.me[:], self.ms[:, w], 1.0 / FF, self.eps, ALU.mult, ALU.add))
        dve.wait_ge(self.r_done, g + 1)
        dve.wait_ge(self.maxed, g * G + G)
        step(v.tensor_tensor(self.am[:], self.amax[:, w], self.r[:], ALU.mult))
        step(v.tensor_scalar(self.unit[:], self.am[:], 1e-5, 1.0 / 127.0, ALU.max, ALU.mult))
        step(v.reciprocal(self.inv[:], self.unit[:]))
        dve.wait_ge(self.hm_done, g * G)
        step(v.tensor_tensor(self.qs[:], self.inv[:], self.r[:], ALU.mult))
        step(v.tensor_scalar(self.uw[:], self.unit[:], self.w2_unit[:, 0:1], None, ALU.mult))
        step.end()

    def scale_and_round(self, act, g, j, Hj):
        if j == 0:
            act.wait_ge(self.steps, g * 6 + 6)
        if later(g, 1) or j > 1:
            act.wait_ge(self.hb_done, g * G + j - 1)
        self.nc.scalar.activation(self.HM[:, j % 2], Hj, ACT.Identity, bias=self.magic[:, 0:1],
                                  scale=self.qs[:, j:j + 1]).then_inc(self.hm_done, 1)

    def integers(self, dve, g, j):
        dve.wait_ge(self.hm_done, g * G + j + 1)
        if later(g, 1) or j > 1:
            dve.wait_ge(self.turned, g * G + j - 1)
        self.nc.vector.tensor_scalar(self.HB[:, j % 2], self.HM[:, j % 2], MAGIC, None, ALU.subtract).then_inc(
            self.hb_done, 1)

    def turn(self, pe, g, j):
        t = g * G + j
        pe.wait_ge(self.hb_done, t + 1)
        pe.wait_ge(self.ht_done, t)
        for c in range(FF // P):
            mm = self.nc.tensor.transpose(self.psV[:, c, :], self.HB[:, j % 2, c * P:(c + 1) * P], self.identb[:])
        mm.then_inc(self.turned, 1)

    def copy_turned(self, act, g, j):
        t = g * G + j
        act.wait_ge(self.turned, t + 1)
        if later(g, 1) or j > 1:
            act.wait_ge(self.out, t - 1)
        self.nc.scalar.copy(self.HT[:, j % 2], self.psV[:]).then_inc(self.ht_done, 1)

    def product(self, pe, g, j):
        t = g * G + j
        pe.wait_ge(self.ht_done, t + 1)
        pe.wait_ge(self.x_done, t)
        for c in range(FF // P):
            mm = self.nc.tensor.matmul(self.psO[:], self.HT[:, j % 2, c, :], self.W2[:, c, :], start=(c == 0),
                                       stop=(c == FF // P - 1))
        mm.then_inc(self.out, 1)

    def add(self, dve, g, j):
        t = g * G + j
        x = self.X[:, t, :]
        dve.wait_ge(self.out, t + 1)
        self.nc.vector.scalar_tensor_tensor(x, self.psO[:], self.uw[:, j:j + 1], x, ALU.mult, ALU.add).then_inc(
            self.x_done, 1)

HALF = FF // 2

def normed_ffn(nc, io, X, ident, identb):
    with ExitStack() as ctx:
        s = Scope(nc, ctx, "nffn")
        W1 = s.sb("W1", [P, KC, FF], BF16)
        W2 = s.sb("W2", [P, FF // P, D], BF16)
        u1, u2 = s.sb("u1", [P, 1]), s.sb("u2", [P, 1])
        b1, gam, bet, b2 = s.sb("b1", [P, FF]), s.sb("gam", [P, FF]), s.sb("bet", [P, FF]), s.sb("b2", [P, D])
        ternary(nc, "nffn_weights", identb, [(io["L1_ffn_w1"], W1, u1), (io["L1_ffn_w2"], W2, u2)],
                [(tile, spread(io["L1_ffn_" + x], 0, P)) for tile, x in ((b1, "b1"), (gam, "ln_g"), (bet, "ln_b"),
                                                                         (b2, "b2"))])
        H = s.sb("H", [P, 2, G, FF])
        q = Rounded(nc, s, X, ident, 1e-5, 1e-5)
        down = Down(nc, s, X, identb, W2, u2, 1e-5)
        uw = s.sb("uw", [P, G])
        stats = s.sb("stats2", [P, G, 2, 6])
        mv = s.sb("mv2", [P, G, 2])
        rstd = s.sb("rstd2", [P, G])
        veps = s.sb("veps2", [P, G])
        psH = s.ps("psH", [P, 2, HALF])
        (uw_done, up, affined, silued, gelued, agg, veps_done, rstd_done, normed, gained, shifted, b2_added) = (
            s.sem(x) for x in ("uw_done", "up", "affined", "silued", "gelued", "agg2", "veps2_done",
                               "rstd2_done", "normed2", "gained", "shifted", "b2_added"))

        with nc.Block() as block:

            @block.gpsimd
            def _(pool):
                q.constants(pool)
                down.constants(pool)

                def step(g, w):
                    b, bw = g - 1, 1 - w
                    if is_group(b):
                        pool.wait_ge(agg, b * G + G)
                        nc.gpsimd.tensor_tensor(veps[:], mv[:, :, 1], q.norm.eps[:], ALU.add).then_inc(veps_done, 1)
                        pool.wait_ge(veps_done, b + 1)
                        nc.gpsimd.tensor_tensor(rstd[:], veps[:], q.norm.mhalf[:], ALU.pow).then_inc(rstd_done, 1)
                        for j in range(G):
                            pool.wait_ge(normed, b * G + j + 1)
                            nc.gpsimd.tensor_tensor(H[:, bw, j], H[:, bw, j], gam[:], ALU.mult).then_inc(gained, 1)
                        down.power(pool, b)
                    if is_group(g + 1):
                        q.on_pool(pool, g + 1)
                    if is_group(b):
                        pool.wait_ge(down.x_done, b * G + G)
                        xs = X[:, bass.ds(b * G, G), :]
                        nc.gpsimd.tensor_tensor(xs, xs, spread(b2[:], 1, G), ALU.add).then_inc(b2_added, 1)

                q.on_pool(pool, 0)
                rounds(pool, step, NG)

            @block.vector
            def _(dve):
                v = nc.vector

                def step(g, w):
                    if is_group(g):
                        v.tensor_scalar(uw[:], q.unit[:, w], u1[:, 0:1], None, ALU.mult).then_inc(uw_done, 1)
                    b, bw = g - 1, 1 - w
                    if is_group(b):
                        for j in range(G):
                            dve.wait_ge(gelued, b * G + j + 1)
                            for h in range(2):
                                v.bn_stats(stats[:, j, h, :], H[:, bw, j, h * HALF:(h + 1) * HALF])
                        dve.drain()
                        for j in range(G):
                            v.bn_aggr(mv[:, j, :], stats[:, j].rearrange("p h s -> p (h s)")).then_inc(agg, 1)
                        dve.wait_ge(rstd_done, b + 1)
                        dve.wait_ge(agg, b * G + G)
                        for j in range(G):
                            v.tensor_scalar(H[:, bw, j], H[:, bw, j], mv[:, j, 0:1], rstd[:, j:j + 1],
                                            ALU.subtract, ALU.mult).then_inc(normed, 1)
                    if is_group(g):
                        dve.wait_ge(uw_done, g + 1)
                    for j in range(G):
                        if is_group(g):
                            for h in range(2):
                                half = slice(h * HALF, (h + 1) * HALF)
                                dve.wait_ge(up, (g * G + j) * 2 + h + 1)
                                v.scalar_tensor_tensor(H[:, w, j, half], psH[:, h, :], uw[:, j:j + 1], b1[:, half],
                                                       ALU.mult, ALU.add).then_inc(affined, 1)
                        if is_group(b):
                            dve.wait_ge(gained, b * G + j + 1)
                            v.tensor_tensor(H[:, bw, j], H[:, bw, j], bet[:], ALU.add).then_inc(shifted, 1)
                            dve.wait_ge(shifted, b * G + j + 1)
                            down.maximum(bw, j, H[:, bw, j])
                    if is_group(b):
                        down.scales(dve, b, bw)
                    for j in range(G):
                        if is_group(b):
                            down.integers(dve, b, j)
                            if j > 0:
                                down.add(dve, b, j - 1)
                        if is_group(g + 1):
                            q.on_vector(dve, g + 1, 1 - w, j)
                    if is_group(b):
                        down.add(dve, b, G - 1)

                for part in range(4):
                    q.on_vector(dve, 0, 0, part)
                rounds(dve, step, NG)

            @block.tensor
            def _(pe):
                def step(g, w):
                    if is_group(g):
                        q.on_tensor(pe, g)
                        pe.wait_ge(q.qt_done, g * KC + KC)
                        for j in range(G):
                            for h in range(2):
                                if later(g, 1) or j > 0:
                                    pe.wait_ge(affined, (g * G + j) * 2 + h - 1)
                                for k in range(KC):
                                    mm = nc.tensor.matmul(psH[:, h, :], q.QT[:, w, k, j * P:(j + 1) * P],
                                                          W1[:, k, h * HALF:(h + 1) * HALF], start=(k == 0),
                                                          stop=(k == KC - 1))
                                mm.then_inc(up, 1)
                    if is_group(g - 1):
                        down.turn(pe, g - 1, 0)
                        for j in range(G):
                            down.product(pe, g - 1, j)
                            if j + 1 < G:
                                down.turn(pe, g - 1, j + 1)

                rounds(pe, step, NG)

            @block.scalar
            def _(act):
                def step(g, w):
                    if is_group(g):
                        q.on_scalar(act, g, w)
                    b, bw = g - 1, 1 - w
                    for j in range(G):
                        if is_group(g):
                            act.wait_ge(affined, (g * G + j) * 2 + 2)
                            nc.scalar.activation(H[:, w, j], H[:, w, j], ACT.Silu).then_inc(silued, 1)
                        if is_group(g - 1):
                            act.wait_ge(shifted, b * G + j + 1)
                            down.squares(act, b, bw, j, H[:, bw, j])
                    if is_group(g - 1):
                        for j in range(G):
                            down.scale_and_round(act, b, j, H[:, bw, j])
                            if j > 0:
                                down.copy_turned(act, b, j - 1)
                        down.copy_turned(act, b, G - 1)
                    if is_group(g):
                        for j in range(G):
                            act.wait_ge(silued, g * G + j + 1)
                            nc.scalar.activation(H[:, w, j], H[:, w, j], ACT.Gelu).then_inc(gelued, 1)

                rounds(act, step, NG)

def softmax_attention(nc, io, X, CT, ident, KX, VB):
    V_AT = [[], [], [], [0, 1, 2], [3, 4, 5], [6, 7]]
    with ExitStack() as ctx:
        s = Scope(nc, ctx, "satt")
        WQ, WK, WV, WO = (s.sb(x, [P, KC, D]) for x in ("WQ", "WK", "WV", "WO"))
        bq, bk = s.sb("bq", [P, KC]), s.sb("bk", [P, KC])
        bv, bo = s.sb("bv", [P, D]), s.sb("bo", [P, D])
        turn_weights(nc, "satt_weights", ident,
                     [(io["L2_xattn_W" + x], W) for x, W in (("q", WQ), ("k", WK), ("v", WV), ("o", WO))],
                     [(b, io["L2_xattn_b" + x].rearrange("(k p) -> p k", p=P)) for x, b in (("q", bq), ("k", bk))]
                     + [(b, spread(io["L2_xattn_b" + x], 0, P)) for x, b in (("v", bv), ("o", bo))])
        norm = Norm(nc, s, X)
        heads = Heads(nc, s, ident, KX, VB)
        Z = s.sb("Z", [P, G, D])
        ZT = s.sb("ZT", [P, KC, G * P])
        KT = s.sb("KT", [P, KC, G * P])
        CG = s.sb("CG", [P, KC, G * P])
        mx = s.sb("mx", [P, 2, NH])
        rs = s.sb("rs", [P, 2, NH])
        AO = s.sb("AO", [P, 2, NH, DH])
        AT = s.sb("AT", [P, 2, KC, P])
        psG = s.ps("psG", [P, 2, 512])
        psF = s.ps("psF", [P, 512])
        (c_in, used, taken, v_used, v_taken, maxed, subbed, inverted, ao_done, ao_turned, at_done, projected,
         x_done, bo_added) = (s.sem(x) for x in (
             "c_in", "used", "taken", "v_used", "v_taken", "maxed", "subbed", "inverted", "ao_done",
             "ao_turned", "at_done", "projected", "x_done", "bo_added"))

        with nc.Block() as block:

            @block.sync
            def _(sp):
                def front(g, w):
                    at, vs, ks = (held(sp, v) for v in (g * (G * P), g * BG, g * 6 + 6))
                    free = heads.free_after(sp, g)
                    sp.wait_ge(v_used, vs)
                    sp.dma_start(CG[:], CT[:, :, bass.ds(at, G * P)]).then_inc(c_in, 16)
                    sp.wait_ge(taken, ks)
                    heads.expand(sp, g, lambda rows, c, half: KT[rows, c, half * HG:(half + 1) * HG], free)

                rounds(sp, lambda g, w: front(g, w) if is_group(g) else None, NG)

            @block.gpsimd
            def _(pool):
                norm.constants(pool)

                def back(g, w):
                    pool.wait_ge(x_done, g * G + G)
                    xs = X[:, bass.ds(g * G, G), :]
                    nc.gpsimd.tensor_tensor(xs, xs, spread(bo[:], 1, G), ALU.add).then_inc(bo_added, 1)

                def step(g, w):
                    if is_group(g + 1):
                        norm.on_pool(pool, g + 1)
                    if is_group(g - 1):
                        back(g - 1, 1 - w)

                norm.on_pool(pool, 0)
                rounds(pool, step, NG)

            @block.vector
            def _(dve):
                v = nc.vector

                def values_of(g, w, b):
                    dve.wait_ge(v_used, g * BG + b + 1)
                    if b == 0 and later(g, 2):
                        dve.wait_ge(heads.valued, g * G - G)
                    for hp in range(2):
                        rows = slice(hp * L, (hp + 1) * L)
                        take = lambda x: x.rearrange("p (i h d) -> p i h d", h=2, d=DH)[:, :, hp, :]
                        v.tensor_tensor(heads.VB[rows, w, b, :, hp, 0:DH], take(psG[rows, b % 2, 0:D]),
                                        take(bv[rows, :]), ALU.add).then_inc(v_taken, 1)

                def max_and_shift(g, i):
                    t = g * G + i
                    p = i % 2
                    S = heads.psS[:].rearrange("p c (h t) -> p (c h) t", t=L)
                    dve.wait_ge(heads.scored, t + 1)
                    v.tensor_reduce(mx[:, p], S, AX.X, ALU.max).then_inc(maxed, 1)
                    if later(g, 1) or i > 1:
                        dve.wait_ge(heads.turned, 2 * t - 2)
                    dve.wait_ge(maxed, t + 1)
                    v.tensor_tensor(heads.PB[:, p], S, spread(mx[:, p], 2, L), ALU.subtract).then_inc(
                        heads.s_taken, 1)

                def step(g, w):
                    bg = g - 1
                    for i in range(G + 2):
                        if is_group(bg) and 1 <= i < G:
                            max_and_shift(bg, i)
                        if is_group(g) and i == G + 1:
                            max_and_shift(g, 0)
                        if is_group(g):
                            for b in V_AT[i]:
                                values_of(g, w, b)
                        if is_group(bg) and 1 <= i <= G:
                            t = bg * G + i - 1
                            p = (i - 1) % 2
                            dve.wait_ge(heads.valued, t + 1)
                            v.reciprocal(rs[:, p], heads.out()[:, :, DH]).then_inc(inverted, 1)
                            dve.wait_ge(inverted, t + 1)
                            if later(bg, 1) or i > 2:
                                dve.wait_ge(ao_turned, t - 1)
                            v.tensor_tensor(AO[:, p], heads.out()[:, :, 0:DH], spread(rs[:, p], 2, DH),
                                            ALU.mult).then_inc(heads.o_taken, 1)
                        if is_group(bg) and i >= 2:
                            t = bg * G + i - 2
                            dve.wait_ge(projected, t + 1)
                            v.tensor_tensor(X[:, t, :], psF[:, 0:D], X[:, t, :], ALU.add).then_inc(x_done, 1)
                        if is_group(g + 1) and i == 1:
                            norm.take_stats(dve, g + 1)
                        if is_group(g + 1) and i == 3:
                            dve.wait_ge(used, g * 6 + 2)
                            norm.normalise(dve, g + 1, Z)

                norm.on_vector(dve, 0, Z)
                rounds(dve, step, NG)

            @block.tensor
            def _(pe):

                def z_turned(g):
                    pe.wait_ge(norm.normed, g * G + G)
                    for k in range(KC):
                        pe.wait_ge(v_taken, g * 2 * BG)
                        for j in range(G):
                            mm = nc.tensor.transpose(psG[:, k, j * P:(j + 1) * P], Z[:, j, k * P:(k + 1) * P], ident[:])
                        mm.then_inc(used, 1)

                def project(g, m, W, src):
                    for e in range(KC):
                        pe.wait_ge(taken, g * 6 + (2 if m == 0 else e + 3))
                        for k in range(KC):
                            mm = nc.tensor.matmul(psG[:, e, :], W[:, k, e * P:(e + 1) * P], src[:, k, :],
                                                  start=(k == 0), stop=(k == KC - 1))
                        mm.then_inc(used, 1)

                def values_of(g, b):
                    if b < 2:
                        pe.wait_ge(taken, g * 6 + 5 + b)
                    else:
                        pe.wait_ge(v_taken, g * 2 * BG + 2 * (b - 1))
                    for k in range(KC):
                        for hp in range(2):
                            mm = nc.tensor.matmul(psG[hp * L:(hp + 1) * L, b % 2, 0:D],
                                                  CG[:, k, b * L:(b + 1) * L], WV[:, k, :], start=(k == 0),
                                                  stop=(k == KC - 1), skip_group_check=True)
                    mm.then_inc(v_used, 1)

                def turn_out(g, j):
                    t = g * G + j
                    pe.wait_ge(heads.o_taken, t + 1)
                    pe.wait_ge(x_done, t)
                    for c in range(KC):
                        mm = nc.tensor.transpose(psF[:, c * P:(c + 1) * P],
                                                 AO[:, j % 2, c * HC:(c + 1) * HC, :].rearrange("p h d -> p (h d)"),
                                                 ident[:])
                    mm.then_inc(ao_turned, 1)

                def project_out(g, j):
                    t = g * G + j
                    pe.wait_ge(at_done, t + 1)
                    for c in range(KC):
                        mm = nc.tensor.matmul(psF[:, 0:D], AT[:, j % 2, c, :], WO[:, c, :], start=(c == 0),
                                              stop=(c == KC - 1))
                    mm.then_inc(projected, 1)

                def step(g, w):
                    bg, bw = g - 1, 1 - w
                    if is_group(bg):
                        pe.wait_ge(v_taken, (bg + 1) * 2 * BG)
                    for i in range(G + 2):
                        if is_group(bg) and 1 <= i < G:
                            heads.scores(pe, bg, bw, i)
                        if is_group(g) and i == G + 1:
                            pe.wait_ge(taken, g * 6 + 4)
                            heads.scores(pe, g, w, 0)
                        if is_group(bg) and i >= 2:
                            turn_out(bg, i - 2)
                        if is_group(bg) and 1 <= i <= G:
                            heads.turn(pe, bg, i - 1)
                        if is_group(g):
                            if i == 0:
                                z_turned(g)
                            if i == 1:
                                project(g, 0, WQ, ZT)
                            if i == 2:
                                pe.wait_ge(c_in, g * 16 + 16)
                                project(g, 1, WK, CG)
                            for b in V_AT[i]:
                                values_of(g, b)
                        if is_group(bg) and 1 <= i <= G:
                            heads.values(pe, bg, bw, i - 1)
                        if is_group(bg) and i >= 2:
                            project_out(bg, i - 2)

                rounds(pe, step, NG)

            @block.scalar
            def _(act):
                SCALE = float(DH) ** -0.5

                def exp(g, i):
                    act.wait_ge(heads.s_taken, g * G + i + 1)
                    nc.scalar.activation(heads.PB[:, i % 2], heads.PB[:, i % 2], ACT.Exp,
                                         scale=SCALE).then_inc(heads.weighted, 1)

                def step(g, w):
                    bg = g - 1
                    for i in range(G + 2):
                        if is_group(bg) and i >= 2:
                            j = i - 2
                            t = bg * G + j
                            act.wait_ge(ao_turned, t + 1)
                            if later(bg, 1) or j > 1:
                                act.wait_ge(projected, t - 1)
                            nc.scalar.copy(AT[:, j % 2].rearrange("p c t -> p (c t)"), psF[:, 0:D]).then_inc(
                                at_done, 1)
                        if is_group(bg) and 1 <= i <= G:
                            heads.copy_turned(act, bg, i - 1)
                        if is_group(g) and i == 0:
                            for k in range(KC):
                                act.wait_ge(used, g * 6 + k + 1)
                                nc.scalar.copy(ZT[:, k, :], psG[:, k, :]).then_inc(taken, 1)
                        if is_group(g) and i == 1:
                            if later(g, 2):
                                act.wait_ge(heads.scored, g * G - G)
                            for e in range(KC):
                                act.wait_ge(used, g * 6 + 3 + e)
                                nc.scalar.activation(heads.QT[:, w, e, :], psG[:, e, :], ACT.Identity,
                                                     bias=bq[:, e:e + 1]).then_inc(taken, 1)
                        if is_group(g) and i == 2:
                            for half in range(2):
                                act.wait_ge(heads.kx_in[half], g * 256)
                            for e in range(KC):
                                act.wait_ge(used, g * 6 + 5 + e)
                                nc.scalar.activation(KT[:, e, :], psG[:, e, :], ACT.Identity,
                                                     bias=bk[:, e:e + 1]).then_inc(taken, 1)
                        if is_group(bg) and 1 <= i < G:
                            exp(bg, i)
                        if is_group(g) and i == G + 1:
                            exp(g, 0)

                rounds(act, step, NG)

def gated_ffn(nc, io, X, ident, identb):
    with ExitStack() as ctx:
        s = Scope(nc, ctx, "gffn")
        WG = s.sb("WG", [P, KC, FF], BF16)
        WU = s.sb("WU", [P, KC, FF], BF16)
        W2 = s.sb("W2", [P, FF // P, D], BF16)
        ug, uu, u2 = s.sb("ug", [P, 1]), s.sb("uu", [P, 1]), s.sb("u2", [P, 1])
        ternary(nc, "gffn_weights", identb, [(io["L2_ffn_w_gate"], WG, ug), (io["L2_ffn_w_up"], WU, uu),
                                       (io["L2_ffn_w_down"], W2, u2)])
        H = s.sb("H", [P, 2, G, FF])
        S = s.sb("S", [P, 2, HALF])
        q = Rounded(nc, s, X, ident, 1e-6, 1e-5)
        down = Down(nc, s, X, identb, W2, u2, 1e-6)
        uwg, uwu = s.sb("uwg", [P, 2, G]), s.sb("uwu", [P, 2, G])
        psG = s.ps("psG", [P, 2, HALF])
        psU = s.ps("psU", [P, 2, HALF])
        uw_done, up, gated, taken = (s.sem(x) for x in ("uw_done", "up", "gated", "taken"))

        with nc.Block() as block:

            @block.gpsimd
            def _(pool):
                q.constants(pool)
                down.constants(pool)

                def step(g, w):
                    if is_group(g - 1):
                        down.power(pool, g - 1)
                    if is_group(g + 1):
                        q.on_pool(pool, g + 1)

                q.on_pool(pool, 0)
                rounds(pool, step, NG)

            @block.vector
            def _(dve):
                v = nc.vector

                def step(g, w):
                    if is_group(g):
                        v.tensor_scalar(uwg[:, w], q.unit[:, w], ug[:, 0:1], None, ALU.mult).then_inc(uw_done, 1)
                        v.tensor_scalar(uwu[:, w], q.unit[:, w], uu[:, 0:1], None, ALU.mult).then_inc(uw_done, 1)
                    if is_group(g - 1):
                        down.scales(dve, g - 1, 1 - w)
                    if is_group(g):
                        dve.wait_ge(uw_done, g * 2 + 2)
                    for j in range(G):
                        if is_group(g - 1):
                            down.integers(dve, g - 1, j)
                        if is_group(g):
                            t = g * G + j
                            for h in range(2):
                                dve.wait_ge(gated, t * 2 + h + 1)
                                v.scalar_tensor_tensor(H[:, w, j, h * HALF:(h + 1) * HALF], psU[:, h, :],
                                                       uwu[:, w, j:j + 1], S[:, h, :], ALU.mult,
                                                       ALU.mult).then_inc(taken, 1)
                            if is_group(g - 1) and j > 0:
                                down.add(dve, g - 1, j - 1)
                            dve.wait_ge(taken, t * 2 + 2)
                            down.maximum(w, j, H[:, w, j])
                        elif j > 0:
                            down.add(dve, g - 1, j - 1)
                        if is_group(g + 1):
                            q.on_vector(dve, g + 1, 1 - w, j)
                    if is_group(g - 1):
                        down.add(dve, g - 1, G - 1)

                for part in range(4):
                    q.on_vector(dve, 0, 0, part)
                rounds(dve, step, NG)

            @block.tensor
            def _(pe):
                def up_(g, w, j):
                    for h in range(2):
                        if later(g, 1) or j > 0:
                            pe.wait_ge(taken, (g * G + j) * 2 + h - 1)
                        for bank, W in ((psG, WG), (psU, WU)):
                            for k in range(KC):
                                mm = nc.tensor.matmul(bank[:, h, :], q.QT[:, w, k, j * P:(j + 1) * P],
                                                      W[:, k, h * HALF:(h + 1) * HALF], start=(k == 0),
                                                      stop=(k == KC - 1))
                        mm.then_inc(up, 1)

                def step(g, w):
                    if is_group(g):
                        q.on_tensor(pe, g)
                        pe.wait_ge(q.qt_done, g * KC + KC)
                        up_(g, w, 0)
                    for j in range(G):
                        if is_group(g - 1):
                            down.turn(pe, g - 1, j)
                        if is_group(g) and j + 1 < G:
                            up_(g, w, j + 1)
                        if is_group(g - 1):
                            down.product(pe, g - 1, j)

                rounds(pe, step, NG)

            @block.scalar
            def _(act):
                def step(g, w):
                    if is_group(g):
                        q.on_scalar(act, g, w)
                        act.wait_ge(uw_done, g * 2 + 2)
                    for j in range(G):
                        t = g * G + j
                        if is_group(g - 1):
                            down.scale_and_round(act, g - 1, j, H[:, 1 - w, j])
                        if is_group(g):
                            for h in range(2):
                                act.wait_ge(up, t * 2 + h + 1)
                                if later(g, 1) or j > 0:
                                    act.wait_ge(taken, t * 2 + h - 1)
                                nc.scalar.activation(S[:, h, :], psG[:, h, :], ACT.Silu,
                                                     scale=uwg[:, w, j:j + 1]).then_inc(gated, 1)
                        if is_group(g - 1):
                            down.copy_turned(act, g - 1, j)
                        if is_group(g):
                            act.wait_ge(taken, t * 2 + 2)
                            down.squares(act, g, w, j, H[:, w, j])

                rounds(act, step, NG)

def quantized_ffn(nc, io, X, ident, out):
    with ExitStack() as ctx:
        s = Scope(nc, ctx, "qffn")
        K = s.sb("K", [P, KC, D])
        KT = s.sb("KT", [P, KC, D])
        W = s.sb("W", [P, KC, D], BF16)
        cols = s.sb("cols", [P, KC, 4])
        unit_w = s.sb("unit_w", [P, D])
        bias = s.sb("bias", [P, D])
        bq = s.sb("bq", [P, D])
        bs = s.sb("bs", [P, 4])
        diag = s.sb("diag", [P, KC, P])
        ones = s.sb("ones", [P, P])
        Y = s.sb("Y", [P, 2, G, D])
        YR = s.sb("YR", [P, G, D])
        q = Rounded(nc, s, X, ident, None, 1e-35)
        ymax, yunit, yinv = s.sb("ymax", [P, G]), s.sb("yunit", [P, G]), s.sb("yinv", [P, G])
        magic = s.sb("magic", [P, 1])
        psK = s.ps("psK", [P, KC, D])
        psW = s.ps("psW", [P, D])
        psU = s.ps("psU", [P, D])
        psY = s.ps("psY", [P, 2, 512])
        (w_in, set_, k_steps, turned, back_turned, spread_out, up, scaled, y_steps, rounded,
         x_done, stored) = (s.sem(x) for x in ("w_in", "set", "k_steps", "turned", "back_turned", "spread_out",
                                               "up", "scaled", "y_steps", "y_rounded", "x_done",
                                               "stored"))
        SETUP = 20

        with nc.Block() as block:

            @block.sync
            def _(sp):
                sp.dma_start(K[:], io["L3_ffn_kernel"].rearrange("(k p) f -> p k f", p=P)).then_inc(w_in, 16)
                sp.dma_start(bias[:], spread(io["L3_ffn_bias"], 0, P)).then_inc(w_in, 16)
                sp.wait_ge(w_in, 32)
                o = out.rearrange("(t u) l d -> (u l) t d", u=2)
                with sp.Fori(0, NG) as g:
                    sp.wait_ge(x_done, g + 1)
                    sp.dma_start(o[:, bass.ds(g * G, G), :], X[:, bass.ds(g * G, G), :]).then_inc(stored, 16)
                sp.wait_ge(stored, 16 * NG)

            @block.gpsimd
            def _(pool):
                nc.gpsimd.memset(ones[:], 1.0).then_inc(set_, 1)
                q.constants(pool)
                nc.gpsimd.memset(magic[:], MAGIC).then_inc(set_, 1)
                q.on_pool(pool, 0)
                rounds(pool, lambda g, w: q.on_pool(pool, g + 1) if is_group(g + 1) else None, NG - 1)

            @block.vector
            def _(dve):
                v = nc.vector
                step = Steps(dve, k_steps, SETUP)
                dve.wait_ge(w_in, 32)
                dve.wait_ge(turned, 2)
                for k in range(KC):
                    step(v.tensor_reduce(cols[:, k, 0:1], psK[:, k, :], AX.X, ALU.max, apply_absolute_value=True))
                    step(v.tensor_scalar(cols[:, k, 1:2], cols[:, k, 0:1], 1e-35, 1.0 / 127.0, ALU.max, ALU.mult))
                    step(v.reciprocal(cols[:, k, 2:3], cols[:, k, 1:2]))
                    step(v.tensor_scalar(KT[:, k, :], psK[:, k, :], cols[:, k, 2:3], MAGIC, ALU.mult, ALU.add))
                    step(v.tensor_scalar(KT[:, k, :], KT[:, k, :], MAGIC, None, ALU.subtract))
                    step(v.tensor_scalar(diag[:, k, :], ident[:], cols[:, k, 1:2], None, ALU.mult))
                step(v.tensor_reduce(bs[:, 0:1], bias[:], AX.X, ALU.max, apply_absolute_value=True))
                step(v.tensor_scalar(bs[:, 1:2], bs[:, 0:1], 1e-35, 1.0 / 127.0, ALU.max, ALU.mult))
                step(v.reciprocal(bs[:, 2:3], bs[:, 1:2]))
                step(v.tensor_scalar(bq[:], bias[:], bs[:, 2:3], MAGIC, ALU.mult, ALU.add))
                step(v.tensor_scalar(bq[:], bq[:], MAGIC, bs[:, 1:2], ALU.subtract, ALU.mult))
                dve.wait_ge(spread_out, 1)
                step(v.tensor_copy(unit_w[:], psU[:]))
                dve.wait_ge(back_turned, 1)
                step(v.tensor_copy(W[:, 0, :], psW[:]))
                dve.wait_ge(back_turned, 2)
                step(v.tensor_copy(W[:, 1, :], psW[:]))
                step.end()

                def step(g, w):
                    y = Y[:, w]
                    step = Steps(dve, y_steps, 5, g)
                    if is_group(g + 1):
                        q.on_vector(dve, g + 1, 1 - w, 0)
                        q.on_vector(dve, g + 1, 1 - w, 1)
                    for j in range(G):
                        dve.wait_ge(up, g * G + j + 1)
                        v.scalar_tensor_tensor(y[:, j], psY[:, j % 2, 0:D], q.unit[:, w, j:j + 1], unit_w[:],
                                               ALU.mult, ALU.mult).then_inc(scaled, 1)
                    dve.wait_ge(scaled, g * G + G)
                    step(v.tensor_tensor(y, y, spread(bq[:], 1, G), ALU.add))
                    step(v.tensor_reduce(ymax[:], y, AX.X, ALU.max))
                    dve.wait_ge(x_done, g)
                    step(v.tensor_scalar(yunit[:], ymax[:], 1e-35, 1.0 / 127.0, ALU.max, ALU.mult))
                    step(v.reciprocal(yinv[:], yunit[:]))
                    if is_group(g + 1):
                        q.on_vector(dve, g + 1, 1 - w, 2)
                    dve.wait_ge(rounded, g * G + G)
                    step(v.tensor_scalar(YR[:], YR[:], MAGIC, 0.0, ALU.subtract, ALU.max))
                    step.end()
                    for j in range(G):
                        x = X[:, g * G + j, :]
                        m = v.scalar_tensor_tensor(x, YR[:, j], yunit[:, j:j + 1], x, ALU.mult, ALU.add)
                    m.then_inc(x_done, 1)
                    if is_group(g + 1):
                        q.on_vector(dve, g + 1, 1 - w, 3)

                for part in range(4):
                    q.on_vector(dve, 0, 0, part)
                rounds(dve, step, NG - 1)

            @block.tensor
            def _(pe):
                pe.wait_ge(w_in, 32)
                for f in range(KC):
                    for k in range(KC):
                        mm = nc.tensor.transpose(psK[:, f, k * P:(k + 1) * P], K[:, k, f * P:(f + 1) * P], ident[:])
                    mm.then_inc(turned, 1)
                pe.wait_ge(k_steps, 12)
                pe.wait_ge(set_, 1)
                for f in range(KC):
                    mm = nc.tensor.matmul(psU[:, f * P:(f + 1) * P], ones[:], diag[:, f, :], start=True, stop=True)
                mm.then_inc(spread_out, 1)
                for k in range(KC):
                    if k == 1:
                        pe.wait_ge(k_steps, SETUP - 1)
                    for f in range(KC):
                        mm = nc.tensor.transpose(psW[:, f * P:(f + 1) * P], KT[:, f, k * P:(k + 1) * P], ident[:])
                    mm.then_inc(back_turned, 1)
                pe.wait_ge(k_steps, SETUP)

                def step(g, w):
                    q.on_tensor(pe, g)
                    pe.wait_ge(q.qt_done, g * KC + KC)
                    for j in range(G):
                        t = g * G + j
                        if later(g, 1) or j > 1:
                            pe.wait_ge(scaled, t - 1)
                        for k in range(KC):
                            mm = nc.tensor.matmul(psY[:, j % 2, 0:D], q.QT[:, w, k, j * P:(j + 1) * P], W[:, k, :],
                                                  start=(k == 0), stop=(k == KC - 1))
                        mm.then_inc(up, 1)

                rounds(pe, step, NG - 1)

            @block.scalar
            def _(act):
                def step(g, w):
                    if later(g, 2):
                        act.wait_ge(up, g * G - G)
                    q.on_scalar(act, g, w)
                    act.wait_ge(y_steps, g * 5 + 4)
                    act.wait_ge(x_done, g)
                    for j in range(G):
                        nc.scalar.activation(YR[:, j], Y[:, w, j], ACT.Identity, bias=magic[:, 0:1],
                                             scale=yinv[:, j:j + 1]).then_inc(rounded, 1)

                act.wait_ge(set_, 2)
                rounds(act, step, NG - 1)

def summary_mix(nc, io, X, CT, ident, sums):
    with ExitStack() as ctx:
        s = Scope(nc, ctx, "mix")
        norm = Norm(nc, s, X)
        WI, WO = s.sb("WI", [P, KC, D]), s.sb("WO", [P, KC, D])
        WIT, WOT = s.sb("WIT", [P, KC, D]), s.sb("WOT", [P, KC, D])
        bi = s.sb("bi", [P, KC])
        bo = s.sb("bo", [L, D])
        gam, bet = s.sb("gam", [P, D]), s.sb("bet", [P, D])
        decay, k = s.sb("decay", [P, 1]), s.sb("k", [P, 3])
        ones = s.sb("ones", [P, L])
        powers, weights, wsum = s.sb("powers", [P, L]), s.sb("weights", [P, L]), s.sb("wsum", [P, 1])
        flip, flipped = s.sb("flip", [L, L]), s.sb("flipped", [L, L])
        col, diag, all1 = s.sb("col", [L, 1]), s.sb("diag", [L, L]), s.sb("all1", [L, P])
        weighted = s.sb("weighted", [P, 2, B // 2, L])
        ST = s.sb("ST", [P, KC, B])
        bw = s.sb("bw", [P, KC])
        HT = s.sb("HT", [P, KC, B])
        SUM = s.sb("SUM", [B, D])
        SM = s.sb("SM", [P, T, D])
        Y = s.sb("Y", [P, 2, G, D])
        stats, mv = s.sb("stats2", [P, G, 6]), s.sb("mv2", [P, G, 2])
        veps, rstd = s.sb("veps2", [P, G]), s.sb("rstd2", [P, G])
        psW = s.ps("psW", [P, 2, KC, D])
        psB = s.ps("psB", [P, 512])
        psH = s.ps("psH", [P, KC, 512])
        psS = s.ps("psS", [B, 512])
        (w_in, ready, steps, expd, w_turned, w_copied, wide, hid, summed, sum_out, sum_in, added, stats_done,
         veps_done, rstd_done, normed, gained, y_steps) = (s.sem(x) for x in (
             "w_in", "ready", "steps", "expd", "w_turned", "w_copied", "wide", "hid", "summed", "sum_out", "sum_in",
             "added", "stats2_done", "veps2_done", "rstd2_done", "normed2", "gained", "y_steps"))
        SETUP = 21

        with nc.Block() as block:

            @block.sync
            def _(sp):
                sp.dma_start(decay[:], spread(io["L3_xattn_decay"], 0, P)).then_inc(w_in, 16)
                sp.dma_start(WI[:], io["L3_xattn_W_in"].rearrange("(k p) d -> p k d", p=P)).then_inc(w_in, 16)
                sp.dma_start(WO[:], io["L3_xattn_W_out"].rearrange("(k p) d -> p k d", p=P)).then_inc(w_in, 16)
                with nc.allow_non_contiguous_dma(reason="one column of biases for each chunk"):
                    sp.dma_start(bi[:], io["L3_xattn_b_in"].rearrange("(k p) -> p k", p=P)).then_inc(w_in, 16)
                sp.dma_start(bo[:], spread(io["L3_xattn_b_out"], 0, L)).then_inc(w_in, 16)
                sp.dma_start(gam[:], spread(io["L3_xattn_gamma"], 0, P)).then_inc(w_in, 16)
                sp.dma_start(bet[:], spread(io["L3_xattn_beta"], 0, P)).then_inc(w_in, 16)
                sp.wait_ge(w_in, 112)
                sp.wait_ge(steps, SETUP)
                sp.dma_start(sums, SUM[:]).then_inc(sum_out, 16)
                sp.wait_ge(sum_out, 16)
                for u in range(2):
                    sp.dma_start(SM[u * L:(u + 1) * L],
                                 spread(sums.rearrange("(t u) d -> u t d", u=2)[u], 0, L)).then_inc(sum_in, 16)

            @block.gpsimd
            def _(pool):
                nc.gpsimd.memset(ones[:], 1.0).then_inc(ready, 1)
                nc.gpsimd.memset(all1[:], 1.0).then_inc(ready, 1)
                nc.gpsimd.memset(flip[:], 0.0).then_inc(ready, 1)
                pool.wait_ge(ready, 3)
                nc.gpsimd.affine_select(out=flip[:], in_=flip[:], compare_op=ALU.not_equal, fill=1.0, base=1 - L,
                                        pattern=[[1, L]], channel_multiplier=1).then_inc(ready, 1)
                norm.constants(pool)
                pool.wait_ge(w_in, 112)

                def with_summary(g, w):
                    pool.wait_ge(norm.normed, g * G + G)
                    nc.gpsimd.tensor_tensor(Y[:, w], Y[:, w], SM[:, bass.ds(g * G, G), :], ALU.add).then_inc(added, 1)

                def step(g, w):
                    if is_group(g + 1):
                        norm.on_pool(pool, g + 1)
                    if is_group(g):
                        pool.wait_ge(stats_done, g * G + G)
                        nc.gpsimd.tensor_tensor(veps[:], mv[:, :, 1], norm.eps[:], ALU.add).then_inc(veps_done, 1)
                        pool.wait_ge(veps_done, g + 1)
                        nc.gpsimd.tensor_tensor(rstd[:], veps[:], norm.mhalf[:], ALU.pow).then_inc(rstd_done, 1)
                    if is_group(g + 1):
                        with_summary(g + 1, 1 - w)
                    if is_group(g):
                        pool.wait_ge(normed, g * G + G)
                        nc.gpsimd.tensor_tensor(Y[:, w], Y[:, w], spread(gam[:], 1, G), ALU.mult).then_inc(gained, 1)

                norm.on_pool(pool, 0)
                pool.wait_ge(sum_in, 32)
                with_summary(0, 0)
                rounds(pool, step, NG)

            @block.vector
            def _(dve):
                v = nc.vector
                step = Steps(dve, steps, SETUP)
                norm.on_vector(dve, 0, Y[:, 0])
                dve.wait_ge(ready, 4)
                dve.wait_ge(expd, 1)
                step(v.tensor_scalar(k[:, 1:2], k[:, 0:1], 1.0, None, ALU.add))
                step(v.reciprocal(k[:, 2:3], k[:, 1:2]))
                step(v.tensor_scalar(weights[:], ones[:], k[:, 2:3], None, ALU.mult))
                step(v.tensor_tensor_scan(powers[:], weights[:], ones[:], 0.0, ALU.mult, ALU.add))
                step(v.tensor_tensor(flipped[:], powers[0:L, :], flip[:], ALU.mult))
                step(v.tensor_reduce(col[:], flipped[:], AX.X, ALU.add))
                step(v.tensor_scalar(diag[:], ident[0:L, 0:L], col[:, 0:1], None, ALU.mult))
                dve.wait_ge(wide, 1)
                step(v.tensor_copy(weights[:], psB[:, 0:L]))
                step(v.tensor_reduce(wsum[:], weights[:], AX.X, ALU.add))
                dve.wait_ge(w_in, 112)
                step(v.tensor_scalar(bw[:], bi[:], wsum[:, 0:1], None, ALU.mult))
                for c in range(KC):
                    for half in range(2):
                        seg = CT[:, c, half * (N // 2):(half + 1) * (N // 2)].rearrange("p (b l) -> p b l", l=L)
                        step(v.tensor_tensor(weighted[:, half], seg, spread(weights[:], 1, B // 2), ALU.mult))
                        step(v.tensor_reduce(ST[:, c, half * (B // 2):(half + 1) * (B // 2)], weighted[:, half], AX.X,
                                             ALU.add))
                for c in range(KC):
                    dve.wait_ge(hid, c + 1)
                    step(v.tensor_scalar(HT[:, c, :], psH[:, c, 0:B], bw[:, c:c + 1], None, ALU.add))
                dve.wait_ge(summed, 1)
                step(v.scalar_tensor_tensor(SUM[:], psS[:, 0:D], 1.0 / L, bo[:], ALU.mult, ALU.add))
                step.end()

                def step(g, w):
                    if is_group(g + 1):
                        norm.take_stats(dve, g + 1)
                    if is_group(g):
                        dve.wait_ge(added, g + 1)
                        for j in range(G):
                            v.bn_stats(stats[:, j, :], Y[:, w, j, :])
                        dve.drain()
                        for j in range(G):
                            v.bn_aggr(mv[:, j, :], stats[:, j, :]).then_inc(stats_done, 1)
                    if is_group(g - 1):
                        dve.wait_ge(gained, g)
                        sum_up = Steps(dve, y_steps, 2, g - 1)
                        sum_up(v.tensor_tensor(Y[:, 1 - w], Y[:, 1 - w], spread(bet[:], 1, G), ALU.add))
                        xs = X[:, bass.ds(g * G - G, G), :]
                        sum_up(v.tensor_tensor(xs, xs, Y[:, 1 - w], ALU.add))
                        sum_up.end()
                    if is_group(g + 1):
                        norm.normalise(dve, g + 1, Y[:, 1 - w])
                    if is_group(g):
                        dve.wait_ge(rstd_done, g + 1)
                        dve.wait_ge(stats_done, g * G + G)
                        for j in range(G):
                            v.tensor_scalar(Y[:, w, j], Y[:, w, j], mv[:, j, 0:1], rstd[:, j:j + 1], ALU.subtract,
                                            ALU.mult).then_inc(normed, 1)

                rounds(dve, step, NG)

            @block.tensor
            def _(pe):
                pe.wait_ge(w_in, 112)
                for m, W in enumerate((WI, WO)):
                    for k_ in range(KC):
                        for c in range(KC):
                            mm = nc.tensor.transpose(psW[:, m, k_, c * P:(c + 1) * P], W[:, c, k_ * P:(k_ + 1) * P],
                                                     ident[:])
                    mm.then_inc(w_turned, 1)
                pe.wait_ge(steps, 7)
                nc.tensor.matmul(psB[:, 0:L], all1[:], diag[:], start=True, stop=True).then_inc(wide, 1)
                pe.wait_ge(steps, 18)
                pe.wait_ge(w_copied, 1)
                for e in range(KC):
                    for c in range(KC):
                        mm = nc.tensor.matmul(psH[:, e, 0:B], WIT[:, c, e * P:(e + 1) * P], ST[:, c, :],
                                              start=(c == 0), stop=(c == KC - 1))
                    mm.then_inc(hid, 1)
                pe.wait_ge(steps, 20)
                pe.wait_ge(w_copied, 2)
                for e in range(KC):
                    mm = nc.tensor.matmul(psS[:, 0:D], HT[:, e, :], WOT[:, e, :], start=(e == 0), stop=(e == KC - 1))
                mm.then_inc(summed, 1)

            @block.scalar
            def _(act):
                act.wait_ge(w_in, 112)
                nc.scalar.activation(k[:, 0:1], decay[:], ACT.Exp, scale=-1.0).then_inc(expd, 1)
                for m, WT in enumerate((WIT, WOT)):
                    act.wait_ge(w_turned, m + 1)
                    nc.scalar.copy(WT[:], psW[:, m]).then_inc(w_copied, 1)

def mk_xattn_ffn_d4(nc, io, out):
    zq = nc.dram_tensor("z_parts", (3, DH0, T // 2, 2 * NH0, 2, D), BF16, kind="Internal").ap()
    ck = nc.dram_tensor("context_parts", (3, DH0, T // 2, 2 * NH0, 2, D), BF16, kind="Internal").ap()
    o_dram = nc.dram_tensor("head_sums", (T, 4, 4, DH0 + 1, D), F32, kind="Internal").ap()
    sums = nc.dram_tensor("summaries", (B, D), F32, kind="Internal").ap()
    with ExitStack() as ctx:
        s = Scope(nc, ctx, "all")
        X = s.sb("X", [P, T, D])
        CT = s.sb("CT", [P, KC, N])
        ident = s.sb("ident", [P, P])
        identb = s.sb("identb", [P, P], BF16)
        prepare(nc, io, X, CT, ident, zq, ck)
        with nc.Block() as block:

            @block.vector
            def _(dve):
                nc.vector.tensor_copy(identb[:], ident[:])

        row_attention(nc, io, X, CT, identb, zq, ck, o_dram)
        selected_ffn(nc, io, X, ident)
        with ExitStack() as inner:
            s = Scope(nc, inner, "heads")
            KX = s.sb("KX", [P, 2, KC, HC, HG])
            VB = s.sb("VB", [P, 2, BG, NP, 2, VW])
            gated_attention(nc, io, X, CT, ident, identb, KX, VB)
            normed_ffn(nc, io, X, ident, identb)
            softmax_attention(nc, io, X, CT, ident, KX, VB)
        gated_ffn(nc, io, X, ident, identb)
        summary_mix(nc, io, X, CT, ident, sums)
        quantized_ffn(nc, io, X, ident, out)

_INS = ["x", "ctx_2048", "L0_ffn_w_r", "L0_ffn_b_r", "L0_ffn_w1", "L0_ffn_b1", "L0_ffn_w2", "L0_ffn_b2",
        "L1_xattn_Wi", "L1_xattn_bi", "L1_xattn_Wf", "L1_xattn_bf", "L1_xattn_ln_scale", "L1_ffn_w1", "L1_ffn_b1",
        "L1_ffn_ln_g", "L1_ffn_ln_b", "L1_ffn_w2", "L1_ffn_b2", "L2_xattn_Wq", "L2_xattn_bq", "L2_xattn_Wk",
        "L2_xattn_bk", "L2_xattn_Wv", "L2_xattn_bv", "L2_xattn_Wo", "L2_xattn_bo", "L2_ffn_w_gate", "L2_ffn_w_up",
        "L2_ffn_w_down", "L3_xattn_decay", "L3_xattn_W_in", "L3_xattn_b_in", "L3_xattn_W_out", "L3_xattn_b_out",
        "L3_xattn_gamma", "L3_xattn_beta", "L3_ffn_kernel", "L3_ffn_bias"]

def kernel(**inputs):
    import numpy as _np
    import concourse.bacc as _bacc
    from concourse import mybir as _mybir
    from concourse.bass_utils import run_bass_kernel_spmd as _run

    nc = _bacc.Bacc("TRN2", target_bir_lowering=False, num_devices=1)
    arrays, io = {}, {}
    for name in _INS:
        a = _np.ascontiguousarray(inputs[name])
        if a.ndim == 0:
            a = a.reshape(1)
        arrays[f"in_{name}_dram"] = a
        io[name] = nc.dram_tensor(f"in_{name}_dram", a.shape, _mybir.dt.from_np(a.dtype), kind="ExternalInput").ap()
    out = nc.dram_tensor("out_0_dram", (B, L, D), F32, kind="ExternalOutput").ap()
    mk_xattn_ffn_d4(nc, io, out)
    r = _run(nc, [arrays], core_ids=[0])
    return r.results[0]["out_0_dram"]
```
